# Optimizing a Trainium2 kernel written in Bass

```python
import numpy as np
import jax
import jax.numpy as jnp

def _softmax(x, axis=-1):
    return jax.nn.softmax(x, axis=axis)

def _gelu(x):
    return jax.nn.gelu(x, approximate=True)

def _silu(x):
    return jax.nn.silu(x)

def _sigmoid(x):
    return jax.nn.sigmoid(x)

def _layernorm(x, axis=-1, eps=1e-05):
    m = jnp.mean(x, axis=axis, keepdims=True)
    v = jnp.var(x, axis=axis, keepdims=True)
    return (x - m) / jnp.sqrt(v + eps)

def _scatter_add(tgt, idx, src, axis=0):
    return tgt.at[idx].add(src)

def _segment_sum(src, seg, n):
    return jax.ops.segment_sum(src, seg, n)
kernel_name = 'mk_sandwich_d1_jaxref_r8_7fbc30'

def setup_inputs(seed: int=0):
    np.random.seed(seed)
    _w = jnp.asarray

    def _L0_attn_setup():
        import jax, jax.numpy as jnp
        import numpy as np
        B_SZ, SEQ = (2, 512)
        D_MODEL = 128
        EXPAND = 2
        HEADDIM = 64
        D_STATE = 128
        D_CONV = 4
        INTER = EXPAND * D_MODEL
        NHEADS = INTER // HEADDIM
        CONV_DIM = INTER + 2 * D_STATE
        PROJ_DIM = 2 * INTER + 2 * D_STATE + NHEADS
        CHUNK = 32
        EPS = 1e-05

        def _silu(x):
            return x * jax.nn.sigmoid(x)

        def _causal_conv1d(x, w, b):
            k = w.shape[1]
            xp = jnp.pad(x, ((0, 0), (k - 1, 0), (0, 0)))
            y = b
            for i in range(k):
                y = y + xp[:, i:i + x.shape[1], :] * w[:, i]
            return y

        def _segsum(x):
            l = x.shape[-1]
            cs = jnp.cumsum(x, -1)
            d = cs[..., :, None] - cs[..., None, :]
            mask = jnp.tril(jnp.ones((l, l), dtype=bool))
            return jnp.where(mask, d, -jnp.inf)

        def _ssd(x, dt, A, Bm, Cm):
            b, s, h, p = x.shape
            n = Bm.shape[-1]
            c = s // CHUNK
            X = (x * dt[..., None]).reshape(b, c, CHUNK, h, p)
            Adt = (dt * A).reshape(b, c, CHUNK, h).transpose(0, 3, 1, 2)
            Bc = Bm.reshape(b, c, CHUNK, n)
            Cc = Cm.reshape(b, c, CHUNK, n)
            A_cum = jnp.cumsum(Adt, -1)
            L = jnp.exp(_segsum(Adt))
            scores = jnp.einsum('bcln,bcsn->bcls', Cc, Bc)
            Y_diag = jnp.einsum('bhcls,bcshp->bclhp', scores[:, None] * L, X)
            decay_states = jnp.exp(A_cum[..., -1:] - A_cum)
            states = jnp.einsum('bcln,bhcl,bclhp->bchpn', Bc, decay_states, X)
            A_chunk = jnp.pad(A_cum[..., -1], ((0, 0), (0, 0), (1, 0)))
            decay_chunk = jnp.exp(_segsum(A_chunk))
            states = jnp.concatenate([jnp.zeros_like(states[:, :1]), states], axis=1)
            states = jnp.einsum('bhzc,bchpn->bzhpn', decay_chunk, states)[:, :-1]
            Y_off = jnp.einsum('bcln,bchpn,bhcl->bclhp', Cc, states, jnp.exp(A_cum))
            return (Y_diag + Y_off).reshape(b, s, h, p)
        key = jax.random.key(seed)
        k = jax.random.split(key, 6)
        u = jax.random.normal(k[0], (B_SZ, SEQ, D_MODEL), jnp.float32)
        in_proj_w = jax.random.normal(k[1], (D_MODEL, PROJ_DIM), jnp.float32) * 0.02
        conv_w = jax.random.normal(k[2], (CONV_DIM, D_CONV), jnp.float32) * 0.2
        conv_b = jnp.zeros((CONV_DIM,), jnp.float32)
        dt0 = jnp.exp(jax.random.uniform(k[3], (NHEADS,), jnp.float32, np.log(0.001), np.log(0.1)))
        dt_bias = jnp.log(jnp.expm1(dt0))
        A_log = jnp.log(jnp.arange(1, NHEADS + 1, dtype=jnp.float32))
        D_param = jnp.ones((NHEADS,), jnp.float32)
        norm_w = jnp.ones((INTER,), jnp.float32)
        out_proj_w = jax.random.normal(k[4], (INTER, D_MODEL), jnp.float32) * 0.02
        return {'u': u, 'in_proj_w': in_proj_w, 'conv_w': conv_w, 'conv_b': conv_b, 'dt_bias': dt_bias, 'A_log': A_log, 'D_param': D_param, 'norm_w': norm_w, 'out_proj_w': out_proj_w}
    _L0_attn_in = _L0_attn_setup()

    def _L0_ffn_setup():
        import jax, jax.numpy as jnp
        import numpy as np
        B, S, D, E, H, K = (4, 256, 128, 8, 64, 2)
        key = jax.random.key(seed)
        ks = jax.random.split(key, 11)
        sc = 0.02
        return {'x': jax.random.normal(ks[0], (B, S, D), dtype=jnp.float32), 'gate_W': jax.random.normal(ks[1], (D, E), dtype=jnp.float32) * sc, 'W1': jax.random.normal(ks[2], (E, D, H), dtype=jnp.float32) * sc, 'b1': jnp.zeros((E, H), dtype=jnp.float32), 'W2': jax.random.normal(ks[3], (E, H, D), dtype=jnp.float32) * sc, 'b2': jnp.zeros((E, D), dtype=jnp.float32), 'Ws1': jax.random.normal(ks[4], (D, H), dtype=jnp.float32) * sc, 'bs1': jnp.zeros((H,), dtype=jnp.float32), 'Ws2': jax.random.normal(ks[5], (H, D), dtype=jnp.float32) * sc, 'bs2': jnp.zeros((D,), dtype=jnp.float32), 'route_scale': jnp.ones((), dtype=jnp.float32)}
    _L0_ffn_in = _L0_ffn_setup()
    _d = {'L0_attn_u': _L0_attn_in['u'], 'L0_attn_in_proj_w': _L0_attn_in['in_proj_w'], 'L0_attn_conv_w': _L0_attn_in['conv_w'], 'L0_attn_conv_b': _L0_attn_in['conv_b'], 'L0_attn_dt_bias': _L0_attn_in['dt_bias'], 'L0_attn_A_log': _L0_attn_in['A_log'], 'L0_attn_D_param': _L0_attn_in['D_param'], 'L0_attn_norm_w': _L0_attn_in['norm_w'], 'L0_attn_out_proj_w': _L0_attn_in['out_proj_w'], 'L0_ffn_gate_W': _L0_ffn_in['gate_W'], 'L0_ffn_W1': _L0_ffn_in['W1'], 'L0_ffn_b1': _L0_ffn_in['b1'], 'L0_ffn_W2': _L0_ffn_in['W2'], 'L0_ffn_b2': _L0_ffn_in['b2'], 'L0_ffn_Ws1': _L0_ffn_in['Ws1'], 'L0_ffn_bs1': _L0_ffn_in['bs1'], 'L0_ffn_Ws2': _L0_ffn_in['Ws2'], 'L0_ffn_bs2': _L0_ffn_in['bs2'], 'L0_ffn_route_scale': _L0_ffn_in['route_scale']}
    _x0 = _d['L0_attn_u']
    _d['L0_attn_u'] = jax.random.normal(jax.random.fold_in(jax.random.key(seed), 1), (8, 1024, 128), dtype=_x0.dtype)
    del _x0
    return _d

def reference(L0_attn_u, L0_attn_in_proj_w, L0_attn_conv_w, L0_attn_conv_b, L0_attn_dt_bias, L0_attn_A_log, L0_attn_D_param, L0_attn_norm_w, L0_attn_out_proj_w, L0_ffn_gate_W, L0_ffn_W1, L0_ffn_b1, L0_ffn_W2, L0_ffn_b2, L0_ffn_Ws1, L0_ffn_bs1, L0_ffn_Ws2, L0_ffn_bs2, L0_ffn_route_scale):

    def _L0_attn_ref(u, in_proj_w, conv_w, conv_b, dt_bias, A_log, D_param, norm_w, out_proj_w):
        import jax, jax.numpy as jnp
        import numpy as np
        B_SZ, SEQ = (2, 512)
        D_MODEL = 128
        EXPAND = 2
        HEADDIM = 64
        D_STATE = 128
        D_CONV = 4
        INTER = EXPAND * D_MODEL
        NHEADS = INTER // HEADDIM
        CONV_DIM = INTER + 2 * D_STATE
        PROJ_DIM = 2 * INTER + 2 * D_STATE + NHEADS
        CHUNK = 32
        EPS = 1e-05

        def _silu(x):
            return x * jax.nn.sigmoid(x)

        def _causal_conv1d(x, w, b):
            k = w.shape[1]
            xp = jnp.pad(x, ((0, 0), (k - 1, 0), (0, 0)))
            y = b
            for i in range(k):
                y = y + xp[:, i:i + x.shape[1], :] * w[:, i]
            return y

        def _segsum(x):
            l = x.shape[-1]
            cs = jnp.cumsum(x, -1)
            d = cs[..., :, None] - cs[..., None, :]
            mask = jnp.tril(jnp.ones((l, l), dtype=bool))
            return jnp.where(mask, d, -jnp.inf)

        def _ssd(x, dt, A, Bm, Cm):
            b, s, h, p = x.shape
            n = Bm.shape[-1]
            c = s // CHUNK
            X = (x * dt[..., None]).reshape(b, c, CHUNK, h, p)
            Adt = (dt * A).reshape(b, c, CHUNK, h).transpose(0, 3, 1, 2)
            Bc = Bm.reshape(b, c, CHUNK, n)
            Cc = Cm.reshape(b, c, CHUNK, n)
            A_cum = jnp.cumsum(Adt, -1)
            L = jnp.exp(_segsum(Adt))
            scores = jnp.einsum('bcln,bcsn->bcls', Cc, Bc)
            Y_diag = jnp.einsum('bhcls,bcshp->bclhp', scores[:, None] * L, X)
            decay_states = jnp.exp(A_cum[..., -1:] - A_cum)
            states = jnp.einsum('bcln,bhcl,bclhp->bchpn', Bc, decay_states, X)
            A_chunk = jnp.pad(A_cum[..., -1], ((0, 0), (0, 0), (1, 0)))
            decay_chunk = jnp.exp(_segsum(A_chunk))
            states = jnp.concatenate([jnp.zeros_like(states[:, :1]), states], axis=1)
            states = jnp.einsum('bhzc,bchpn->bzhpn', decay_chunk, states)[:, :-1]
            Y_off = jnp.einsum('bcln,bchpn,bhcl->bclhp', Cc, states, jnp.exp(A_cum))
            return (Y_diag + Y_off).reshape(b, s, h, p)
        b, s, _ = u.shape
        zxbcdt = u @ in_proj_w
        z = zxbcdt[..., :INTER]
        xBC = zxbcdt[..., INTER:INTER + CONV_DIM]
        dt = zxbcdt[..., INTER + CONV_DIM:]
        xBC = _silu(_causal_conv1d(xBC, conv_w, conv_b))
        x = xBC[..., :INTER]
        Bm = xBC[..., INTER:INTER + D_STATE]
        Cm = xBC[..., INTER + D_STATE:]
        dt = jax.nn.softplus(dt + dt_bias)
        A = -jnp.exp(A_log)
        xh = x.reshape(b, s, NHEADS, HEADDIM)
        y = _ssd(xh, dt, A, Bm, Cm) + D_param[None, None, :, None] * xh
        y = y.reshape(b, s, INTER)
        g = y * _silu(z)
        g = g * jax.lax.rsqrt(jnp.mean(g * g, -1, keepdims=True) + EPS) * norm_w
        return g @ out_proj_w

    def _L0_ffn_ref(x, gate_W, W1, b1, W2, b2, Ws1, bs1, Ws2, bs2, route_scale):
        import jax, jax.numpy as jnp
        import numpy as np
        B, S, D, E, H, K = (4, 256, 128, 8, 64, 2)
        scores = jax.nn.sigmoid(x @ gate_W) * route_scale
        topk_scores, topk_idx = jax.lax.top_k(scores, K)
        topk_w = topk_scores / topk_scores.sum(-1, keepdims=True)
        onehot = jax.nn.one_hot(topk_idx, E, dtype=x.dtype)
        gate_full = jnp.einsum('bsk,bske->bse', topk_w, onehot)
        h = jax.nn.gelu(jnp.einsum('bsd,edh->bseh', x, W1) + b1, approximate=False)
        y = jnp.einsum('bseh,ehd->bsed', h, W2) + b2
        expert_out = jnp.einsum('bse,bsed->bsd', gate_full, y)
        shared = jax.nn.gelu(x @ Ws1 + bs1, approximate=False) @ Ws2 + bs2
        return expert_out + shared
    x = L0_attn_u
    x = x + _layernorm(_L0_attn_ref(_layernorm(x, axis=-1), L0_attn_in_proj_w, L0_attn_conv_w, L0_attn_conv_b, L0_attn_dt_bias, L0_attn_A_log, L0_attn_D_param, L0_attn_norm_w, L0_attn_out_proj_w), axis=-1)
    x = x + _layernorm(_L0_ffn_ref(_layernorm(x, axis=-1), L0_ffn_gate_W, L0_ffn_W1, L0_ffn_b1, L0_ffn_W2, L0_ffn_b2, L0_ffn_Ws1, L0_ffn_bs1, L0_ffn_Ws2, L0_ffn_bs2, L0_ffn_route_scale), axis=-1)
    return x

_drawn_inputs = setup_inputs


def setup_inputs(seed=0):
    import zlib

    import numpy as np

    out = dict(_drawn_inputs(seed))
    spreads = {'L0_attn_conv_b': (0.0, 0.1),
     'L0_attn_D_param': (1.0, 0.2),
     'L0_attn_norm_w': (1.0, 0.2),
     'L0_ffn_b1': (0.0, 0.1),
     'L0_ffn_b2': (0.0, 0.1),
     'L0_ffn_bs1': (0.0, 0.1),
     'L0_ffn_bs2': (0.0, 0.1)}
    factors = {'L0_attn_dt_bias': 24.597, 'L0_attn_A_log': 23.304}
    for name, (base, spread) in spreads.items():
        noise = np.random.default_rng([zlib.crc32(name.encode()), seed]).standard_normal(out[name].shape)
        drawn = base * np.exp(spread * noise) if base else spread * noise
        out[name] = jnp.asarray(drawn.astype(out[name].dtype))
    for name, factor in factors.items():
        out[name] = (out[name] * factor).astype(out[name].dtype)
    return out
```

```python
import concourse.bass as bass
from concourse import mybir
from contextlib import ExitStack


def ssd_moe_block(nc, dram, out):
    f32, bf16, i32 = mybir.dt.float32, mybir.dt.bfloat16, mybir.dt.int32
    ALU, ACT = mybir.AluOpType, mybir.ActivationFunctionType
    ds = bass.ds

    P = 128
    NSEQ, SEQ, D = dram["u"].shape
    INTER = dram["norm_w"].shape[0]
    H = dram["dt_bias"].shape[0]
    HD = INTER // H
    TPS = SEQ // P
    NT = NSEQ * TPS
    MT = 4
    MW = MT * P
    NM = NT // MT
    CONV0 = INTER
    NCONV = (dram["conv_w"].shape[0]) // P
    KC = dram["conv_w"].shape[1]
    DT0 = INTER + NCONV * P
    NE = dram["gate_W"].shape[1]
    HID = dram["W1"].shape[2]
    NPAIR = NE * HID // P
    EPS = 1e-5
    LN_CHAIN = 14
    UNITS = 4
    SGRP = 32

    u_v = dram["u"].rearrange("s (t p) d -> p (s t) d", p=P)
    out_v = out.rearrange("s (t p) d -> p (s t) d", p=P)

    with ExitStack() as ctx:
        def sb(name, shape, dt=f32):
            return ctx.enter_context(nc.sbuf_tensor(name, shape, dt))

        def sem(name):
            return ctx.enter_context(nc.semaphore(name))

        x_all = sb("x_all", [P, NT, D])
        xT_all = sb("xT_all", [P, NT * P])
        LE = sb("LE", [P, TPS, 2, H * P])
        xbc = sb("xbc", [P, 2, NCONV, SEQ])
        zs = sb("zs", [P, 2, 2, SEQ])
        gbuf = sb("gbuf", [P, 2, SEQ])
        raw = sb("raw", [P, 2, KC - 1 + SEQ])
        Xdt = sb("Xdt", [P, 2, INTER])
        Xw = sb("Xw", [P, 2, INTER])
        St = sb("St", [P, 2, INTER])
        Sd = sb("Sd", [P, INTER])
        Btok = sb("Btok", [P, 2, P])
        on = sb("on", [P, 2, MT, D])
        xn_tile = sb("xn_tile", [P, MT, D])
        stage_tile = sb("stage_tile", [P, MW])
        w_in = sb("w_in", [P, DT0 + H])
        w_gate = sb("w_gate", [P, NE])
        w_out = sb("w_out", [P, 2, D])
        nw = sb("nw", [P, 2])
        cw = sb("cw", [P, NCONV, KC])
        cb = sb("cb", [P, NCONV])
        dskip = sb("dskip", [P, 2])
        ident = sb("ident", [P, P])
        identb = sb("identb", [P, P], bf16)
        tri = sb("tri", [P, P])
        ones = sb("ones", [P, P])
        maskb = sb("maskb", [P, H, P], bf16)
        csl = sb("csl", [3 + 3 * H, TPS, P], bf16)
        csr = sb("csr", [3 + 3 * H, TPS, H * P], bf16)
        bias4 = sb("bias4", [P, H])
        alog4 = sb("alog4", [P, H])
        dt_all = sb("dt_all", [P, NT, H])
        dec_all = sb("dec_all", [P, NT, H])
        tot_all = sb("tot_all", [P, NT, H])
        logits = sb("logits", [P, NT, NE])
        w1 = sb("w1", [P, NPAIR * P + HID])
        b1 = sb("b1", [P, NPAIR + 1])
        w2 = sb("w2", [P, NPAIR + 1, D])
        selb = sb("selb", [P, NPAIR, P], bf16)
        brow = sb("brow", [P, 3, P], bf16)
        gst = sb("gst", [P, 2, MT, P], bf16)
        rank0 = sb("rank0", [P, NE])
        rscale = sb("rscale", [P, 1])
        NC = UNITS * MT
        st6 = sb("st6", [P, NC, 6])
        mv = sb("mv", [P, NC, 2])
        nt_a = sb("nt_a", [P, NC])
        nt_b = sb("nt_b", [P, NC])
        nt_y = sb("nt_y", [P, NC])
        veps = sb("veps", [P, NC])
        rst = sb("rst", [P, NC])
        nmean = sb("nmean", [P, NC])
        msb = sb("msb", [P, MT])

        TN = NT * H
        le_flat = LE[:, :, :, :].rearrange("p t a n -> p (t a n)")
        s1 = [le_flat[:, k * TN:(k + 1) * TN] for k in range(12)]
        csp = le_flat[:, 12 * TN:14 * TN].bitcast(bf16)[:, 0:3 * TN].rearrange("p (k n) -> p k n", k=3)
        mask_f = le_flat[:, 16 * TN:16 * TN + P]
        rows_f = le_flat[:, 18 * TN:18 * TN + H * P + P]
        sel_f = le_flat[:, 21 * TN:21 * TN + NPAIR * P]
        brow_f = le_flat[:, 23 * TN:23 * TN + P]
        brow_r = le_flat[:, 24 * TN:24 * TN + 2 * P].rearrange("p (k n) -> p k n", k=2)
        stage = [stage_tile, le_flat[:, 27 * TN + P:27 * TN + P + MW]]
        xn3 = [xn_tile, le_flat[:, 25 * TN + P:25 * TN + P + MW].rearrange("p (t d) -> p t d", t=MT)]
        NF = NPAIR + 1
        xbc_flat = xbc[:, :, :, :].rearrange("p a c n -> p (a c n)")
        hbuf = [xbc_flat[:, k * MW:(k + 1) * MW] for k in range(2)]
        hg = [[xbc_flat[:, (2 + q * NF + j) * MW:(3 + q * NF + j) * MW] for j in range(NF)] for q in range(2)]
        gt = [xbc_flat[:, 12 * MW + q * (MW // 2):12 * MW + (q + 1) * (MW // 2)].bitcast(bf16) for q in range(2)]
        onf = [xbc_flat[:, (13 + q) * MW:(14 + q) * MW].rearrange("p (t d) -> p t d", t=MT) for q in range(2)]
        r1 = [le_flat[:, k * NT * NE:(k + 1) * NT * NE].rearrange("p (t e) -> p t e", e=NE) for k in range(6)]
        gates = le_flat[:, 6 * NT * NE:6 * NT * NE + NT * NE * 3 // 2].bitcast(bf16).rearrange(
            "p (t k e) -> p t k e", k=3, e=NE)
        outb = [le_flat[:, (8 + q) * MW:(9 + q) * MW].rearrange("p (t d) -> p t d", t=MT) for q in range(2)]

        proj_bank = [ctx.enter_context(nc.psum_tensor(f"proj_bank{k}", [P, MW], f32)) for k in range(2)]
        exp_bank = ctx.enter_context(nc.psum_tensor("exp_bank", [P, 2, H * P], f32))
        sx_bank = ctx.enter_context(nc.psum_tensor("sx_bank", [P, 512], f32))
        ys_bank = ctx.enter_context(nc.psum_tensor("ys_bank", [P, 512], f32))
        bt_bank = ctx.enter_context(nc.psum_tensor("bt_bank", [P, 512], f32))
        tail_bank = ctx.enter_context(nc.psum_tensor("tail_bank", [P, 512], f32))
        dt_bank = exp_bank[:, 0, :]
        fout_bank = [sx_bank, ys_bank]
        gt_bank = bt_bank[:, 0:MW // 2].bitcast(bf16)

        cs_rows = nc.dram_tensor("cs_rows", (3, NT * H * P), bf16, kind="Internal").ap()

        names = """settled started first_consts consts consts_cast zeroed rows_out
            p0_chain p0_norm p0_tr p0_evac p0_dt p0_dtread pre_exp pre_dve pre_pe
            proj_done proj_read a0_done taps xbc_ready de_done exp_done b_done bt_done btok_done
            xdt_done m_done ch_done xw_done sd_done c_done s_ready y_done
            g_done sq_done sqs_done ms_done ms_read out_done chained on_done x1_done xn3_done
            tr_done xft_done lg_done lg_read route route_exp gst_done gtt_done gt_done f1_done
            gelu_done gb_done hg_done fout_done fout_chain onf_done ob_done""".split()
        S = {n: sem(n) for n in names}
        cs_in = [sem(f"cs_in{k}") for k in range(2)]
        u_in = [sem(f"u_in{k}") for k in range(UNITS)]
        x1_saved = [sem(f"x1_saved{k}") for k in range(2)]
        stored = [sem(f"stored{k}") for k in range(2)]
        block = ctx.enter_context(nc.Block())

        def wait(eng, name, value):
            if isinstance(value, int) and value <= 0:
                return
            eng.wait_ge(S[name], value)

        JOBS = [(0, 0, 0), (0, 0, 1), (2, 1, 0), (2, 1, 1), (3, NCONV, 0), (3, NCONV + 1, 0), (4, 2, 0), (4, 2, 1),
                (6, 3, 0), (6, 3, 1), (7, NCONV, 1), (7, NCONV + 1, 1)]
        NJOB = len(JOBS)

        def settle(eng):
            eng.sem_inc(S["settled"], 1)

        EXPS = {1: (4, 5, 6), 2: (7,), 5: (8, 9, 10), 6: (11,)}
        def steps(scan, proj, prev):
            for t in range(TPS + 1):
                if proj and t % 2 == 0 and t:
                    yield "silu", t // 2 - 1
                if scan and t < TPS:
                    yield "chunk", t
                exps = []
                if scan and t in (1, 2):
                    exps = EXPS[t]
                if proj and t in (5, 6):
                    exps = EXPS[t]
                for k in exps[0:1]:
                    yield "exp", k
                if prev and t == 1:
                    yield "outproj", 1
                if scan and t == 5:
                    yield "outproj", 0
                if prev and t == 2:
                    yield "ms", 1
                if scan and t == 6:
                    yield "ms", 0
                if proj:
                    for n, (slot, c, m) in enumerate(JOBS):
                        if slot == t:
                            yield "job", n
                    if t % 2 == 1:
                        yield "conv", t // 2
                if prev and t == 2:
                    yield "chain", 1
                if (scan or prev) and t == 6:
                    yield "chain", 0
                for k in exps[1:2]:
                    yield "exp", k
                if prev and t in (3, 7):
                    yield "back", t // 4
                if prev and t in (3, 7):
                    yield "logits", t // 4
                if scan and t >= 1:
                    yield "state", t - 1
                for k in exps[2:3]:
                    yield "exp", k
                if scan and t in (4, 8):
                    yield "gate", t // 4 - 1

        def run_bodies(eng, emit):
            emit(-1, 1, False, True, False)
            emit(0, 0, True, True, False)
            with eng.Fori(0, (NSEQ - 2) // 2) as i:
                emit(i * 2 + 1, 1, True, True, True)
                emit(i * 2 + 2, 0, True, True, True)
            emit(NSEQ - 1, 1, True, False, True)
            emit(NSEQ, 0, False, False, True)

        def run_peeled(eng, count, emit):
            emit(0)
            with eng.Fori(1, count) as i:
                emit(i)

        NTAP = KC - 1

        def half_of(m):
            return slice(m * MW, (m + 1) * MW)

        def tile_of(t):
            return slice(t * P, (t + 1) * P)

        @block.sync
        def _(sp):
            def units(i):
                for k in range(UNITS):
                    g = i * UNITS + k
                    if not isinstance(i, int):
                        sp.wait_ge(u_in[k], i * 16)
                        settle(sp)
                    sp.dma_start(x_all[:, ds(g * MT, MT), :], u_v[:, ds(g * MT, MT), :]).then_inc(u_in[k], 16)

            run_peeled(sp, NM // UNITS, units)
            sp.wait_ge(S["pre_dve"], 17)
            for k in range(3):
                sp.dma_start(cs_rows[k, :].rearrange("(a r l) -> r a l", a=2, l=P),
                             csp[:, k, :].rearrange("p (a l) -> p a l", a=2)).then_inc(S["rows_out"], 16)
            sp.wait_ge(S["rows_out"], 48)

            def load_rows(s, half):
                HT = TPS // 2
                at = s * (TPS * H * P) + half * (HT * H * P)
                to = slice(half * HT, (half + 1) * HT)
                sp.dma_start(csr[0:3, to, :], cs_rows[:, ds(at, HT * H * P)].rearrange("k (t n) -> k t n", t=HT)
                             ).then_inc(cs_in[half], 16)
                for k in range(3):
                    src = cs_rows[k, ds(at, HT * H * P)].rearrange("(t h l) -> h t l", t=HT, h=H)
                    sp.dma_start(csl[3 + H * k:3 + H * k + H, to, :], src).then_inc(cs_in[half], 16)

            sp.wait_ge(S["consts_cast"], 4)
            load_rows(0, 0)
            load_rows(0, 1)

            def emit(s, par, scan, proj, prev):
                for what, k in steps(scan, proj, prev):
                    if what == "chain" and (k == 1 or scan):
                        g = (s - k) * 2 + k
                        sp.wait_ge(S["x1_done"], g + 1)
                        settle(sp)
                        sp.dma_start(x_all[:, ds(g * MT, MT), :] if not isinstance(g, int)
                                     else x_all[:, g * MT:(g + 1) * MT, :], on[:, k, :, :]).then_inc(x1_saved[k], 16)
                    elif what == "chunk" and proj and k in (0, 3):
                        half = min(k, 1)
                        sp.wait_ge(S["de_done"], s * TPS + (half + 1) * TPS // 2)
                        sp.wait_ge(cs_in[half], (s + 1) * 64)
                        settle(sp)
                        load_rows(s + 1, half)

            run_bodies(sp, emit)

            def store(i):
                for q in range(2):
                    g = i * 2 + q
                    sp.wait_ge(S["ob_done"], g + 1)
                    settle(sp)
                    if not isinstance(i, int):
                        sp.wait_ge(stored[q], i * 16)
                        settle(sp)
                    sp.dma_start(out_v[:, ds(g * MT, MT), :], outb[q]).then_inc(stored[q], 16)

            run_peeled(sp, NM // 2, store)
            for q in range(2):
                sp.wait_ge(stored[q], NM // 2 * 16)
            for k in range(2):
                sp.wait_ge(x1_saved[k], NSEQ * 16)

        loads = []

        @block.scalar
        def _(act):
            def load(dst, src):
                loads.append(1)
                act.dma_start(dst, src).then_inc(S["consts"], 16)

            act.dma_start(ident[:, :], dram["c_ident"]).then_inc(S["first_consts"], 16)
            act.dma_start(w_in[:, :], dram["in_proj_w"]).then_inc(S["first_consts"], 16)
            load(tri[:, :], dram["c_tri"])
            load(bias4[:, :], dram["dt_bias"].unsqueeze(0).to_broadcast([P, H]))
            load(alog4[:, :], dram["A_log"].unsqueeze(0).to_broadcast([P, H]))
            load(mask_f, dram["c_mask"])
            load(rows_f[0:3 + 3 * H, :], dram["c_rows"])
            load(w_out[:, :, :], dram["out_proj_w"].rearrange("(c p) n -> p c n", p=P))
            load(w_gate[:, :], dram["gate_W"])
            load(nw[:, :], dram["norm_w_cols"])
            load(cw[:, :, :], dram["conv_w"].rearrange("(c p) k -> p c k", p=P))
            load(cb[:, :], dram["conv_b_cols"])
            load(sel_f, dram["c_sel"])
            load(rank0[:, :], dram["c_rank"])
            load(rscale[:, :], dram["route_scale"].unsqueeze(0).to_broadcast([P, 1]))
            load(w1[:, 0:NPAIR * P].rearrange("p (e h) -> p e h", e=NE), dram["W1"].rearrange("e d h -> d e h"))
            load(w1[:, NPAIR * P:], dram["Ws1"])
            load(b1[:, 0:NPAIR], dram["b1_cols"])
            load(b1[0:HID, NPAIR:NF], dram["bs1"].unsqueeze(1))
            load(w2[:, 0:NPAIR, :], dram["W2"].rearrange("(j a) h d -> (a h) j d", j=NPAIR))
            load(w2[0:HID, NPAIR, :], dram["Ws2"])
            for h in range(H):
                load(dskip[(h % 2) * HD:(h % 2 + 1) * HD, h // 2:h // 2 + 1],
                     dram["D_param"][h:h + 1].unsqueeze(0).to_broadcast([HD, 1]))
            act.wait_ge(S["zeroed"], 1)
            for k in range(3):
                load(brow_f[SGRP * k:SGRP * k + NE, :], dram["b2"])
            load(brow_f[3 * SGRP:3 * SGRP + 1, :], dram["bs2"].unsqueeze(0))

            def first_norm(i):
                for k in range(UNITS):
                    g, q = i * UNITS + k, k % 2
                    act.wait_ge(S["p0_tr"], g + 1)
                    wait(act, "p0_dt", g - 1)
                    nc.scalar.activation(stage[q][:, :], proj_bank[q][:, :], ACT.Copy).then_inc(S["p0_evac"], 1)
                    nc.scalar.activation(xT_all[:, ds(g * MW, MW)], proj_bank[q][:, :], ACT.Copy
                                         ).then_inc(S["p0_evac"], 1)
                    if k or not isinstance(i, int):
                        read_dt(g - 1)

            def read_dt(g):
                act.wait_ge(S["p0_dt"], g + 1)
                nc.scalar.activation(dt_all[:, ds(g * MT, MT), :].rearrange("p t h -> p (t h)"),
                                     dt_bank[:, 0:MT * H], ACT.Copy).then_inc(S["p0_dtread"], 1)

            run_peeled(act, NM // UNITS, first_norm)
            read_dt(NM - 1)

            act.wait_ge(S["pre_dve"], 2)
            nc.scalar.activation(s1[2], s1[1], ACT.Exp, scale=-1.0).then_inc(S["pre_exp"], 1)
            act.wait_ge(S["consts"], 16 * len(loads))
            nc.scalar.activation(s1[11][:, 0:H], alog4[:, :], ACT.Exp).then_inc(S["pre_exp"], 1)
            act.wait_ge(S["pre_dve"], 3)
            nc.scalar.activation(s1[4], s1[3], ACT.Ln).then_inc(S["pre_exp"], 1)
            act.wait_ge(S["pre_dve"], 12)
            nc.scalar.activation(dec_all[:, :, :].rearrange("p t h -> p (t h)"), s1[9], ACT.Exp
                                 ).then_inc(S["pre_exp"], 1)
            nc.scalar.activation(tot_all[:, :, :].rearrange("p t h -> p (t h)"), ys_bank[:, 0:TN], ACT.Exp
                                 ).then_inc(S["pre_exp"], 1)

            def emit(s, par, scan, proj, prev):
                for what, k in steps(scan, proj, prev):
                    T = s * TPS + k
                    if what == "exp":
                        act.wait_ge(S["de_done"], T + 1)
                        wait(act, "c_done", (s - 1) * TPS + k + 1)
                        nc.scalar.activation(LE[:, k % TPS, :, :], exp_bank[:, :, :], ACT.Exp).then_inc(S["exp_done"], 1)
                    elif what == "chunk":
                        act.wait_ge(S["bt_done"], T + 1)
                        wait(act, "c_done", T - 1)
                        nc.scalar.activation(Btok[:, k % 2, :], bt_bank[:, 0:P], ACT.Copy).then_inc(S["btok_done"], 1)
                    elif what == "job":
                        _, c, m = JOBS[k]
                        act.wait_ge(S["proj_done"], (s + 1) * NJOB + k + 1)
                        if c < NCONV:
                            wait(act, "y_done", s * TPS)
                            nc.scalar.activation(xbc[:, 1 - par, c, half_of(m)], proj_bank[k % 2][:, :], ACT.Identity,
                                                 scale=cw[:, c, NTAP:KC], bias=cb[:, c:c + 1]).then_inc(S["a0_done"], 1)
                            wait(act, "taps", ((s + 1) * NCONV + c - 1) * NTAP)
                            nc.scalar.activation(raw[:, c % 2, NTAP + m * MW:NTAP + (m + 1) * MW],
                                                 proj_bank[k % 2][:, :], ACT.Copy).then_inc(S["proj_read"], 1)
                        else:
                            wait(act, "ms_done", s * 2 - 1 + m)
                            nc.scalar.activation(zs[:, 1 - par, c - NCONV, half_of(m)],
                                                 proj_bank[k % 2][:, :], ACT.Silu).then_inc(S["proj_read"], 1)
                    elif what == "silu":
                        act.wait_ge(S["taps"], ((s + 1) * NCONV + k + 1) * NTAP)
                        nc.scalar.activation(xbc[:, 1 - par, k, :], xbc[:, 1 - par, k, :], ACT.Silu
                                             ).then_inc(S["xbc_ready"], 1)
                    elif what == "gate":
                        g = s * 2 + k
                        act.wait_ge(S["g_done"], g + 1)
                        nc.scalar.activation(zs[:, par, :, half_of(k)], gbuf[:, :, half_of(k)], ACT.Square
                                             ).then_inc(S["sq_done"], 1)
                    elif what == "ms":
                        g = (s - k) * 2 + k
                        act.wait_ge(S["ms_done"], g + 1)
                        wait(act, "on_done", g)
                        nc.scalar.activation(msb[:, :], bt_bank[:, P:P + MT], ACT.Copy, scale=EPS / INTER,
                                             bias=EPS * EPS).then_inc(S["ms_read"], 1)
                    elif what == "back":
                        g = (s - 1) * 2 + k
                        act.wait_ge(S["tr_done"], g + 1)
                        wait(act, "lg_done", g)
                        nc.scalar.activation(stage[0][:, :], tail_bank[:, :], ACT.Copy).then_inc(S["xft_done"], 1)
                        nc.scalar.activation(xT_all[:, ds(g * MW, MW)] if not isinstance(g, int)
                                             else xT_all[:, g * MW:(g + 1) * MW], tail_bank[:, :], ACT.Copy
                                             ).then_inc(S["xft_done"], 1)
                    elif what == "logits":
                        g = (s - 1) * 2 + k
                        act.wait_ge(S["lg_done"], g + 1)
                        nc.scalar.activation(
                            (logits[:, ds(g * MT, MT), :] if not isinstance(g, int)
                             else logits[:, g * MT:(g + 1) * MT, :]).rearrange("p t e -> p (t e)"),
                            bt_bank[:, 2 * P:2 * P + MT * NE], ACT.Copy).then_inc(S["lg_read"], 1)

            run_bodies(act, emit)

            act.wait_ge(S["y_done"], NT)
            act.wait_ge(S["lg_read"], NM)
            nc.scalar.activation(r1[0], logits[:, :, :], ACT.Exp, scale=-1.0).then_inc(S["route_exp"], 1)

            def ffn(i):
                for q in range(2):
                    g = i * 2 + q
                    act.wait_ge(S["gtt_done"], g + 1)
                    wait(act, "fout_done", g - 1)
                    nc.scalar.activation(gt[q], gt_bank, ACT.Copy).then_inc(S["gt_done"], 1)
                    for j in range(NF):
                        act.wait_ge(S["f1_done"], g * NF + j + 1)
                        src = proj_bank[(q * NF + j) % 2]
                        if j < NPAIR:
                            wait(act, "hg_done", g * NPAIR + j - 1)
                            nc.scalar.activation(hbuf[j % 2], src[:, :], ACT.Gelu, bias=b1[:, j:j + 1]
                                                 ).then_inc(S["gelu_done"], 1)
                        else:
                            nc.scalar.activation(hg[q][j][0:HID, :], src[0:HID, :], ACT.Gelu, bias=b1[0:HID, j:j + 1]
                                                 ).then_inc(S["gelu_done"], 1)

            run_peeled(act, NM // 2, ffn)

        @block.gpsimd
        def _(pool):
            nc.gpsimd.memset(ones[:, :], 1.0).then_inc(S["started"], 1)
            nc.gpsimd.memset(brow_f, 0.0).then_inc(S["zeroed"], 1)
            nc.gpsimd.memset(raw[:, :, 0:NTAP], 0.0).then_inc(S["zeroed"], 1)
            nc.gpsimd.memset(gst[:, :, :, :], 0.0).then_inc(S["zeroed"], 1)
            pool.wait_ge(S["zeroed"], 3)
            nc.gpsimd.memset(gst[:, :, :, 3 * SGRP:3 * SGRP + 1], 1.0).then_inc(S["zeroed"], 1)

            def emit(s, par, scan, proj, prev):
                for what, k in steps(scan, proj, prev):
                    T = s * TPS + k
                    if what == "chunk":
                        if k >= 1:
                            pool.wait_ge(S["exp_done"], T + 1)
                            pool.wait_ge(S["xbc_ready"], (s + 1) * NCONV)
                            e = LE[:, k, 0, :].rearrange("p (h l) -> p h l", h=H)
                            nc.gpsimd.tensor_tensor(e, e, xbc[:, par, NCONV - 1, tile_of(k)].unsqueeze(1)
                                                    .to_broadcast([P, H, P]), ALU.mult).then_inc(S["ch_done"], 1)
                        if k < TPS - 1:
                            pool.wait_ge(S["xdt_done"], T + 1)
                            wait(pool, "c_done", T - 1)
                            dec = dec_all[:, T, :] if isinstance(T, int) else dec_all[:, ds(T, 1), :].rearrange(
                                "p t h -> p (t h)")
                            nc.gpsimd.tensor_tensor(Xw[:, k % 2, :].rearrange("p (h d) -> p h d", h=H),
                                                    Xdt[:, k % 2, :].rearrange("p (h d) -> p h d", h=H),
                                                    dec.unsqueeze(2).to_broadcast([P, H, HD]), ALU.mult
                                                    ).then_inc(S["xw_done"], 1)
                    elif what == "state" and 1 <= k < TPS - 1:
                        pool.wait_ge(S["s_ready"], s * (TPS - 1) + k)
                        tot = tot_all[:, T, :] if isinstance(T, int) else tot_all[:, ds(T, 1), :].rearrange(
                            "p t h -> p (t h)")
                        nc.gpsimd.tensor_tensor(Sd[:, :].rearrange("p (h d) -> p h d", h=H),
                                                St[:, (k - 1) % 2, :].rearrange("p (h d) -> p h d", h=H),
                                                tot.unsqueeze(2).to_broadcast([P, H, HD]), ALU.mult
                                                ).then_inc(S["sd_done"], 1)
                    elif what == "gate":
                        pool.wait_ge(S["sq_done"], s * 2 + k + 1)
                        nc.gpsimd.tensor_tensor(zs[:, par, 0, half_of(k)], zs[:, par, 0, half_of(k)],
                                                zs[:, par, 1, half_of(k)], ALU.add).then_inc(S["sqs_done"], 1)
                    elif what == "chain":
                        g = (s - k) * 2 + k
                        if prev:
                            pool.wait_ge(S["chained"], (g + 1) * LN_CHAIN)
                            wait(pool, "tr_done", g - 1)
                            settle(pool)
                            for t in range(MT):
                                last = nc.gpsimd.tensor_scalar(xn3[0][:, t, :], on[:, 1 - k, t, :],
                                                               nmean[:, MT + t:MT + t + 1], rst[:, MT + t:MT + t + 1],
                                                               ALU.add, ALU.mult)
                            last.then_inc(S["xn3_done"], 1)
                        if k == 1 or scan:
                            pool.wait_ge(S["on_done"], g + 1)
                            nc.gpsimd.tensor_tensor(on[:, k, :, :], on[:, k, :, :],
                                                    x_all[:, ds(g * MT, MT), :] if not isinstance(g, int)
                                                    else x_all[:, g * MT:(g + 1) * MT, :], ALU.add
                                                    ).then_inc(S["x1_done"], 1)

            run_bodies(pool, emit)

            def ffn(i):
                for q in range(2):
                    g = i * 2 + q
                    pool.wait_ge(S["onf_done"], g + 1)
                    if not isinstance(i, int):
                        pool.wait_ge(stored[q], i * 16)
                    else:
                        for k in range(2):
                            pool.wait_ge(x1_saved[k], NSEQ * 16)
                    nc.gpsimd.tensor_tensor(outb[q], onf[q], x_all[:, ds(g * MT, MT), :] if not isinstance(g, int)
                                            else x_all[:, g * MT:(g + 1) * MT, :], ALU.add).then_inc(S["ob_done"], 1)

            run_peeled(pool, NM // 2, ffn)

        @block.vector
        def _(dve):
            MAGIC = float(0x5F3759DF)

            def norm_coefs(sources, chain, at, first, last_col, variance=None):
                def link(ins):
                    nonlocal at
                    at = at + 1
                    ins.then_inc(S[chain], 1)
                    dve.wait_ge(S[chain], at)

                cols = slice(first, last_col)
                v, a, b, yy = veps[:, cols], nt_a[:, cols], nt_b[:, cols], nt_y[:, cols]
                for n, source in enumerate(sources):
                    last = nc.vector.bn_stats(st6[:, first + n, :], source)
                link(last)
                settle(dve)
                for n in range(first, last_col):
                    last = nc.vector.bn_aggr(mv[:, n, :], st6[:, n, :])
                link(last)
                if variance is None:
                    nc.vector.tensor_scalar(nmean[:, cols], mv[:, cols, 0], -1.0, None, ALU.mult)
                    link(nc.vector.tensor_scalar(v, mv[:, cols, 1], EPS, None, ALU.add))
                else:
                    link(variance())
                link(nc.vector.tensor_scalar(a.bitcast(i32), v.bitcast(i32), 1, None, ALU.logical_shift_right))
                link(nc.vector.tensor_scalar(yy.bitcast(i32), a.bitcast(i32), -1.0, MAGIC, ALU.mult, ALU.add))
                for n in range(3):
                    link(nc.vector.tensor_tensor(a, yy, yy, ALU.mult))
                    link(nc.vector.scalar_tensor_tensor(b, a, -0.5, v, ALU.mult, ALU.mult))
                    link(nc.vector.scalar_tensor_tensor(rst[:, cols] if n == 2 else yy, b, 1.5, yy, ALU.add, ALU.mult))

            def first_norm(i):
                sources = []
                for k in range(UNITS):
                    dve.wait_ge(u_in[k], i * 16 + 16)
                    for t in range(MT):
                        at = (i * UNITS + k) * MT + t
                        sources.append(x_all[:, ds(at, 1), :].rearrange("p t d -> p (t d)"))
                settle(dve)
                norm_coefs(sources, "p0_chain", i * LN_CHAIN, 0, NC)
                for k in range(UNITS):
                    wait(dve, "p0_tr", i * UNITS + k - 1)
                    for t in range(MT):
                        n = k * MT + t
                        last = nc.vector.tensor_scalar(xn3[k % 2][:, t, :], sources[n], mv[:, n, 0:1], rst[:, n:n + 1],
                                                       ALU.subtract, ALU.mult)
                    last.then_inc(S["p0_norm"], 1)

            run_peeled(dve, NM // UNITS, first_norm)

            dve.wait_ge(S["consts"], 16 * len(loads))
            dve.wait_ge(S["first_consts"], 32)
            dve.wait_ge(S["zeroed"], 4)
            nc.vector.tensor_copy(identb[:, :], ident[:, :]).then_inc(S["consts_cast"], 1)
            nc.vector.tensor_copy(maskb[:, :, :], mask_f.unsqueeze(1).to_broadcast([P, H, P])).then_inc(S["consts_cast"], 1)
            R = 3 + 3 * H
            nc.vector.tensor_copy(csr[0:R, :, :], rows_f[0:R, 0:H * P].unsqueeze(1).to_broadcast([R, TPS, H * P])
                                  ).then_inc(S["consts_cast"], 1)
            nc.vector.tensor_copy(csl[0:R, :, :], rows_f[0:R, H * P:H * P + P].unsqueeze(1).to_broadcast([R, TPS, P])
                                  ).then_inc(S["consts_cast"], 1)
            for c in range(2):
                nc.vector.tensor_scalar(w_out[:, c, :], w_out[:, c, :], nw[:, c:c + 1], None, ALU.mult
                                        ).then_inc(S["consts_cast"], 1)
            nc.vector.tensor_copy(selb[:, :, :].rearrange("p j m -> p (j m)"), sel_f).then_inc(S["consts_cast"], 1)
            nc.vector.tensor_copy(brow[:, 0, :], brow_f).then_inc(S["consts_cast"], 1)
            dve.wait_ge(S["consts_cast"], 8)
            nc.vector.tensor_tensor(brow_r[:, 0, :], brow_f, brow[:, 0, :], ALU.subtract).then_inc(S["consts_cast"], 1)
            dve.wait_ge(S["consts_cast"], 9)
            nc.vector.tensor_copy(brow[:, 1, :], brow_r[:, 0, :]).then_inc(S["consts_cast"], 1)
            dve.wait_ge(S["consts_cast"], 10)
            nc.vector.tensor_tensor(brow_r[:, 1, :], brow_r[:, 0, :], brow[:, 1, :], ALU.subtract
                                    ).then_inc(S["consts_cast"], 1)
            dve.wait_ge(S["consts_cast"], 11)
            nc.vector.tensor_copy(brow[:, 2, :], brow_r[:, 1, :]).then_inc(S["consts_cast"], 1)

            done = 0

            def pre(ins):
                nonlocal done
                done += 1
                ins.then_inc(S["pre_dve"], 1)
                dve.wait_ge(S["pre_dve"], done)

            dve.wait_ge(S["p0_dtread"], NM)
            v3 = s1[0].rearrange("p (t h) -> p t h", h=H)
            pre(nc.vector.tensor_tensor(v3, dt_all[:, :, :], bias4[:, :].unsqueeze(1).to_broadcast([P, NT, H]), ALU.add))
            pre(nc.vector.scalar_tensor_tensor(s1[1], s1[0], -1.0, s1[0], ALU.mult, ALU.max))
            dve.wait_ge(S["pre_exp"], 1)
            pre(nc.vector.tensor_scalar(s1[3], s1[2], 1.0, None, ALU.add))
            pre(nc.vector.tensor_scalar(s1[5], s1[3], -1.0, None, ALU.add))
            pre(nc.vector.tensor_tensor(s1[6], s1[2], s1[5], ALU.subtract))
            pre(nc.vector.reciprocal(s1[7], s1[3]))
            pre(nc.vector.tensor_tensor(s1[5], s1[6], s1[7], ALU.mult))
            dve.wait_ge(S["pre_exp"], 3)
            pre(nc.vector.scalar_tensor_tensor(s1[6], s1[0], 0.0, s1[4], ALU.max, ALU.add))
            pre(nc.vector.tensor_tensor(dt_all[:, :, :].rearrange("p t h -> p (t h)"), s1[6], s1[5], ALU.add))
            pre(nc.vector.scalar_tensor_tensor(s1[8].rearrange("p (t h) -> p t h", h=H), dt_all[:, :, :], -1.0,
                                               s1[11][:, 0:H].unsqueeze(1).to_broadcast([P, NT, H]), ALU.mult, ALU.mult))
            dve.wait_ge(S["pre_pe"], 1)
            pre(nc.vector.tensor_copy(s1[10], sx_bank[:, 0:TN]))
            pre(nc.vector.tensor_tensor(s1[9], ys_bank[:, 0:TN], s1[10], ALU.subtract))
            dve.wait_ge(S["pre_pe"], 2)
            pre(nc.vector.tensor_copy(csp[:, 0, :], tail_bank[:, 0:TN]))
            pre(nc.vector.tensor_tensor(s1[0], tail_bank[:, 0:TN], csp[:, 0, :], ALU.subtract))
            pre(nc.vector.tensor_copy(csp[:, 1, :], s1[0]))
            pre(nc.vector.tensor_tensor(s1[1], s1[0], csp[:, 1, :], ALU.subtract))
            pre(nc.vector.tensor_copy(csp[:, 2, :], s1[1]))
            assert done == 17

            def emit(s, par, scan, proj, prev):
                for what, k in steps(scan, proj, prev):
                    T = s * TPS + k
                    if what == "chunk":
                        dve.wait_ge(S["b_done"], T + 1)
                        wait(dve, "c_done", T - 1)
                        dt = dt_all[:, T, :] if isinstance(T, int) else dt_all[:, ds(T, 1), :].rearrange(
                            "p t h -> p (t h)")
                        nc.vector.tensor_tensor(Xdt[:, k % 2, :].rearrange("p (h d) -> p h d", h=H),
                                                sx_bank[:, P:P + INTER].rearrange("p (h d) -> p h d", h=H),
                                                dt.unsqueeze(2).to_broadcast([P, H, HD]), ALU.mult
                                                ).then_inc(S["xdt_done"], 1)
                        dve.wait_ge(S["exp_done"], T + 1)
                        m = LE[:, k, 1, :].rearrange("p (h l) -> p h l", h=H)
                        nc.vector.tensor_tensor(m, m, sx_bank[:, 0:P].unsqueeze(1).to_broadcast([P, H, P]), ALU.mult
                                                ).then_inc(S["m_done"], 1)
                    elif what == "conv":
                        n = (s + 1) * NCONV + k
                        dve.wait_ge(S["a0_done"], 2 * n + 2)
                        dve.wait_ge(S["proj_read"], (s + 1) * NJOB + max(n for n, job in enumerate(JOBS) if job[1] == k) + 1)
                        y = xbc[:, 1 - par, k, :]
                        for i in range(NTAP):
                            if i:
                                dve.wait_ge(S["taps"], n * NTAP + i)
                            nc.vector.scalar_tensor_tensor(y, raw[:, k % 2, i:i + SEQ], cw[:, k, i:i + 1], y,
                                                           ALU.mult, ALU.add).then_inc(S["taps"], 1)
                    elif what == "state":
                        dve.wait_ge(S["c_done"], T + 1)
                        if k == 0:
                            nc.vector.tensor_copy(St[:, 0, :], ys_bank[:, INTER:2 * INTER]).then_inc(S["s_ready"], 1)
                        elif k < TPS - 1:
                            dve.wait_ge(S["sd_done"], s * (TPS - 2) + k)
                            nc.vector.tensor_tensor(St[:, k % 2, :], ys_bank[:, INTER:2 * INTER], Sd[:, :], ALU.add
                                                    ).then_inc(S["s_ready"], 1)
                        wait(dve, "out_done", s * 2 - 1 + (k // MT))
                        for c in range(2):
                            last = nc.vector.scalar_tensor_tensor(
                                gbuf[:, c, tile_of(k)], xbc[:, par, c, tile_of(k)], dskip[:, c:c + 1],
                                ys_bank[:, c * P:(c + 1) * P], ALU.mult, ALU.add)
                        last.then_inc(S["y_done"], 1)
                    elif what == "gate":
                        if k == 0:
                            dve.wait_ge(S["proj_read"], (s + 1) * NJOB)
                        dve.wait_ge(S["y_done"], s * TPS + (k + 1) * MT)
                        nc.vector.tensor_tensor(gbuf[:, :, half_of(k)], gbuf[:, :, half_of(k)],
                                                zs[:, par, :, half_of(k)], ALU.mult).then_inc(S["g_done"], 1)
                    elif what == "chain":
                        g = (s - k) * 2 + k
                        norm1 = k == 1 or scan
                        sources = []
                        if norm1:
                            dve.wait_ge(S["out_done"], g + 1)
                            sources += [tail_bank[:, t * D:(t + 1) * D] for t in range(MT)]
                        if prev:
                            dve.wait_ge(S["x1_done"], g)
                            wait(dve, "xn3_done", g - 1)
                            sources += [on[:, 1 - k, t, :] for t in range(MT)]

                        def variance():
                            if prev:
                                last = nc.vector.tensor_scalar(veps[:, MT:2 * MT], mv[:, MT:2 * MT, 1], EPS, None, ALU.add)
                                last = nc.vector.tensor_scalar(nmean[:, MT:2 * MT], mv[:, MT:2 * MT, 0], -1.0, None, ALU.mult)
                            if norm1:
                                dve.wait_ge(S["ms_read"], g + 1)
                                last = nc.vector.tensor_tensor(veps[:, 0:MT], msb[:, :], mv[:, 0:MT, 1], ALU.add)
                            return last

                        norm_coefs(sources, "chained", g * LN_CHAIN, 0 if norm1 else MT, 2 * MT if prev else MT, variance)
                        if norm1:
                            if not isinstance(s, int) or s - k > 0:
                                dve.wait_ge(x1_saved[k], (s - k) * 16)
                            for t in range(MT):
                                last = nc.vector.tensor_scalar(on[:, k, t, :], tail_bank[:, t * D:(t + 1) * D],
                                                               mv[:, t, 0:1], rst[:, t:t + 1],
                                                               ALU.subtract, ALU.mult)
                            last.then_inc(S["on_done"], 1)

            run_bodies(dve, emit)

            done = 0

            def rt(ins):
                nonlocal done
                done += 1
                ins.then_inc(S["route"], 1)
                dve.wait_ge(S["route"], done)

            dve.wait_ge(S["route_exp"], 1)
            rt(nc.vector.tensor_scalar(r1[1], r1[0], 1.0, None, ALU.add))
            rt(nc.vector.reciprocal(r1[2], r1[1]))
            sc, rank, beat = r1[3], r1[4], r1[5]
            rt(nc.vector.tensor_scalar(sc, r1[2], rscale[:, 0:1], None, ALU.mult))
            rt(nc.vector.tensor_copy(rank, rank0[:, :].unsqueeze(1).to_broadcast([P, NT, NE])))
            for d in range(1, NE):
                n = NE - d
                rt(nc.vector.tensor_tensor(beat[:, :, 0:n], sc[:, :, 0:n], sc[:, :, d:NE], ALU.is_ge))
                rt(nc.vector.tensor_tensor(rank[:, :, d:NE], rank[:, :, d:NE], beat[:, :, 0:n], ALU.add))
                rt(nc.vector.tensor_tensor(rank[:, :, 0:n], rank[:, :, 0:n], beat[:, :, 0:n], ALU.subtract))
            rt(nc.vector.scalar_tensor_tensor(r1[0], rank, 1.5, sc, ALU.is_lt, ALU.mult))
            total = r1[1].rearrange("p t e -> p (t e)")
            rt(nc.vector.reduce_sum(total[:, 0:NT], r1[0], mybir.AxisListType.X))
            rt(nc.vector.reciprocal(total[:, NT:2 * NT], total[:, 0:NT]))
            rt(nc.vector.tensor_tensor(r1[2], r1[0], total[:, NT:2 * NT].unsqueeze(2).to_broadcast([P, NT, NE]), ALU.mult))
            rt(nc.vector.tensor_copy(gates[:, :, 0, :], r1[2]))
            rt(nc.vector.tensor_tensor(r1[3], r1[2], gates[:, :, 0, :], ALU.subtract))
            rt(nc.vector.tensor_copy(gates[:, :, 1, :], r1[3]))
            rt(nc.vector.tensor_tensor(r1[4], r1[3], gates[:, :, 1, :], ALU.subtract))
            rt(nc.vector.tensor_copy(gates[:, :, 2, :], r1[4]))


            def last_norm(g, q):
                dve.wait_ge(S["fout_done"], g + 1)
                norm_coefs([fout_bank[q][:, t * D:(t + 1) * D] for t in range(MT)], "fout_chain", g * LN_CHAIN, 0, MT)
                wait(dve, "ob_done", g - 1)
                for t in range(MT):
                    last = nc.vector.tensor_scalar(onf[q][:, t, :], fout_bank[q][:, t * D:(t + 1) * D],
                                                   mv[:, t, 0:1], rst[:, t:t + 1], ALU.subtract, ALU.mult)
                last.then_inc(S["onf_done"], 1)

            def ffn(i):
                for q in range(2):
                    g = i * 2 + q
                    wait(dve, "gtt_done", g - 1)
                    nc.vector.tensor_copy(gst[:, q, :, :].rearrange("p t (k c) -> p t k c", c=SGRP)[:, :, 0:3, 0:NE],
                                          gates[:, ds(g * MT, MT), :, :] if not isinstance(g, int)
                                          else gates[:, g * MT:(g + 1) * MT, :, :]).then_inc(S["gst_done"], 1)
                    for j in range(NPAIR):
                        dve.wait_ge(S["gelu_done"], g * NF + j + 1)
                        dve.wait_ge(S["gb_done"], g * NPAIR + j + 1)
                        if j == 0:
                            wait(dve, "fout_done", g - 1)
                        nc.vector.tensor_tensor(hg[q][j], hbuf[j % 2], exp_bank[:, j % 2, :], ALU.mult
                                                ).then_inc(S["hg_done"], 1)
                    if not (isinstance(g, int) and g == 0):
                        last_norm(g - 1, 1 - q)

            run_peeled(dve, NM // 2, ffn)
            last_norm(NM - 1, 1)

        @block.tensor
        def _(pe):
            mm = nc.tensor.matmul
            pe.wait_ge(S["first_consts"], 32)

            def project_dt(g, q):
                pe.wait_ge(S["p0_evac"], 2 * g + 1)
                wait(pe, "p0_dtread", g)
                for t in range(MT):
                    last = mm(dt_bank[:, t * H:(t + 1) * H], stage[q][:, tile_of(t)], w_in[:, DT0:DT0 + H],
                              start=True, stop=True)
                last.then_inc(S["p0_dt"], 1)

            def first_norm(i):
                for k in range(UNITS):
                    g, q = i * UNITS + k, k % 2
                    pe.wait_ge(S["p0_norm"], g + 1)
                    wait(pe, "p0_evac", 2 * g - 2)
                    for t in range(MT):
                        last = nc.tensor.transpose(proj_bank[q][:, tile_of(t)], xn3[q][:, t, :], ident[:, :])
                    last.then_inc(S["p0_tr"], 1)
                    if k or not isinstance(i, int):
                        project_dt(g - 1, 1 - q)

            run_peeled(pe, NM // UNITS, first_norm)
            project_dt(NM - 1, 1)

            pe.wait_ge(S["consts"], 16 * len(loads))
            pe.wait_ge(S["started"], 1)
            pe.wait_ge(S["pre_dve"], 10)
            mm(sx_bank[:, 0:TN], tri[:, :], s1[8], start=True, stop=True)
            mm(ys_bank[:, 0:TN], ones[:, :], s1[8], start=True, stop=True).then_inc(S["pre_pe"], 1)
            pe.wait_ge(S["pre_dve"], 11)
            for a in range(2):
                last = nc.tensor.transpose(tail_bank[:, tile_of(a)], s1[10][:, tile_of(a)], ident[:, :])
            last.then_inc(S["pre_pe"], 1)
            pe.wait_ge(S["consts_cast"], 12)
            pe.wait_ge(S["pre_exp"], 5)
            pe.wait_ge(S["p0_dtread"], NM)

            def emit(s, par, scan, proj, prev):
                seen = 0
                for what, k in steps(scan, proj, prev):
                    T = s * TPS + k
                    B, C = xbc[:, par, NCONV - 2, :], xbc[:, par, NCONV - 1, :]
                    if what == "exp":
                        j = k % TPS
                        if j % (TPS // 2) == 0:
                            pe.wait_ge(cs_in[j // (TPS // 2)], (s + k // TPS + 1) * 64)
                        wait(pe, "exp_done", T)
                        mm(exp_bank[:, 0, :], csl[0:3, j, :], csr[0:3, j, :], start=True, stop=True)
                        mm(exp_bank[:, 1, :], csl[:, j, :], csr[:, j, :], start=True, stop=False)
                        mm(exp_bank[:, 1, :], identb[:, :], maskb[:, :, :].rearrange("p h l -> p (h l)"),
                           start=False, stop=True).then_inc(S["de_done"], 1)
                    elif what == "chunk":
                        if k == 0:
                            pe.wait_ge(S["xbc_ready"], (s + 1) * NCONV)
                        wait(pe, "m_done", T)
                        nc.tensor.transpose(sx_bank[:, P:2 * P], xbc[:, par, 0, tile_of(k)], ident[:, :])
                        nc.tensor.transpose(sx_bank[:, 2 * P:3 * P], xbc[:, par, 1, tile_of(k)], ident[:, :])
                        mm(sx_bank[:, 0:P], B[:, tile_of(k)], C[:, tile_of(k)], start=True, stop=True
                           ).then_inc(S["b_done"], 1)
                        seen = k + 1
                        wait(pe, "btok_done", T)
                        if k == 0:
                            wait(pe, "lg_read", s * 2 - 2)
                        if k == 3 and prev:
                            wait(pe, "ms_read", s * 2)
                        if k == 4 and prev:
                            wait(pe, "lg_read", s * 2 - 1)
                        if k == 7:
                            wait(pe, "ms_read", s * 2 + 1)
                        nc.tensor.transpose(bt_bank[:, 0:P], B[:, tile_of(k)], ident[:, :]).then_inc(S["bt_done"], 1)
                    elif what == "state":
                        wait(pe, "y_done", T)
                        pe.wait_ge(S["m_done"], T + 1)
                        if k < TPS - 1:
                            pe.wait_ge(S["btok_done"], T + 1)
                            pe.wait_ge(S["xw_done"], s * (TPS - 1) + k + 1)
                            mm(ys_bank[:, INTER:2 * INTER], Btok[:, k % 2, :], Xw[:, k % 2, :], start=True, stop=True)
                        if k:
                            pe.wait_ge(S["ch_done"], s * (TPS - 1) + k)
                            pe.wait_ge(S["s_ready"], s * (TPS - 1) + k)
                        for c in range(2):
                            for part in range(2 if k else 1):
                                for a in range(2):
                                    h = 2 * c + a
                                    lhs = (Xdt[:, k % 2, :] if part == 0 else St[:, (k - 1) % 2, :])[:, h * HD:(h + 1) * HD]
                                    last = mm(ys_bank[a * HD:(a + 1) * HD, c * P:(c + 1) * P], lhs,
                                              LE[:, k, 1 - part, h * P:(h + 1) * P], start=(part == 0),
                                              stop=(part == 1 or not k))
                        last.then_inc(S["c_done"], 1)
                    elif what == "job":
                        _, c, m = JOBS[k]
                        J = (s + 1) * NJOB + k
                        col = CONV0 + c * P if c < NCONV else (c - NCONV) * P
                        wait(pe, "proj_read", J - 1)
                        at = (s + 1) * SEQ + m * MW
                        mm(proj_bank[k % 2][:, :], w_in[:, col:col + P],
                           xT_all[:, ds(at, MW)] if not isinstance(at, int) else xT_all[:, at:at + MW],
                           start=True, stop=True).then_inc(S["proj_done"], 1)
                    elif what == "outproj":
                        g = (s - k) * 2 + k
                        pe.wait_ge(S["g_done"], g + 1)
                        wait(pe, "xft_done", 2 * g - 2)
                        for t in range(MT):
                            at = k * MW + t * P
                            for c in range(2):
                                last = mm(tail_bank[:, t * D:(t + 1) * D], gbuf[:, c, at:at + P], w_out[:, c, :],
                                          start=(c == 0), stop=(c == 1))
                        last.then_inc(S["out_done"], 1)
                    elif what == "ms":
                        g, pq = (s - k) * 2 + k, par if k == 0 else 1 - par
                        pe.wait_ge(S["sqs_done"], g + 1)
                        pe.wait_ge(S["btok_done"], s * TPS + seen)
                        if not scan:
                            pe.wait_ge(S["lg_read"], g - 1)
                        for t in range(MT):
                            at = k * MW + t * P
                            last = mm(bt_bank[:, P + t:P + t + 1], zs[:, pq, 0, at:at + P], ones[:, 0:1],
                                      start=True, stop=True)
                        last.then_inc(S["ms_done"], 1)
                    elif what == "back":
                        g = (s - 1) * 2 + k
                        pe.wait_ge(S["xn3_done"], g + 1)
                        if k == 0 or scan:
                            pe.wait_ge(S["on_done"], g + 2)
                        else:
                            pe.wait_ge(S["xft_done"], 2 * g)
                        for t in range(MT):
                            last = nc.tensor.transpose(tail_bank[:, tile_of(t)], xn3[0][:, t, :], ident[:, :])
                        last.then_inc(S["tr_done"], 1)
                    elif what == "logits":
                        g = (s - 1) * 2 + k
                        pe.wait_ge(S["xft_done"], 2 * g + 1)
                        pe.wait_ge(S["btok_done"], s * TPS + seen)
                        wait(pe, "ms_read", g + 2 if k == 0 or scan else g + 1)
                        for t in range(MT):
                            last = mm(bt_bank[:, 2 * P + t * NE:2 * P + (t + 1) * NE],
                                      stage[0][:, tile_of(t)], w_gate[:, :], start=True, stop=True)
                        last.then_inc(S["lg_done"], 1)

            run_bodies(pe, emit)

            def second(g, q):
                pe.wait_ge(S["hg_done"], (g + 1) * NPAIR)
                pe.wait_ge(S["gelu_done"], (g + 1) * NF)
                wait(pe, "onf_done", g - 1)
                for t in range(MT):
                    o = fout_bank[q][:, t * D:(t + 1) * D]
                    for j in range(NPAIR):
                        mm(o, hg[q][j][:, tile_of(t)], w2[:, j, :], start=(j == 0), stop=False)
                    mm(o, hg[q][NPAIR][0:HID, tile_of(t)], w2[0:HID, NPAIR, :], start=False, stop=False)
                    for n in range(3):
                        last = mm(o, gt[q][:, tile_of(t)], brow[:, n, :], start=False, stop=(n == 2))
                last.then_inc(S["fout_done"], 1)

            def ffn(i):
                for q in range(2):
                    g = i * 2 + q
                    pe.wait_ge(S["gst_done"], g + 1)
                    if isinstance(g, int) and g == 0:
                        pe.wait_ge(S["lg_read"], NM)
                    wait(pe, "gt_done", g)
                    for t in range(MT):
                        last = nc.tensor.transpose(gt_bank[:, tile_of(t)], gst[:, q, t, :], identb[:, :])
                    last.then_inc(S["gtt_done"], 1)
                    for j in range(NF):
                        wait(pe, "gelu_done", g * NF + j - 1)
                        at = g * MW
                        src = xT_all[:, ds(at, MW)] if not isinstance(at, int) else xT_all[:, at:at + MW]
                        if j < NPAIR:
                            mm(proj_bank[(q * NF + j) % 2][:, :], w1[:, j * P:(j + 1) * P], src, start=True, stop=True
                               ).then_inc(S["f1_done"], 1)
                            if j == 0:
                                pe.wait_ge(S["gt_done"], g + 1)
                            wait(pe, "hg_done", g * NPAIR + j - 1)
                            mm(exp_bank[:, j % 2, :], selb[:, j, :], gt[q], start=True, stop=True).then_inc(S["gb_done"], 1)
                        else:
                            settle(pe)
                            mm(proj_bank[(q * NF + j) % 2][0:HID, :], w1[:, NPAIR * P:], src, start=True, stop=True
                               ).then_inc(S["f1_done"], 1)
                        if j == 1 and not (isinstance(g, int) and g == 0):
                            second(g - 1, 1 - q)

            run_peeled(pe, NM // 2, ffn)
            second(NM - 1, 1)


def kernel(**inputs):
    import numpy as _np
    import concourse.bacc as _bacc
    from concourse import mybir as _mybir
    from concourse.bass_utils import run_bass_kernel_spmd as _run

    given = {n.replace("L0_attn_", "").replace("L0_ffn_", ""): _np.asarray(v) for n, v in inputs.items()}
    arrays = {n: given[n] for n in ("u", "in_proj_w", "conv_w", "dt_bias", "A_log", "D_param", "out_proj_w",
                                    "gate_W", "W1", "W2", "b2", "Ws1", "bs1", "Ws2", "bs2", "norm_w")}
    arrays["route_scale"] = given["route_scale"].reshape(1)
    arrays["norm_w_cols"] = given["norm_w"].reshape(-1, 128).T
    arrays["conv_b_cols"] = given["conv_b"].reshape(-1, 128).T
    arrays["b1_cols"] = given["b1"].reshape(-1, 128).T
    one = _np.ones((128, 128), _np.float32)
    arrays["c_ident"] = _np.eye(128, dtype=_np.float32)
    arrays["c_tri"] = _np.triu(one)
    arrays["c_mask"] = _np.tril(one, -1) * _np.float32(-1e30)
    heads = given["dt_bias"].shape[0]
    rows = _np.zeros((3 + 3 * heads, heads * 128 + 128), _np.float32)
    rows[0:3, heads * 128:] = 1.0
    for r in range(3 * heads):
        h = r % heads
        rows[3 + r, h * 128:(h + 1) * 128] = -1.0
    arrays["c_rows"] = rows
    experts, hid = given["W1"].shape[0], given["W1"].shape[2]
    sel = _np.zeros((128, experts * hid), _np.float32)
    for e in range(experts):
        for k in range(3):
            sel[32 * k + e, e * hid:(e + 1) * hid] = 1.0
    arrays["c_sel"] = sel
    arrays["c_rank"] = _np.tile(_np.arange(experts - 1, -1, -1, dtype=_np.float32), (128, 1))

    nc = _bacc.Bacc("TRN2", target_bir_lowering=False, num_devices=1)
    feeds, dram = {}, {}
    for name, a in arrays.items():
        a = _np.ascontiguousarray(a)
        feeds[f"in_{name}"] = a
        dram[name] = nc.dram_tensor(f"in_{name}", a.shape, _mybir.dt.from_np(a.dtype), kind="ExternalInput").ap()
    out = nc.dram_tensor("out_dram", given["u"].shape, _mybir.dt.float32, kind="ExternalOutput").ap()
    ssd_moe_block(nc, dram, out)
    r = _run(nc, [feeds], core_ids=[0])
    return r.results[0]["out_dram"]
```

```python
import concourse.bass as bass
from concourse import mybir
from contextlib import ExitStack


def ssd_moe_block(nc, dram, out):
    f32, bf16, i32 = mybir.dt.float32, mybir.dt.bfloat16, mybir.dt.int32
    ALU, ACT = mybir.AluOpType, mybir.ActivationFunctionType
    ds = bass.ds

    P = 128
    NSEQ, SEQ, D = dram["u"].shape
    INTER = dram["norm_w"].shape[0]
    H = dram["dt_bias"].shape[0]
    HD = INTER // H
    TPS = SEQ // P
    NT = NSEQ * TPS
    MT = 4
    MW = MT * P
    NM = NT // MT
    CONV0 = INTER
    NCONV = (dram["conv_w"].shape[0]) // P
    KC = dram["conv_w"].shape[1]
    DT0 = INTER + NCONV * P
    NE = dram["gate_W"].shape[1]
    HID = dram["W1"].shape[2]
    NPAIR = NE * HID // P
    EPS = 1e-5
    LN_CHAIN = 14
    TAIL_CHAIN = 6
    NEWTON = 12
    UNITS = 4
    SGRP = 32
    ONE = 3 * NE
    PT = 2 * MT
    WEIGH = 13

    u_v = dram["u"].rearrange("s (t p) d -> p (s t) d", p=P)
    out_v = out.rearrange("s (t p) d -> p (s t) d", p=P)

    with ExitStack() as ctx:
        def sb(name, shape, dt=f32):
            return ctx.enter_context(nc.sbuf_tensor(name, shape, dt))

        def sem(name):
            return ctx.enter_context(nc.semaphore(name))

        x_all = sb("x_all", [P, NT, D])
        xT_all = sb("xT_all", [P, NT * P])
        LE = sb("LE", [P, TPS, 2, H * P])
        xbc = sb("xbc", [P, 2, NCONV, SEQ])
        zs = sb("zs", [P, 2, 2, SEQ])
        gbuf = sb("gbuf", [P, 2, SEQ])
        raw = sb("raw", [P, 2, KC - 1 + SEQ])
        Xdt = sb("Xdt", [P, 2, INTER])
        Xw = sb("Xw", [P, 2, INTER])
        St = sb("St", [P, 2, INTER])
        Sd = sb("Sd", [P, INTER])
        Btok = sb("Btok", [P, 2, P])
        on = sb("on", [P, 2, MT, D])
        xn_tile = sb("xn_tile", [P, MT, D])
        stage_tile = sb("stage_tile", [P, MW])
        w_in = sb("w_in", [P, DT0 + H])
        w_gate = sb("w_gate", [P, NE])
        w_out = sb("w_out", [P, 2, D])
        nw = sb("nw", [P, 2])
        cw = sb("cw", [P, NCONV, KC])
        cb = sb("cb", [P, NCONV])
        dskip = sb("dskip", [P, 2])
        ident = sb("ident", [P, P])
        identb = sb("identb", [P, P], bf16)
        tri = sb("tri", [P, P])
        ones = sb("ones", [P, P])
        maskb = sb("maskb", [P, H, P], bf16)
        csl = sb("csl", [3 + 3 * H, TPS, P], bf16)
        csr = sb("csr", [3 + 3 * H, TPS, H * P], bf16)
        bias4 = sb("bias4", [P, H])
        alog4 = sb("alog4", [P, H])
        dt_all = sb("dt_all", [P, NT, H])
        dec_all = sb("dec_all", [P, NT, H])
        tot_all = sb("tot_all", [P, NT, H])
        logits = sb("logits", [P, NT, NE])
        w1 = sb("w1", [P, NPAIR * P + HID])
        b1 = sb("b1", [P, NPAIR + 1])
        w2 = sb("w2", [P, NPAIR + 1, D])
        selb = sb("selb", [P, NPAIR, P], bf16)
        brow = sb("brow", [P, P], bf16)
        gst = sb("gst", [P, 2, MT, P], bf16)
        rank0 = sb("rank0", [P, NE])
        earlier = sb("earlier", [P, NE * NE])
        rscale = sb("rscale", [P, 1])
        NC = UNITS * MT
        st6 = sb("st6", [P, NC, 6])
        mv = sb("mv", [P, NC, 2])
        nt_a = sb("nt_a", [P, NC])
        nt_b = sb("nt_b", [P, NC])
        nt_y = sb("nt_y", [P, NC])
        veps = sb("veps", [P, NC])
        rst = sb("rst", [P, NC])
        nmean = sb("nmean", [P, NC])
        PC = 2 * MT
        mhalf = sb("mhalf", [P, PC])
        pn_a, pn_b, pn_c, pn_y = [sb(f"pn_{n}", [P, PC]) for n in "abcy"]
        three_halves = sb("three_halves", [P, PC])
        gtot = sb("gtot", [P, 2 * PT])
        msb = sb("msb", [P, MT])

        TN = NT * H
        le_flat = LE[:, :, :, :].rearrange("p t a n -> p (t a n)")
        s1 = [le_flat[:, k * TN:(k + 1) * TN] for k in range(12)]
        csp = le_flat[:, 12 * TN:14 * TN].bitcast(bf16)[:, 0:3 * TN].rearrange("p (k n) -> p k n", k=3)
        mask_f = le_flat[:, 16 * TN:16 * TN + P]
        rows_f = le_flat[:, 18 * TN:18 * TN + H * P + P]
        sel_f = le_flat[:, 21 * TN:21 * TN + NPAIR * P]
        brow_f = le_flat[:, 23 * TN:23 * TN + P]
        brow_p = le_flat[:, 14 * TN:15 * TN].bitcast(bf16)[:, 0:3 * P].rearrange("p (k n) -> p k n", k=3)
        brow_r = le_flat[:, 24 * TN:24 * TN + 2 * P].rearrange("p (k n) -> p k n", k=2)
        stage = [stage_tile, le_flat[:, 27 * TN + P:27 * TN + P + MW]]
        xn3 = [xn_tile, le_flat[:, 25 * TN + P:25 * TN + P + MW].rearrange("p (t d) -> p t d", t=MT)]
        NF = NPAIR + 1
        xbc_flat = xbc[:, :, :, :].rearrange("p a c n -> p (a c n)")
        hbuf = [xbc_flat[:, k * MW:(k + 1) * MW] for k in range(2)]
        hg = [[xbc_flat[:, (2 + q * NF + j) * MW:(3 + q * NF + j) * MW] for j in range(NF)] for q in range(2)]
        gt = [xbc_flat[:, 12 * MW + q * (MW // 2):12 * MW + (q + 1) * (MW // 2)].bitcast(bf16) for q in range(2)]
        onf = [xbc_flat[:, (13 + q) * MW:(14 + q) * MW].rearrange("p (t d) -> p t d", t=MT) for q in range(2)]
        r1 = [le_flat[:, k * NT * NE:(k + 1) * NT * NE].rearrange("p (t e) -> p t e", e=NE) for k in range(6)]
        at_rt = 6 * NT * NE
        rank, wins, losses, gate = [le_flat[:, at_rt + k * PT * NE:at_rt + (k + 1) * PT * NE].rearrange(
            "p (t e) -> p t e", e=NE) for k in range(4)]
        at_rt = 10 * MW
        beats, before = [le_flat[:, at_rt + k * PT * NE * NE:at_rt + (k + 1) * PT * NE * NE].rearrange(
            "p (t e f) -> p t e f", e=NE, f=NE) for k in range(2)]
        outb = [le_flat[:, (8 + q) * MW:(9 + q) * MW].rearrange("p (t d) -> p t d", t=MT) for q in range(2)]

        proj_bank = [ctx.enter_context(nc.psum_tensor(f"proj_bank{k}", [P, MW], f32)) for k in range(2)]
        exp_bank = ctx.enter_context(nc.psum_tensor("exp_bank", [P, 2, H * P], f32))
        sx_bank = ctx.enter_context(nc.psum_tensor("sx_bank", [P, 512], f32))
        ys_bank = ctx.enter_context(nc.psum_tensor("ys_bank", [P, 512], f32))
        bt_bank = ctx.enter_context(nc.psum_tensor("bt_bank", [P, 512], f32))
        tail_bank = ctx.enter_context(nc.psum_tensor("tail_bank", [P, 512], f32))
        dt_bank = exp_bank[:, 0, :]
        fout_bank = [sx_bank, ys_bank]
        gt_bank = bt_bank[:, 0:MW // 2].bitcast(bf16)

        cs_rows = nc.dram_tensor("cs_rows", (3, NT * H * P), bf16, kind="Internal").ap()

        names = """settled started first_consts consts consts_cast zeroed rows_out
            p0_chain p0_norm p0_tr p0_evac p0_dt p0_dtread pre_exp pre_dve pre_pe
            proj_done proj_read a0_done taps xbc_ready de_done exp_done b_done bt_done btok_done
            xdt_done m_done ch_done xw_done sd_done c_done s_ready y_done
            g_done sq_done sqs_done ms_done ms_read out_done chained newton on_done x1_done xn3_done
            tr_done xft_done lg_done lg_read route route_exp compared kept weighed gtt_done gt_done f1_done
            gelu_done gb_done hg_done fout_done fout_chain onf_done ob_done""".split()
        S = {n: sem(n) for n in names}
        cs_in = [sem(f"cs_in{k}") for k in range(2)]
        u_in = [sem(f"u_in{k}") for k in range(UNITS)]
        x1_saved = [sem(f"x1_saved{k}") for k in range(2)]
        stored = [sem(f"stored{k}") for k in range(2)]
        block = ctx.enter_context(nc.Block())

        def wait(eng, name, value):
            if isinstance(value, int) and value <= 0:
                return
            eng.wait_ge(S[name], value)

        JOBS = [(0, 0, 0), (0, 0, 1), (1, 1, 0), (2, 1, 1), (2, NCONV, 0), (3, 2, 0), (4, 2, 1), (4, NCONV + 1, 0),
                (5, 3, 0), (6, 3, 1), (6, NCONV, 1), (7, NCONV + 1, 1)]
        NJOB = len(JOBS)

        def settle(eng):
            eng.sem_inc(S["settled"], 1)

        EXPS = {0: (4,), 1: (5, 6), 2: (7,), 4: (8,), 5: (9, 10), 6: (11,)}
        def steps(scan, proj, prev):
            for t in range(TPS + 1):
                if scan and t < TPS:
                    yield "chunk", t
                exps = EXPS.get(t, ()) if (scan if t < TPS // 2 else proj) else ()
                early, late = (exps[:0], exps) if t == TPS // 2 else (exps[:1], exps[1:])
                for k in early:
                    yield "exp", k
                if proj and t % 2 == 0 and t:
                    yield "silu", t // 2 - 1
                if prev and t in (0, 2, 4, 5):
                    yield {0: ("square", 1), 2: ("ms", 1), 4: ("x1", 1), 5: ("logits", 0)}[t]
                if prev and t == 1:
                    yield "outproj", 1
                if scan and t in (5, 6, 8):
                    yield {5: "outproj", 6: "ms", 8: "x1"}[t], 0
                if proj:
                    for n, (slot, c, m) in enumerate(JOBS):
                        if slot == t:
                            yield "job", n
                if scan and t == 5:
                    yield "square", 0
                if proj and t < TPS:
                    yield "conv", t
                if prev and t == 2:
                    yield "chain", 1
                if (scan or prev) and t == 6:
                    yield "chain", 0
                for k in late:
                    yield "exp", k
                if prev and t == 3:
                    yield "apply", 1
                if scan and t == 7:
                    yield "apply", 0
                if prev and t in (4, 8):
                    yield "back", t // 4 - 1
                if scan and t >= 1:
                    yield "state", t - 1
                if prev and t == 8:
                    yield "logits", 1
                if scan and t in (4, 8):
                    yield "gate", t // 4 - 1

        def run_bodies(eng, emit, before_last=None):
            emit(-1, 1, False, True, False)
            emit(0, 0, True, True, False)
            with eng.Fori(0, (NSEQ - 2) // 2) as i:
                emit(i * 2 + 1, 1, True, True, True)
                emit(i * 2 + 2, 0, True, True, True)
            emit(NSEQ - 1, 1, True, False, True)
            if before_last:
                before_last()
            emit(NSEQ, 0, False, False, True)

        def run_peeled(eng, count, emit):
            emit(0)
            with eng.Fori(1, count) as i:
                emit(i)

        NTAP = KC - 1

        def half_of(m):
            return slice(m * MW, (m + 1) * MW)

        def tile_of(t):
            return slice(t * P, (t + 1) * P)

        @block.sync
        def _(sp):
            def units(i):
                for k in range(UNITS):
                    g = i * UNITS + k
                    if not isinstance(i, int):
                        sp.wait_ge(u_in[k], i * 16)
                        settle(sp)
                    sp.dma_start(x_all[:, ds(g * MT, MT), :], u_v[:, ds(g * MT, MT), :]).then_inc(u_in[k], 16)

            run_peeled(sp, NM // UNITS, units)
            sp.wait_ge(S["pre_dve"], 17)
            for k in range(3):
                sp.dma_start(cs_rows[k, :].rearrange("(a r l) -> r a l", a=2, l=P),
                             csp[:, k, :].rearrange("p (a l) -> p a l", a=2)).then_inc(S["rows_out"], 16)
            sp.wait_ge(S["rows_out"], 48)

            def load_rows(s, half):
                HT = TPS // 2
                at = s * (TPS * H * P) + half * (HT * H * P)
                to = slice(half * HT, (half + 1) * HT)
                sp.dma_start(csr[0:3, to, :], cs_rows[:, ds(at, HT * H * P)].rearrange("k (t n) -> k t n", t=HT)
                             ).then_inc(cs_in[half], 16)
                for k in range(3):
                    src = cs_rows[k, ds(at, HT * H * P)].rearrange("(t h l) -> h t l", t=HT, h=H)
                    sp.dma_start(csl[3 + H * k:3 + H * k + H, to, :], src).then_inc(cs_in[half], 16)

            sp.wait_ge(S["consts_cast"], 4)
            load_rows(0, 0)
            load_rows(0, 1)

            def emit(s, par, scan, proj, prev):
                for what, k in steps(scan, proj, prev):
                    if what == "x1":
                        g = (s - k) * 2 + k
                        sp.wait_ge(S["x1_done"], g + 1)
                        settle(sp)
                        sp.dma_start(x_all[:, ds(g * MT, MT), :] if not isinstance(g, int)
                                     else x_all[:, g * MT:(g + 1) * MT, :], on[:, k, :, :]).then_inc(x1_saved[k], 16)
                    elif what == "chunk" and proj and k in (0, 3):
                        half = min(k, 1)
                        sp.wait_ge(S["de_done"], s * TPS + (half + 1) * TPS // 2)
                        sp.wait_ge(cs_in[half], (s + 1) * 64)
                        settle(sp)
                        load_rows(s + 1, half)

            run_bodies(sp, emit)

            def store(i):
                for q in range(2):
                    g = i * 2 + q
                    sp.wait_ge(S["ob_done"], g + 3)
                    settle(sp)
                    if not isinstance(i, int):
                        sp.wait_ge(stored[q], i * 16)
                        settle(sp)
                    sp.dma_start(out_v[:, ds(g * MT, MT), :], outb[q]).then_inc(stored[q], 16)

            run_peeled(sp, NM // 2, store)
            for q in range(2):
                sp.wait_ge(stored[q], NM // 2 * 16)
            for k in range(2):
                sp.wait_ge(x1_saved[k], NSEQ * 16)

        loads = []

        @block.scalar
        def _(act):
            def load(dst, src):
                loads.append(1)
                act.dma_start(dst, src).then_inc(S["consts"], 16)

            act.dma_start(ident[:, :], dram["c_ident"]).then_inc(S["first_consts"], 16)
            act.dma_start(w_in[:, :], dram["in_proj_w"]).then_inc(S["first_consts"], 16)
            load(tri[:, :], dram["c_tri"])
            load(bias4[:, :], dram["dt_bias"].unsqueeze(0).to_broadcast([P, H]))
            load(alog4[:, :], dram["A_log"].unsqueeze(0).to_broadcast([P, H]))
            load(mask_f, dram["c_mask"])
            load(rows_f[0:3 + 3 * H, :], dram["c_rows"])
            load(w_out[:, :, :], dram["out_proj_w"].rearrange("(c p) n -> p c n", p=P))
            load(w_gate[:, :], dram["gate_W"])
            load(nw[:, :], dram["norm_w_cols"])
            load(cw[:, :, :], dram["conv_w"].rearrange("(c p) k -> p c k", p=P))
            load(cb[:, :], dram["conv_b_cols"])
            load(sel_f, dram["c_sel"])
            load(rank0[:, :], dram["c_rank"])
            load(earlier[:, :], dram["c_earlier"])
            load(rscale[:, :], dram["route_scale"].unsqueeze(0).to_broadcast([P, 1]))
            load(w1[:, 0:NPAIR * P].rearrange("p (e h) -> p e h", e=NE), dram["W1"].rearrange("e d h -> d e h"))
            load(w1[:, NPAIR * P:], dram["Ws1"])
            load(b1[:, 0:NPAIR], dram["b1_cols"])
            load(b1[0:HID, NPAIR:NF], dram["bs1"].unsqueeze(1))
            load(w2[:, 0:NPAIR, :], dram["W2"].rearrange("(j a) h d -> (a h) j d", j=NPAIR))
            load(w2[0:HID, NPAIR, :], dram["Ws2"])
            for h in range(H):
                load(dskip[(h % 2) * HD:(h % 2 + 1) * HD, h // 2:h // 2 + 1],
                     dram["D_param"][h:h + 1].unsqueeze(0).to_broadcast([HD, 1]))
            act.wait_ge(S["zeroed"], 1)
            for k in range(3):
                for n in range(3):
                    load(brow_f[SGRP * k + NE * n:SGRP * k + NE * n + NE, :], dram["b2"])
                load(brow_f[SGRP * k + ONE:SGRP * k + ONE + 1, :], dram["bs2"].unsqueeze(0))

            def first_norm(i):
                for k in range(UNITS):
                    g, q = i * UNITS + k, k % 2
                    act.wait_ge(S["p0_tr"], g + 1)
                    wait(act, "p0_dt", g - 1)
                    nc.scalar.activation(stage[q][:, :], proj_bank[q][:, :], ACT.Copy).then_inc(S["p0_evac"], 1)
                    nc.scalar.activation(xT_all[:, ds(g * MW, MW)], proj_bank[q][:, :], ACT.Copy
                                         ).then_inc(S["p0_evac"], 1)
                    if k or not isinstance(i, int):
                        read_dt(g - 1)

            def read_dt(g):
                act.wait_ge(S["p0_dt"], g + 1)
                nc.scalar.activation(dt_all[:, ds(g * MT, MT), :].rearrange("p t h -> p (t h)"),
                                     dt_bank[:, 0:MT * H], ACT.Copy).then_inc(S["p0_dtread"], 1)

            run_peeled(act, NM // UNITS, first_norm)
            read_dt(NM - 1)

            act.wait_ge(S["pre_dve"], 2)
            nc.scalar.activation(s1[2], s1[1], ACT.Exp, scale=-1.0).then_inc(S["pre_exp"], 1)
            act.wait_ge(S["consts"], 16 * len(loads))
            nc.scalar.activation(s1[11][:, 0:H], alog4[:, :], ACT.Exp).then_inc(S["pre_exp"], 1)
            act.wait_ge(S["pre_dve"], 3)
            nc.scalar.activation(s1[4], s1[3], ACT.Ln).then_inc(S["pre_exp"], 1)
            act.wait_ge(S["pre_dve"], 12)
            nc.scalar.activation(dec_all[:, :, :].rearrange("p t h -> p (t h)"), s1[9], ACT.Exp
                                 ).then_inc(S["pre_exp"], 1)
            nc.scalar.activation(tot_all[:, :, :].rearrange("p t h -> p (t h)"), ys_bank[:, 0:TN], ACT.Exp
                                 ).then_inc(S["pre_exp"], 1)

            def emit(s, par, scan, proj, prev):
                for what, k in steps(scan, proj, prev):
                    T = s * TPS + k
                    if what == "exp":
                        act.wait_ge(S["de_done"], T + 1)
                        wait(act, "c_done", (s - 1) * TPS + k + 1)
                        nc.scalar.activation(LE[:, k % TPS, :, :], exp_bank[:, :, :], ACT.Exp).then_inc(S["exp_done"], 1)
                    elif what == "chunk":
                        act.wait_ge(S["bt_done"], T + 1)
                        wait(act, "c_done", T - 1)
                        nc.scalar.activation(Btok[:, k % 2, :], bt_bank[:, 0:P], ACT.Copy).then_inc(S["btok_done"], 1)
                    elif what == "job":
                        _, c, m = JOBS[k]
                        act.wait_ge(S["proj_done"], (s + 1) * NJOB + k + 1)
                        if c < NCONV:
                            wait(act, "y_done", s * TPS)
                            nc.scalar.activation(xbc[:, 1 - par, c, half_of(m)], proj_bank[k % 2][:, :], ACT.Identity,
                                                 scale=cw[:, c, NTAP:KC], bias=cb[:, c:c + 1]).then_inc(S["a0_done"], 1)
                            wait(act, "taps", ((s + 1) * 2 * NCONV + 2 * c - 2) * NTAP)
                            nc.scalar.activation(raw[:, c % 2, NTAP + m * MW:NTAP + (m + 1) * MW],
                                                 proj_bank[k % 2][:, :], ACT.Copy).then_inc(S["proj_read"], 1)
                        else:
                            wait(act, "ms_done", s * 2 - 1 + m)
                            nc.scalar.activation(zs[:, 1 - par, c - NCONV, half_of(m)],
                                                 proj_bank[k % 2][:, :], ACT.Silu).then_inc(S["proj_read"], 1)
                    elif what == "silu":
                        act.wait_ge(S["taps"], ((s + 1) * 2 * NCONV + 2 * k + 2) * NTAP)
                        nc.scalar.activation(xbc[:, 1 - par, k, :], xbc[:, 1 - par, k, :], ACT.Silu
                                             ).then_inc(S["xbc_ready"], 1)
                    elif what == "square":
                        g, pq = (s - k) * 2 + k, par if k == 0 else 1 - par
                        act.wait_ge(S["g_done"], g + 1)
                        nc.scalar.activation(zs[:, pq, :, half_of(k)], gbuf[:, :, half_of(k)], ACT.Square
                                             ).then_inc(S["sq_done"], 1)
                    elif what == "ms":
                        g = (s - k) * 2 + k
                        act.wait_ge(S["ms_done"], g + 1)
                        wait(act, "on_done", g)
                        nc.scalar.activation(msb[:, :], bt_bank[:, P:P + MT], ACT.Copy, scale=EPS / INTER,
                                             bias=EPS * EPS).then_inc(S["ms_read"], 1)
                    elif what == "back":
                        g = (s - 1) * 2 + k
                        act.wait_ge(S["tr_done"], g + 1)
                        wait(act, "lg_done", g)
                        nc.scalar.activation(stage[0][:, :], tail_bank[:, :], ACT.Copy).then_inc(S["xft_done"], 1)
                        nc.scalar.activation(xT_all[:, ds(g * MW, MW)] if not isinstance(g, int)
                                             else xT_all[:, g * MW:(g + 1) * MW], tail_bank[:, :], ACT.Copy
                                             ).then_inc(S["xft_done"], 1)
                    elif what == "logits":
                        g = (s - 1) * 2 + k
                        act.wait_ge(S["lg_done"], g + 1)
                        nc.scalar.activation(
                            (logits[:, ds(g * MT, MT), :] if not isinstance(g, int)
                             else logits[:, g * MT:(g + 1) * MT, :]).rearrange("p t e -> p (t e)"),
                            bt_bank[:, 2 * P:2 * P + MT * NE], ACT.Copy).then_inc(S["lg_read"], 1)

            def route_exp(tiles):
                nc.scalar.activation(r1[0][:, tiles, :], logits[:, tiles, :], ACT.Exp, scale=-1.0
                                     ).then_inc(S["route_exp"], 1)

            def first_scores():
                act.wait_ge(S["y_done"], NT)
                act.wait_ge(S["lg_read"], NM - 2)
                route_exp(slice(0, NT - PT))

            run_bodies(act, emit, first_scores)
            act.wait_ge(S["lg_read"], NM)
            route_exp(slice(NT - PT, NT))

            def ffn(i):
                for q in range(2):
                    g = i * 2 + q
                    act.wait_ge(S["gtt_done"], g + 1)
                    wait(act, "fout_done", g - 1)
                    nc.scalar.activation(gt[q], gt_bank, ACT.Copy).then_inc(S["gt_done"], 1)
                    for n in range(NF):
                        j = (n - 1) % NF
                        act.wait_ge(S["f1_done"], g * NF + n + 1)
                        src = proj_bank[(q * NF + n) % 2]
                        if j < NPAIR:
                            wait(act, "hg_done", g * NPAIR + j - 1)
                            nc.scalar.activation(hbuf[j % 2], src[:, :], ACT.Gelu, bias=b1[:, j:j + 1]
                                                 ).then_inc(S["gelu_done"], 1)
                        else:
                            nc.scalar.activation(hg[q][j][0:HID, :], src[0:HID, :], ACT.Gelu, bias=b1[0:HID, j:j + 1]
                                                 ).then_inc(S["gelu_done"], 1)

            run_peeled(act, NM // 2, ffn)

        @block.gpsimd
        def _(pool):
            nc.gpsimd.memset(ones[:, :], 1.0).then_inc(S["started"], 1)
            nc.gpsimd.memset(brow_f, 0.0).then_inc(S["zeroed"], 1)
            nc.gpsimd.memset(raw[:, :, 0:NTAP], 0.0).then_inc(S["zeroed"], 1)
            nc.gpsimd.memset(three_halves[:, :], 1.5)
            nc.gpsimd.memset(gst[:, :, :, :], 0.0).then_inc(S["zeroed"], 1)
            pool.wait_ge(S["zeroed"], 3)
            nc.gpsimd.memset(gst[:, :, :, 0:3 * SGRP].rearrange("p a t (k c) -> p a t k c", c=SGRP)[:, :, :, :, ONE:ONE + 1],
                             1.0).then_inc(S["zeroed"], 1)

            def decay_state(s, k):
                T = s * TPS + k
                pool.wait_ge(S["s_ready"], s * (TPS - 1) + k)
                tot = tot_all[:, T, :] if isinstance(T, int) else tot_all[:, ds(T, 1), :].rearrange("p t h -> p (t h)")
                nc.gpsimd.tensor_tensor(Sd[:, :].rearrange("p (h d) -> p h d", h=H),
                                        St[:, (k - 1) % 2, :].rearrange("p (h d) -> p h d", h=H),
                                        tot.unsqueeze(2).to_broadcast([P, H, HD]), ALU.mult).then_inc(S["sd_done"], 1)

            def emit(s, par, scan, proj, prev):
                for what, k in steps(scan, proj, prev):
                    T = s * TPS + k
                    if what == "chunk":
                        if 2 <= k < TPS:
                            decay_state(s, k - 1)
                        if k >= 1:
                            pool.wait_ge(S["exp_done"], T + 1)
                            pool.wait_ge(S["xbc_ready"], (s + 1) * NCONV)
                            e = LE[:, k, 0, :].rearrange("p (h l) -> p h l", h=H)
                            nc.gpsimd.tensor_tensor(e, e, xbc[:, par, NCONV - 1, tile_of(k)].unsqueeze(1)
                                                    .to_broadcast([P, H, P]), ALU.mult).then_inc(S["ch_done"], 1)
                        if k < TPS - 1:
                            pool.wait_ge(S["xdt_done"], T + 1)
                            wait(pool, "c_done", T - 1)
                            dec = dec_all[:, T, :] if isinstance(T, int) else dec_all[:, ds(T, 1), :].rearrange(
                                "p t h -> p (t h)")
                            nc.gpsimd.tensor_tensor(Xw[:, k % 2, :].rearrange("p (h d) -> p h d", h=H),
                                                    Xdt[:, k % 2, :].rearrange("p (h d) -> p h d", h=H),
                                                    dec.unsqueeze(2).to_broadcast([P, H, HD]), ALU.mult
                                                    ).then_inc(S["xw_done"], 1)
                    elif what == "square":
                        g, pq = (s - k) * 2 + k, par if k == 0 else 1 - par
                        pool.wait_ge(S["sq_done"], g + 1)
                        nc.gpsimd.tensor_tensor(zs[:, pq, 0, half_of(k)], zs[:, pq, 0, half_of(k)],
                                                zs[:, pq, 1, half_of(k)], ALU.add).then_inc(S["sqs_done"], 1)
                    elif what == "chain":
                        g = (s - k) * 2 + k
                        pool.wait_ge(S["chained"], (g + 1) * TAIL_CHAIN)
                        newton_steps(g * NEWTON, slice(0 if k == 1 or scan else MT, 2 * MT if prev else MT))
                        if prev:
                            wait(pool, "tr_done", g - 1)
                            settle(pool)
                            for t in range(MT):
                                last = nc.gpsimd.tensor_scalar(xn3[0][:, t, :], on[:, 1 - k, t, :],
                                                               nmean[:, MT + t:MT + t + 1], rst[:, MT + t:MT + t + 1],
                                                               ALU.add, ALU.mult)
                            last.then_inc(S["xn3_done"], 1)
                    elif what == "x1":
                        g = (s - k) * 2 + k
                        pool.wait_ge(S["on_done"], g + 1)
                        nc.gpsimd.tensor_tensor(on[:, k, :, :], on[:, k, :, :],
                                                x_all[:, ds(g * MT, MT), :] if not isinstance(g, int)
                                                else x_all[:, g * MT:(g + 1) * MT, :], ALU.add
                                                ).then_inc(S["x1_done"], 1)

            def newton_steps(at, cols):
                def link(ins):
                    nonlocal at
                    at = at + 1
                    ins.then_inc(S["newton"], 1)
                    pool.wait_ge(S["newton"], at)

                y = nt_y
                for n in range(3):
                    new = rst if n == 2 else pn_y
                    link(nc.gpsimd.tensor_tensor(pn_a[:, cols], y[:, cols], y[:, cols], ALU.mult))
                    link(nc.gpsimd.tensor_tensor(pn_b[:, cols], pn_a[:, cols], mhalf[:, cols], ALU.mult))
                    link(nc.gpsimd.tensor_tensor(pn_c[:, cols], pn_b[:, cols], three_halves[:, cols], ALU.add))
                    link(nc.gpsimd.tensor_tensor(new[:, cols], pn_c[:, cols], y[:, cols], ALU.mult))
                    y = pn_y

            def keep_earlier(i):
                pool.wait_ge(S["compared"], i + 1)
                wait(pool, "weighed", i * WEIGH)
                nc.gpsimd.tensor_tensor(before, beats, earlier[:, :].rearrange("p (e f) -> p e f", f=NE).unsqueeze(1)
                                        .to_broadcast([P, PT, NE, NE]), ALU.mult).then_inc(S["kept"], 1)

            run_bodies(pool, emit, lambda: keep_earlier(0))
            for k in range(2):
                pool.wait_ge(x1_saved[k], NSEQ * 16)

            def output(i, q):
                g = i * 2 + q
                pool.wait_ge(S["onf_done"], g + 1)
                if not isinstance(i, int) or i:
                    pool.wait_ge(stored[q], i * 16)
                settle(pool)
                nc.gpsimd.tensor_tensor(outb[q], onf[q], x_all[:, ds(g * MT, MT), :] if not isinstance(g, int)
                                        else x_all[:, g * MT:(g + 1) * MT, :], ALU.add).then_inc(S["ob_done"], 1)

            pool.sem_inc(S["ob_done"], 2)
            keep_earlier(1)
            keep_earlier(2)
            output(0, 0)
            output(0, 1)
            with pool.Fori(1, NM // 2 - 2) as i:
                keep_earlier(i + 2)
                output(i, 0)
                output(i, 1)
            for i in range(NM // 2 - 2, NM // 2):
                output(i, 0)
                output(i, 1)

        @block.vector
        def _(dve):
            MAGIC = float(0x5F3759DF)

            def norm_coefs(sources, chain, at, first, last_col, variance=None, pause=None, guess_only=False):
                def link(ins):
                    nonlocal at
                    at = at + 1
                    ins.then_inc(S[chain], 1)
                    dve.wait_ge(S[chain], at)

                cols = slice(first, last_col)
                v, a, b, yy = veps[:, cols], nt_a[:, cols], nt_b[:, cols], nt_y[:, cols]
                for n, source in enumerate(sources):
                    last = nc.vector.bn_stats(st6[:, first + n, :], source)
                link(last)
                if pause:
                    pause(1)
                settle(dve)
                for n in range(first, last_col):
                    last = nc.vector.bn_aggr(mv[:, n, :], st6[:, n, :])
                link(last)
                if variance is None:
                    nc.vector.tensor_scalar(nmean[:, cols], mv[:, cols, 0], -1.0, None, ALU.mult)
                    link(nc.vector.tensor_scalar(v, mv[:, cols, 1], EPS, None, ALU.add))
                else:
                    link(variance())
                link(nc.vector.tensor_scalar(a.bitcast(i32), v.bitcast(i32), 1, None, ALU.logical_shift_right))
                link(nc.vector.tensor_scalar(yy.bitcast(i32), a.bitcast(i32), -1.0, MAGIC, ALU.mult, ALU.add))
                if guess_only:
                    link(nc.vector.tensor_scalar(mhalf[:, cols], v, -0.5, None, ALU.mult))
                    return
                for n in range(3):
                    if pause and n < 2:
                        pause(2 + n)
                    link(nc.vector.tensor_tensor(a, yy, yy, ALU.mult))
                    link(nc.vector.scalar_tensor_tensor(b, a, -0.5, v, ALU.mult, ALU.mult))
                    link(nc.vector.scalar_tensor_tensor(rst[:, cols] if n == 2 else yy, b, 1.5, yy, ALU.add, ALU.mult))

            def first_norm(i):
                sources = []
                for k in range(UNITS):
                    dve.wait_ge(u_in[k], i * 16 + 16)
                    for t in range(MT):
                        at = (i * UNITS + k) * MT + t
                        sources.append(x_all[:, ds(at, 1), :].rearrange("p t d -> p (t d)"))
                settle(dve)
                norm_coefs(sources, "p0_chain", i * LN_CHAIN, 0, NC)
                for k in range(UNITS):
                    wait(dve, "p0_tr", i * UNITS + k - 1)
                    for t in range(MT):
                        n = k * MT + t
                        last = nc.vector.tensor_scalar(xn3[k % 2][:, t, :], sources[n], mv[:, n, 0:1], rst[:, n:n + 1],
                                                       ALU.subtract, ALU.mult)
                    last.then_inc(S["p0_norm"], 1)

            run_peeled(dve, NM // UNITS, first_norm)

            dve.wait_ge(S["consts"], 16 * len(loads))
            dve.wait_ge(S["first_consts"], 32)
            dve.wait_ge(S["zeroed"], 4)
            nc.vector.tensor_copy(identb[:, :], ident[:, :]).then_inc(S["consts_cast"], 1)
            nc.vector.tensor_copy(maskb[:, :, :], mask_f.unsqueeze(1).to_broadcast([P, H, P])).then_inc(S["consts_cast"], 1)
            R = 3 + 3 * H
            nc.vector.tensor_copy(csr[0:R, :, :], rows_f[0:R, 0:H * P].unsqueeze(1).to_broadcast([R, TPS, H * P])
                                  ).then_inc(S["consts_cast"], 1)
            nc.vector.tensor_copy(csl[0:R, :, :], rows_f[0:R, H * P:H * P + P].unsqueeze(1).to_broadcast([R, TPS, P])
                                  ).then_inc(S["consts_cast"], 1)
            for c in range(2):
                nc.vector.tensor_scalar(w_out[:, c, :], w_out[:, c, :], nw[:, c:c + 1], None, ALU.mult
                                        ).then_inc(S["consts_cast"], 1)
            nc.vector.tensor_copy(selb[:, :, :].rearrange("p j m -> p (j m)"), sel_f).then_inc(S["consts_cast"], 1)
            nc.vector.tensor_copy(brow_p[:, 0, :], brow_f).then_inc(S["consts_cast"], 1)
            dve.wait_ge(S["consts_cast"], 8)
            nc.vector.tensor_tensor(brow_r[:, 0, :], brow_f, brow_p[:, 0, :], ALU.subtract).then_inc(S["consts_cast"], 1)
            dve.wait_ge(S["consts_cast"], 9)
            nc.vector.tensor_copy(brow_p[:, 1, :], brow_r[:, 0, :]).then_inc(S["consts_cast"], 1)
            dve.wait_ge(S["consts_cast"], 10)
            nc.vector.tensor_tensor(brow_r[:, 1, :], brow_r[:, 0, :], brow_p[:, 1, :], ALU.subtract
                                    ).then_inc(S["consts_cast"], 1)
            dve.wait_ge(S["consts_cast"], 11)
            nc.vector.tensor_copy(brow_p[:, 2, :], brow_r[:, 1, :]).then_inc(S["consts_cast"], 1)
            dve.wait_ge(S["consts_cast"], 12)
            for k in range(4):
                rows = slice(SGRP * k, SGRP * (k + 1))
                nc.vector.tensor_copy(brow[rows, :], brow_p[rows, k % 3, :]).then_inc(S["consts_cast"], 1)

            done = 0

            def pre(ins):
                nonlocal done
                done += 1
                ins.then_inc(S["pre_dve"], 1)
                dve.wait_ge(S["pre_dve"], done)

            dve.wait_ge(S["p0_dtread"], NM)
            v3 = s1[0].rearrange("p (t h) -> p t h", h=H)
            pre(nc.vector.tensor_tensor(v3, dt_all[:, :, :], bias4[:, :].unsqueeze(1).to_broadcast([P, NT, H]), ALU.add))
            pre(nc.vector.scalar_tensor_tensor(s1[1], s1[0], -1.0, s1[0], ALU.mult, ALU.max))
            dve.wait_ge(S["pre_exp"], 1)
            pre(nc.vector.tensor_scalar(s1[3], s1[2], 1.0, None, ALU.add))
            pre(nc.vector.tensor_scalar(s1[5], s1[3], -1.0, None, ALU.add))
            pre(nc.vector.tensor_tensor(s1[6], s1[2], s1[5], ALU.subtract))
            pre(nc.vector.reciprocal(s1[7], s1[3]))
            pre(nc.vector.tensor_tensor(s1[5], s1[6], s1[7], ALU.mult))
            dve.wait_ge(S["pre_exp"], 3)
            pre(nc.vector.scalar_tensor_tensor(s1[6], s1[0], 0.0, s1[4], ALU.max, ALU.add))
            pre(nc.vector.tensor_tensor(dt_all[:, :, :].rearrange("p t h -> p (t h)"), s1[6], s1[5], ALU.add))
            pre(nc.vector.scalar_tensor_tensor(s1[8].rearrange("p (t h) -> p t h", h=H), dt_all[:, :, :], -1.0,
                                               s1[11][:, 0:H].unsqueeze(1).to_broadcast([P, NT, H]), ALU.mult, ALU.mult))
            dve.wait_ge(S["pre_pe"], 1)
            pre(nc.vector.tensor_copy(s1[10], sx_bank[:, 0:TN]))
            pre(nc.vector.tensor_tensor(s1[9], ys_bank[:, 0:TN], s1[10], ALU.subtract))
            dve.wait_ge(S["pre_pe"], 2)
            pre(nc.vector.tensor_copy(csp[:, 0, :], tail_bank[:, 0:TN]))
            pre(nc.vector.tensor_tensor(s1[0], tail_bank[:, 0:TN], csp[:, 0, :], ALU.subtract))
            pre(nc.vector.tensor_copy(csp[:, 1, :], s1[0]))
            pre(nc.vector.tensor_tensor(s1[1], s1[0], csp[:, 1, :], ALU.subtract))
            pre(nc.vector.tensor_copy(csp[:, 2, :], s1[1]))
            assert done == 17

            def emit(s, par, scan, proj, prev):
                for what, k in steps(scan, proj, prev):
                    T = s * TPS + k
                    if what == "chunk":
                        dve.wait_ge(S["b_done"], T + 1)
                        wait(dve, "c_done", T - 1)
                        dt = dt_all[:, T, :] if isinstance(T, int) else dt_all[:, ds(T, 1), :].rearrange(
                            "p t h -> p (t h)")
                        nc.vector.tensor_tensor(Xdt[:, k % 2, :].rearrange("p (h d) -> p h d", h=H),
                                                sx_bank[:, P:P + INTER].rearrange("p (h d) -> p h d", h=H),
                                                dt.unsqueeze(2).to_broadcast([P, H, HD]), ALU.mult
                                                ).then_inc(S["xdt_done"], 1)
                        dve.wait_ge(S["exp_done"], T + 1)
                        m = LE[:, k, 1, :].rearrange("p (h l) -> p h l", h=H)
                        nc.vector.tensor_tensor(m, m, sx_bank[:, 0:P].unsqueeze(1).to_broadcast([P, H, P]), ALU.mult
                                                ).then_inc(S["m_done"], 1)
                    elif what == "conv":
                        c, m = k // 2, k % 2
                        n = (s + 1) * 2 * NCONV + k
                        dve.wait_ge(S["a0_done"], n + 1)
                        dve.wait_ge(S["proj_read"],
                                    (s + 1) * NJOB + next(j for j, job in enumerate(JOBS) if job[1:] == (c, m)) + 1)
                        y = xbc[:, 1 - par, c, half_of(m)]
                        for i in range(NTAP):
                            if i:
                                dve.wait_ge(S["taps"], n * NTAP + i)
                            nc.vector.scalar_tensor_tensor(y, raw[:, c % 2, m * MW + i:(m + 1) * MW + i],
                                                           cw[:, c, i:i + 1], y, ALU.mult, ALU.add).then_inc(S["taps"], 1)
                    elif what == "state":
                        dve.wait_ge(S["c_done"], T + 1)
                        if k == 0:
                            nc.vector.tensor_copy(St[:, 0, :], ys_bank[:, INTER:2 * INTER]).then_inc(S["s_ready"], 1)
                        elif k < TPS - 1:
                            dve.wait_ge(S["sd_done"], s * (TPS - 2) + k)
                            nc.vector.tensor_tensor(St[:, k % 2, :], ys_bank[:, INTER:2 * INTER], Sd[:, :], ALU.add
                                                    ).then_inc(S["s_ready"], 1)
                        wait(dve, "out_done", s * 2 - 1 + (k // MT))
                        for c in range(2):
                            last = nc.vector.scalar_tensor_tensor(
                                gbuf[:, c, tile_of(k)], xbc[:, par, c, tile_of(k)], dskip[:, c:c + 1],
                                ys_bank[:, c * P:(c + 1) * P], ALU.mult, ALU.add)
                        last.then_inc(S["y_done"], 1)
                    elif what == "gate":
                        if k == 0:
                            dve.wait_ge(S["proj_read"], (s + 1) * NJOB)
                        dve.wait_ge(S["y_done"], s * TPS + (k + 1) * MT)
                        nc.vector.tensor_tensor(gbuf[:, :, half_of(k)], gbuf[:, :, half_of(k)],
                                                zs[:, par, :, half_of(k)], ALU.mult).then_inc(S["g_done"], 1)
                    elif what == "chain":
                        g = (s - k) * 2 + k
                        norm1 = k == 1 or scan
                        sources = []
                        if norm1:
                            dve.wait_ge(S["out_done"], g + 1)
                            sources += [tail_bank[:, t * D:(t + 1) * D] for t in range(MT)]
                        if prev:
                            dve.wait_ge(S["x1_done"], g)
                            dve.wait_ge(S["newton"], g * NEWTON)
                            wait(dve, "xn3_done", g - 1)
                            sources += [on[:, 1 - k, t, :] for t in range(MT)]

                        def variance():
                            if prev:
                                last = nc.vector.tensor_scalar(veps[:, MT:2 * MT], mv[:, MT:2 * MT, 1], EPS, None, ALU.add)
                                last = nc.vector.tensor_scalar(nmean[:, MT:2 * MT], mv[:, MT:2 * MT, 0], -1.0, None, ALU.mult)
                            if norm1:
                                dve.wait_ge(S["ms_read"], g + 1)
                                last = nc.vector.tensor_tensor(veps[:, 0:MT], msb[:, :], mv[:, 0:MT, 1], ALU.add)
                            return last

                        norm_coefs(sources, "chained", g * TAIL_CHAIN, 0 if norm1 else MT, 2 * MT if prev else MT,
                                   variance, guess_only=True)
                    elif what == "apply":
                        g = (s - k) * 2 + k
                        dve.wait_ge(S["newton"], (g + 1) * NEWTON)
                        if not isinstance(s, int) or s - k > 0:
                            dve.wait_ge(x1_saved[k], (s - k) * 16)
                        for t in range(MT):
                            last = nc.vector.tensor_scalar(on[:, k, t, :], tail_bank[:, t * D:(t + 1) * D],
                                                           mv[:, t, 0:1], rst[:, t:t + 1],
                                                           ALU.subtract, ALU.mult)
                        last.then_inc(S["on_done"], 1)

            done = 0

            def rt(ins):
                nonlocal done
                done += 1
                ins.then_inc(S["route"], 1)
                dve.wait_ge(S["route"], done)

            def scores(tiles):
                rt(nc.vector.tensor_scalar(r1[1][:, tiles, :], r1[0][:, tiles, :], 1.0, None, ALU.add))
                rt(nc.vector.reciprocal(r1[2][:, tiles, :], r1[1][:, tiles, :]))
                rt(nc.vector.tensor_scalar(r1[3][:, tiles, :], r1[2][:, tiles, :], rscale[:, 0:1], None, ALU.mult))

            def first_scores():
                dve.wait_ge(S["route_exp"], 1)
                scores(slice(0, NT - PT))
                compare(0)

            def compare(i):
                wait(dve, "kept", i)
                s_t = r1[3][:, ds(i * PT, PT), :]
                nc.vector.tensor_tensor(beats, s_t.unsqueeze(2).to_broadcast([P, PT, NE, NE]),
                                        s_t.unsqueeze(3).to_broadcast([P, PT, NE, NE]), ALU.is_ge
                                        ).then_inc(S["compared"], 1)

            def gates(i, first=True, second=True):
                at = i * WEIGH + (0 if first else WEIGH - 5)

                def link(ins):
                    nonlocal at
                    at = at + 1
                    ins.then_inc(S["weighed"], 1)
                    dve.wait_ge(S["weighed"], at)

                if first:
                    dve.wait_ge(S["kept"], i + 1)
                    rank_and_weigh(i, link)
                if second:
                    split(i, link)

            def rank_and_weigh(i, link):
                link(nc.vector.reduce_sum(wins, before, mybir.AxisListType.X))
                link(nc.vector.reduce_sum(losses, before.rearrange("p t e f -> p t f e"), mybir.AxisListType.X))
                link(nc.vector.tensor_tensor(wins, wins, losses, ALU.subtract))
                link(nc.vector.tensor_tensor(rank, wins, rank0[:, :].unsqueeze(1).to_broadcast([P, PT, NE]), ALU.add))
                link(nc.vector.scalar_tensor_tensor(gate, rank, 1.5, r1[3][:, ds(i * PT, PT), :], ALU.is_lt, ALU.mult))
                link(nc.vector.reduce_sum(gtot[:, 0:PT], gate, mybir.AxisListType.X))
                link(nc.vector.reciprocal(gtot[:, PT:2 * PT], gtot[:, 0:PT]))
                link(nc.vector.tensor_tensor(gate, gate, gtot[:, PT:2 * PT].unsqueeze(2).to_broadcast([P, PT, NE]), ALU.mult))

            def split(i, link):
                wait(dve, "gtt_done", i * 2)
                copies = gst[:, :, :, 0:3 * SGRP].rearrange("p a t (k c) -> p (a t) k c", c=SGRP)
                for k in range(3):
                    part = copies[:, :, :, k * NE:(k + 1) * NE]
                    link(nc.vector.tensor_copy(part, gate.unsqueeze(2).to_broadcast([P, PT, 3, NE])))
                    if k < 2:
                        link(nc.vector.tensor_tensor(gate, gate, part[:, :, 0, :], ALU.subtract))

            run_bodies(dve, emit, first_scores)
            gates(0)
            dve.wait_ge(S["route_exp"], 2)
            scores(slice(NT - PT, NT))

            def gated(g, q, j):
                dve.wait_ge(S["gelu_done"], g * NF + j + 2)
                dve.wait_ge(S["gb_done"], g * NPAIR + j + 1)
                if j == 0:
                    wait(dve, "fout_done", g - 1)
                nc.vector.tensor_tensor(hg[q][j], hbuf[j % 2], exp_bank[:, j % 2, :], ALU.mult
                                        ).then_inc(S["hg_done"], 1)

            def last_norm(g, q, pause=None):
                dve.wait_ge(S["fout_done"], g + 1)
                norm_coefs([fout_bank[q][:, t * D:(t + 1) * D] for t in range(MT)], "fout_chain", g * LN_CHAIN, 0, MT,
                           pause=pause)
                dve.wait_ge(S["ob_done"], g + 1)
                for t in range(MT):
                    last = nc.vector.tensor_scalar(onf[q][:, t, :], fout_bank[q][:, t * D:(t + 1) * D],
                                                   mv[:, t, 0:1], rst[:, t:t + 1], ALU.subtract, ALU.mult)
                last.then_inc(S["onf_done"], 1)

            def ffn(i, more=True):
                for q in range(2):
                    g = i * 2 + q
                    gated(g, q, 0)
                    if q == 0 and more:
                        compare(i + 1)
                    if isinstance(i, int) and i == 0:
                        for j in range(1, NPAIR):
                            gated(g, q, j)
                    else:
                        def pause(j):
                            gated(g, q, j)
                            if q and j == 1 and more:
                                gates(i + 1, first=False)

                        last_norm(g - 2, q, pause)
                    if q == 0 and more:
                        gates(i + 1, second=False)
                    if isinstance(i, int) and i == 0 and q:
                        gates(1, first=False)

            ffn(0)
            with dve.Fori(1, NM // 2 - 1) as i:
                ffn(i)
            ffn(NM // 2 - 1, False)
            last_norm(NM - 2, 0)
            last_norm(NM - 1, 1)

        @block.tensor
        def _(pe):
            mm = nc.tensor.matmul
            pe.wait_ge(S["first_consts"], 32)

            def project_dt(g, q):
                pe.wait_ge(S["p0_evac"], 2 * g + 1)
                wait(pe, "p0_dtread", g)
                for t in range(MT):
                    last = mm(dt_bank[:, t * H:(t + 1) * H], stage[q][:, tile_of(t)], w_in[:, DT0:DT0 + H],
                              start=True, stop=True)
                last.then_inc(S["p0_dt"], 1)

            def first_norm(i):
                for k in range(UNITS):
                    g, q = i * UNITS + k, k % 2
                    pe.wait_ge(S["p0_norm"], g + 1)
                    wait(pe, "p0_evac", 2 * g - 2)
                    for t in range(MT):
                        last = nc.tensor.transpose(proj_bank[q][:, tile_of(t)], xn3[q][:, t, :], ident[:, :])
                    last.then_inc(S["p0_tr"], 1)
                    if k or not isinstance(i, int):
                        project_dt(g - 1, 1 - q)

            run_peeled(pe, NM // UNITS, first_norm)
            project_dt(NM - 1, 1)

            pe.wait_ge(S["consts"], 16 * len(loads))
            pe.wait_ge(S["started"], 1)
            pe.wait_ge(S["pre_dve"], 10)
            mm(sx_bank[:, 0:TN], tri[:, :], s1[8], start=True, stop=True)
            mm(ys_bank[:, 0:TN], ones[:, :], s1[8], start=True, stop=True).then_inc(S["pre_pe"], 1)
            pe.wait_ge(S["pre_dve"], 11)
            for a in range(2):
                last = nc.tensor.transpose(tail_bank[:, tile_of(a)], s1[10][:, tile_of(a)], ident[:, :])
            last.then_inc(S["pre_pe"], 1)
            pe.wait_ge(S["consts_cast"], 16)
            pe.wait_ge(S["pre_exp"], 5)
            pe.wait_ge(S["p0_dtread"], NM)

            def emit(s, par, scan, proj, prev):
                seen = 0
                for what, k in steps(scan, proj, prev):
                    T = s * TPS + k
                    B, C = xbc[:, par, NCONV - 2, :], xbc[:, par, NCONV - 1, :]
                    if what == "exp":
                        j = k % TPS
                        if j % (TPS // 2) == 0:
                            pe.wait_ge(cs_in[j // (TPS // 2)], (s + k // TPS + 1) * 64)
                        wait(pe, "exp_done", T)
                        mm(exp_bank[:, 0, :], csl[0:3, j, :], csr[0:3, j, :], start=True, stop=True)
                        mm(exp_bank[:, 1, :], csl[:, j, :], csr[:, j, :], start=True, stop=False)
                        mm(exp_bank[:, 1, :], identb[:, :], maskb[:, :, :].rearrange("p h l -> p (h l)"),
                           start=False, stop=True).then_inc(S["de_done"], 1)
                    elif what == "chunk":
                        if k == 0:
                            pe.wait_ge(S["xbc_ready"], (s + 1) * NCONV)
                        wait(pe, "m_done", T)
                        nc.tensor.transpose(sx_bank[:, P:2 * P], xbc[:, par, 0, tile_of(k)], ident[:, :])
                        nc.tensor.transpose(sx_bank[:, 2 * P:3 * P], xbc[:, par, 1, tile_of(k)], ident[:, :])
                        mm(sx_bank[:, 0:P], B[:, tile_of(k)], C[:, tile_of(k)], start=True, stop=True
                           ).then_inc(S["b_done"], 1)
                        seen = k + 1
                        wait(pe, "btok_done", T)
                        if k == 0:
                            wait(pe, "lg_read", s * 2 - 2)
                        if k == 3 and prev:
                            wait(pe, "ms_read", s * 2)
                        if k == 6 and prev:
                            wait(pe, "lg_read", s * 2 - 1)
                        if k == 7:
                            wait(pe, "ms_read", s * 2 + 1)
                        nc.tensor.transpose(bt_bank[:, 0:P], B[:, tile_of(k)], ident[:, :]).then_inc(S["bt_done"], 1)
                    elif what == "state":
                        wait(pe, "y_done", T)
                        pe.wait_ge(S["m_done"], T + 1)
                        if k < TPS - 1:
                            pe.wait_ge(S["btok_done"], T + 1)
                            pe.wait_ge(S["xw_done"], s * (TPS - 1) + k + 1)
                            mm(ys_bank[:, INTER:2 * INTER], Btok[:, k % 2, :], Xw[:, k % 2, :], start=True, stop=True)
                        if k:
                            pe.wait_ge(S["ch_done"], s * (TPS - 1) + k)
                            pe.wait_ge(S["s_ready"], s * (TPS - 1) + k)
                        for c in range(2):
                            for part in range(2 if k else 1):
                                for a in range(2):
                                    h = 2 * c + a
                                    lhs = (Xdt[:, k % 2, :] if part == 0 else St[:, (k - 1) % 2, :])[:, h * HD:(h + 1) * HD]
                                    last = mm(ys_bank[a * HD:(a + 1) * HD, c * P:(c + 1) * P], lhs,
                                              LE[:, k, 1 - part, h * P:(h + 1) * P], start=(part == 0),
                                              stop=(part == 1 or not k))
                        last.then_inc(S["c_done"], 1)
                    elif what == "job":
                        _, c, m = JOBS[k]
                        J = (s + 1) * NJOB + k
                        col = CONV0 + c * P if c < NCONV else (c - NCONV) * P
                        wait(pe, "proj_read", J - 1)
                        at = (s + 1) * SEQ + m * MW
                        mm(proj_bank[k % 2][:, :], w_in[:, col:col + P],
                           xT_all[:, ds(at, MW)] if not isinstance(at, int) else xT_all[:, at:at + MW],
                           start=True, stop=True).then_inc(S["proj_done"], 1)
                    elif what == "outproj":
                        g = (s - k) * 2 + k
                        pe.wait_ge(S["g_done"], g + 1)
                        wait(pe, "xft_done", 2 * g - 2)
                        for t in range(MT):
                            at = k * MW + t * P
                            for c in range(2):
                                last = mm(tail_bank[:, t * D:(t + 1) * D], gbuf[:, c, at:at + P], w_out[:, c, :],
                                          start=(c == 0), stop=(c == 1))
                        last.then_inc(S["out_done"], 1)
                    elif what == "ms":
                        g, pq = (s - k) * 2 + k, par if k == 0 else 1 - par
                        pe.wait_ge(S["sqs_done"], g + 1)
                        pe.wait_ge(S["btok_done"], s * TPS + seen)
                        if not scan:
                            pe.wait_ge(S["lg_read"], g - 1)
                        for t in range(MT):
                            at = k * MW + t * P
                            last = mm(bt_bank[:, P + t:P + t + 1], zs[:, pq, 0, at:at + P], ones[:, 0:1],
                                      start=True, stop=True)
                        last.then_inc(S["ms_done"], 1)
                    elif what == "back":
                        g = (s - 1) * 2 + k
                        pe.wait_ge(S["xn3_done"], g + 1)
                        if k == 0 or scan:
                            pe.wait_ge(S["on_done"], g + 2)
                        else:
                            pe.wait_ge(S["xft_done"], 2 * g)
                        for t in range(MT):
                            last = nc.tensor.transpose(tail_bank[:, tile_of(t)], xn3[0][:, t, :], ident[:, :])
                        last.then_inc(S["tr_done"], 1)
                    elif what == "logits":
                        g = (s - 1) * 2 + k
                        pe.wait_ge(S["xft_done"], 2 * g + 1)
                        pe.wait_ge(S["btok_done"], s * TPS + seen)
                        wait(pe, "ms_read", g + 2 if k == 0 or scan else g + 1)
                        for t in range(MT):
                            last = mm(bt_bank[:, 2 * P + t * NE:2 * P + (t + 1) * NE],
                                      stage[0][:, tile_of(t)], w_gate[:, :], start=True, stop=True)
                        last.then_inc(S["lg_done"], 1)

            run_bodies(pe, emit)

            def second(g, q, t):
                if t == 0:
                    pe.wait_ge(S["hg_done"], (g + 1) * NPAIR)
                    pe.wait_ge(S["gelu_done"], (g + 1) * NF)
                    wait(pe, "onf_done", g - 1)
                o = fout_bank[q][:, t * D:(t + 1) * D]
                for j in range(NPAIR):
                    mm(o, hg[q][j][:, tile_of(t)], w2[:, j, :], start=(j == 0), stop=False)
                mm(o, hg[q][NPAIR][0:HID, tile_of(t)], w2[0:HID, NPAIR, :], start=False, stop=False)
                last = mm(o, gt[q][:, tile_of(t)], brow[:, :], start=False, stop=True)
                if t == MT - 1:
                    last.then_inc(S["fout_done"], 1)

            pe.wait_ge(S["lg_read"], NM)

            def ffn(i):
                for q in range(2):
                    g = i * 2 + q
                    pe.wait_ge(S["weighed"], (i + 1) * WEIGH)
                    wait(pe, "gt_done", g)
                    for t in range(MT):
                        last = nc.tensor.transpose(gt_bank[:, tile_of(t)], gst[:, q, t, :], identb[:, :])
                    last.then_inc(S["gtt_done"], 1)
                    for n in range(NF):
                        j = (n - 1) % NF
                        wait(pe, "gelu_done", g * NF + n - 1)
                        at = g * MW
                        src = xT_all[:, ds(at, MW)] if not isinstance(at, int) else xT_all[:, at:at + MW]
                        if j < NPAIR:
                            mm(proj_bank[(q * NF + n) % 2][:, :], w1[:, j * P:(j + 1) * P], src, start=True, stop=True
                               ).then_inc(S["f1_done"], 1)
                            if j == 0:
                                pe.wait_ge(S["gt_done"], g + 1)
                            wait(pe, "hg_done", g * NPAIR + j - 1)
                            mm(exp_bank[:, j % 2, :], selb[:, j, :], gt[q], start=True, stop=True).then_inc(S["gb_done"], 1)
                            if not (isinstance(g, int) and g == 0):
                                second(g - 1, 1 - q, j)
                        else:
                            settle(pe)
                            mm(proj_bank[(q * NF + n) % 2][0:HID, :], w1[:, NPAIR * P:], src, start=True, stop=True
                               ).then_inc(S["f1_done"], 1)

            run_peeled(pe, NM // 2, ffn)
            for t in range(MT):
                second(NM - 1, 1, t)


def kernel(**inputs):
    import numpy as _np
    import concourse.bacc as _bacc
    from concourse import mybir as _mybir
    from concourse.bass_utils import run_bass_kernel_spmd as _run

    given = {n.replace("L0_attn_", "").replace("L0_ffn_", ""): _np.asarray(v) for n, v in inputs.items()}
    arrays = {n: given[n] for n in ("u", "in_proj_w", "conv_w", "dt_bias", "A_log", "D_param", "out_proj_w",
                                    "gate_W", "W1", "W2", "b2", "Ws1", "bs1", "Ws2", "bs2", "norm_w")}
    arrays["route_scale"] = given["route_scale"].reshape(1)
    arrays["norm_w_cols"] = given["norm_w"].reshape(-1, 128).T
    arrays["conv_b_cols"] = given["conv_b"].reshape(-1, 128).T
    arrays["b1_cols"] = given["b1"].reshape(-1, 128).T
    one = _np.ones((128, 128), _np.float32)
    arrays["c_ident"] = _np.eye(128, dtype=_np.float32)
    arrays["c_tri"] = _np.triu(one)
    arrays["c_mask"] = _np.tril(one, -1) * _np.float32(-1e30)
    heads = given["dt_bias"].shape[0]
    rows = _np.zeros((3 + 3 * heads, heads * 128 + 128), _np.float32)
    rows[0:3, heads * 128:] = 1.0
    for r in range(3 * heads):
        h = r % heads
        rows[3 + r, h * 128:(h + 1) * 128] = -1.0
    arrays["c_rows"] = rows
    experts, hid = given["W1"].shape[0], given["W1"].shape[2]
    sel = _np.zeros((128, experts * hid), _np.float32)
    for e in range(experts):
        for k in range(3):
            sel[experts * k + e, e * hid:(e + 1) * hid] = 1.0
    arrays["c_sel"] = sel
    arrays["c_rank"] = _np.tile(_np.arange(experts - 1, -1, -1, dtype=_np.float32), (128, 1))

    arrays["c_earlier"] = _np.tile(_np.tril(_np.ones((experts, experts), _np.float32), -1).reshape(1, -1), (128, 1))

    nc = _bacc.Bacc("TRN2", target_bir_lowering=False, num_devices=1)
    feeds, dram = {}, {}
    for name, a in arrays.items():
        a = _np.ascontiguousarray(a)
        feeds[f"in_{name}"] = a
        dram[name] = nc.dram_tensor(f"in_{name}", a.shape, _mybir.dt.from_np(a.dtype), kind="ExternalInput").ap()
    out = nc.dram_tensor("out_dram", given["u"].shape, _mybir.dt.float32, kind="ExternalOutput").ap()
    ssd_moe_block(nc, dram, out)
    r = _run(nc, [feeds], core_ids=[0])
    return r.results[0]["out_dram"]
```

```python
import concourse.bass as bass
from concourse import mybir
from contextlib import ExitStack


def ssd_moe_block(nc, dram, out):
    f32, bf16, i32 = mybir.dt.float32, mybir.dt.bfloat16, mybir.dt.int32
    ALU, ACT = mybir.AluOpType, mybir.ActivationFunctionType
    ds = bass.ds

    P = 128
    NSEQ, SEQ, D = dram["u"].shape
    INTER = dram["norm_w"].shape[0]
    H = dram["dt_bias"].shape[0]
    HD = INTER // H
    TPS = SEQ // P
    NT = NSEQ * TPS
    MT = 4
    MW = MT * P
    NM = NT // MT
    CONV0 = INTER
    NCONV = (dram["conv_w"].shape[0]) // P
    KC = dram["conv_w"].shape[1]
    DT0 = INTER + NCONV * P
    NE = dram["gate_W"].shape[1]
    HID = dram["W1"].shape[2]
    NPAIR = NE * HID // P
    EPS = 1e-5
    LN_CHAIN = 14
    TAIL_CHAIN = 6
    NEWTON = 12
    UNITS = 4
    SGRP = 32
    ONE = 3 * NE
    PT = 2 * MT
    WEIGH = 13

    u_v = dram["u"].rearrange("s (t p) d -> p (s t) d", p=P)
    out_v = out.rearrange("s (t p) d -> p (s t) d", p=P)

    with ExitStack() as ctx:
        def sb(name, shape, dt=f32):
            return ctx.enter_context(nc.sbuf_tensor(name, shape, dt))

        def sem(name):
            return ctx.enter_context(nc.semaphore(name))

        x_all = sb("x_all", [P, NT, D])
        xT_all = sb("xT_all", [P, NT * P])
        LE = sb("LE", [P, TPS, 2, H * P])
        xbc = sb("xbc", [P, 2, NCONV, SEQ])
        zs = sb("zs", [P, 2, 2, SEQ])
        gbuf = sb("gbuf", [P, 2, SEQ])
        raw = sb("raw", [P, 2, KC - 1 + SEQ])
        Xdt = sb("Xdt", [P, 2, INTER])
        Xw = sb("Xw", [P, 2, INTER])
        St = sb("St", [P, 2, INTER])
        Sd = sb("Sd", [P, INTER])
        Btok = sb("Btok", [P, 2, P])
        on = sb("on", [P, 2, MT, D])
        xn_tile = sb("xn_tile", [P, MT, D])
        stage = sb("stage", [P, MW])
        w_in = sb("w_in", [P, DT0 + H])
        w_dt = sb("w_dt", [P, SGRP])
        w_gate = sb("w_gate", [P, NE])
        w_out = sb("w_out", [P, 2, D])
        nw = sb("nw", [P, 2])
        cw = sb("cw", [P, NCONV, KC])
        cb = sb("cb", [P, NCONV])
        dskip = sb("dskip", [P, 2])
        ident = sb("ident", [P, P])
        identb = sb("identb", [P, P], bf16)
        tri = sb("tri", [P, P])
        ones = sb("ones", [P, P])
        maskb = sb("maskb", [P, H, P], bf16)
        csl = sb("csl", [3 + 3 * H, TPS, P], bf16)
        csr = sb("csr", [3 + 3 * H, TPS, H * P], bf16)
        bias4 = sb("bias4", [P, H])
        alog4 = sb("alog4", [P, H])
        dt_all = sb("dt_all", [P, NT, H])
        dec_all = sb("dec_all", [P, NT, H])
        tot_all = sb("tot_all", [P, NT, H])
        logits = sb("logits", [P, NT, NE])
        w1 = sb("w1", [P, NPAIR * P + HID])
        b1 = sb("b1", [P, NPAIR + 1])
        w2 = sb("w2", [P, NPAIR + 1, D])
        selb = sb("selb", [P, NPAIR, P], bf16)
        brow = sb("brow", [P, P], bf16)
        gst = sb("gst", [P, 2, MT, P], bf16)
        rank0 = sb("rank0", [P, NE])
        earlier = sb("earlier", [P, NE * NE])
        rscale = sb("rscale", [P, 1])
        NC = UNITS * MT
        st6 = sb("st6", [P, NC, 6])
        mv = sb("mv", [P, NC, 2])
        nt_a = sb("nt_a", [P, NC])
        nt_b = sb("nt_b", [P, NC])
        nt_y = sb("nt_y", [P, NC])
        veps = sb("veps", [P, NC])
        rst = sb("rst", [P, NC])
        nmean = sb("nmean", [P, NC])
        shift = sb("shift", [P, NC])
        PC = 2 * MT
        mhalf = sb("mhalf", [P, PC])
        pn_a, pn_b, pn_c, pn_y = [sb(f"pn_{n}", [P, PC]) for n in "abcy"]
        three_halves = sb("three_halves", [P, PC])
        gtot = sb("gtot", [P, 2 * PT])
        msb = sb("msb", [P, MT])

        TN = NT * H
        le_flat = LE[:, :, :, :].rearrange("p t a n -> p (t a n)")
        s1 = [le_flat[:, k * TN:(k + 1) * TN] for k in range(12)]
        csp = le_flat[:, 12 * TN:14 * TN].bitcast(bf16)[:, 0:3 * TN].rearrange("p (k n) -> p k n", k=3)
        mask_f = le_flat[:, 16 * TN:16 * TN + P]
        rows_f = le_flat[:, 18 * TN:18 * TN + H * P + P]
        sel_f = le_flat[:, 21 * TN:21 * TN + NPAIR * P]
        brow_f = le_flat[:, 23 * TN:23 * TN + P]
        brow_p = le_flat[:, 14 * TN:15 * TN].bitcast(bf16)[:, 0:3 * P].rearrange("p (k n) -> p k n", k=3)
        brow_r = le_flat[:, 24 * TN:24 * TN + 2 * P].rearrange("p (k n) -> p k n", k=2)
        at_xn = 25 * TN + P
        xn3 = [xn_tile] + [le_flat[:, at_xn + k * MW:at_xn + (k + 1) * MW].rearrange("p (t d) -> p t d", t=MT)
                           for k in range(3)]
        NF = NPAIR + 1
        xbc_flat = xbc[:, :, :, :].rearrange("p a c n -> p (a c n)")
        hbuf = [xbc_flat[:, (3 + k) * MW:(4 + k) * MW] for k in range(2)]
        hg = [[xbc_flat[:, (5 + q * NF + j) * MW:(6 + q * NF + j) * MW] for j in range(NF)] for q in range(2)]
        gt = [le_flat[:, q * (MW // 2):(q + 1) * (MW // 2)].bitcast(bf16) for q in range(2)]
        onf = [le_flat[:, (1 + q) * MW:(2 + q) * MW].rearrange("p (t d) -> p t d", t=MT) for q in range(2)]
        raw_flat = raw[:, :, :].rearrange("p a n -> p (a n)")
        r1 = [raw_flat[:, k * NT * NE:(k + 1) * NT * NE].rearrange("p (t e) -> p t e", e=NE) for k in range(4)]
        beats, before = [xbc_flat[:, k * PT * NE * NE:(k + 1) * PT * NE * NE].rearrange(
            "p (t e f) -> p t e f", e=NE, f=NE) for k in range(2)]
        at_rt = 2 * PT * NE * NE
        rank, wins, losses, gate = [xbc_flat[:, at_rt + k * PT * NE:at_rt + (k + 1) * PT * NE].rearrange(
            "p (t e) -> p t e", e=NE) for k in range(4)]
        outb = [le_flat[:, (8 + q) * MW:(9 + q) * MW].rearrange("p (t d) -> p t d", t=MT) for q in range(2)]

        proj_bank = [ctx.enter_context(nc.psum_tensor(f"proj_bank{k}", [P, MW], f32)) for k in range(2)]
        exp_bank = ctx.enter_context(nc.psum_tensor("exp_bank", [P, 2, H * P], f32))
        sx_bank = ctx.enter_context(nc.psum_tensor("sx_bank", [P, 512], f32))
        ys_bank = ctx.enter_context(nc.psum_tensor("ys_bank", [P, 512], f32))
        bt_bank = ctx.enter_context(nc.psum_tensor("bt_bank", [P, 512], f32))
        tail_bank = ctx.enter_context(nc.psum_tensor("tail_bank", [P, 512], f32))
        dt_bank, dt_back = exp_bank[:, 0, :], exp_bank[:, 1, :]
        fout_bank = [sx_bank, ys_bank]
        gt_bank = bt_bank[:, 0:MW // 2].bitcast(bf16)

        cs_rows = nc.dram_tensor("cs_rows", (3, NT * H * P), bf16, kind="Internal").ap()

        names = """settled started first_consts consts consts_cast zeroed rows_out
            p0_chain p0_shift p0_norm p0_norm_act p0_tr p0_evac p0_dt p0_dtread pre_exp pre_dve pre_pe
            proj_done proj_read a0_done taps xbc_ready de_done exp_done b_done bt_done btok_done
            xdt_done m_done ch_done xw_done sd_done c_done s_ready y_done
            g_done sq_done sqs_done ms_done ms_read out_done chained newton on_done x1_done xn3_done
            tr_done xft_done lg_done lg_read route route_exp compared kept weighed gtt_done gt_done f1_done
            gelu_done gb_done hg_done fout_done fout_chain fout_newton onf_done ob_done""".split()
        S = {n: sem(n) for n in names}
        cs_in = [sem(f"cs_in{k}") for k in range(2)]
        u_in = [sem(f"u_in{k}") for k in range(UNITS)]
        x1_saved = [sem(f"x1_saved{k}") for k in range(2)]
        stored = [sem(f"stored{k}") for k in range(2)]
        block = ctx.enter_context(nc.Block())

        def wait(eng, name, value):
            if isinstance(value, int) and value <= 0:
                return
            eng.wait_ge(S[name], value)

        STEPS = [
            ('chunk', 0), ('exp', 4), ('square', 1), ('sum', 1), ('job', (0, 0)), ('job', (0, 1)),
            ('chunk', 1), ('exp', 5), ('outproj', 1), ('job', (1, 0)), ('conv', 0), ('exp', 6), ('state', 0),
            ('chunk', 2), ('exp', 7), ('silu', 0), ('ms', 1), ('job', (1, 1)), ('job', (4, 0)), ('chain', 1),
            ('state', 1),
            ('chunk', 3), ('job', (2, 0)), ('newton', 1), ('conv', 1), ('state', 2),
            ('chunk', 4), ('apply', 1), ('job', (2, 1)), ('silu', 1), ('job', (5, 0)), ('x1', 1), ('exp', 8),
            ('state', 3), ('gate', 0), ('back', 0),
            ('chunk', 5), ('job', (3, 0)), ('exp', 9), ('logits', 0), ('outproj', 0), ('square', 0),
            ('conv', 2), ('sum', 0), ('exp', 10), ('state', 4),
            ('chunk', 6), ('exp', 11), ('silu', 2), ('ms', 0), ('job', (3, 1)), ('job', (4, 1)),
            ('chain', 0), ('newton', 0), ('state', 5),
            ('chunk', 7), ('job', (5, 1)), ('conv', 3), ('apply', 0), ('state', 6), ('silu', 3), ('x1', 0),
            ('back', 1), ('state', 7), ('logits', 1), ('gate', 1),
        ]
        FIRST = [
            ('job', (0, 0)), ('sizes', 0), ('sizes', 1), ('job', (0, 1)), ('job', (1, 0)), ('job', (1, 1)),
            ('sizes', 2), ('sizes', 3), ('sizes', 4), ('conv', 0), ('conv', 1), ('job', (4, 0)),
            ('job', (2, 0)), ('silu', 0), ('job', (2, 1)), ('conv', 2), ('silu', 1), ('job', (5, 0)),
            ('job', (3, 0)), ('job', (3, 1)), ('conv', 3), ('job', (4, 1)), ('job', (5, 1)), ('silu', 2),
            ('exp', 8), ('silu', 3), ('exp', 9), ('exp', 10), ('exp', 11),
        ]

        JOBS = [k for what, k in STEPS if what == "job"]
        NJOB = len(JOBS)

        def settle(eng):
            eng.sem_inc(S["settled"], 1)


        WHEN = {
            "chunk": "s", "state": "s", "gate": "s", "silu": "p", "conv": "p", "sizes": "p", "job": "p",
            "back": "v", "logits": "v",
            "outproj": "sv", "square": "sv", "sum": "sv", "ms": "sv", "apply": "sv",
            "x1": "sv", "chain": "av", "newton": "av",
            "exp": "sp"}

        STAGE = {("apply", 1): 2, ("x1", 1): 2, ("back", 0): 2, ("logits", 0): 2, ("chain", 0): 3, ("newton", 0): 3,
                 ("back", 1): 4, ("logits", 1): 4}

        def steps(scan, proj, prev):
            for what, k in STEPS if scan or prev else FIRST:
                if not scan and prev and prev != STAGE.get((what, k), 1):
                    continue
                when = WHEN[what]
                if when == "sp":
                    there = scan if k < TPS else proj
                elif len(when) == 2:
                    there = prev if k == 1 else scan or (when == "av" and prev)
                else:
                    there = {"s": scan, "p": proj, "v": prev}[when]
                if there:
                    yield what, JOBS.index(k) if what == "job" else k

        def chunk_after(step):
            return next((k for what, k in STEPS[STEPS.index(step):] if what == "chunk"), 0)

        def run_bodies(eng, emit, before_scan=None, before_tail=None):
            emit(-1, 1, False, True, False)
            emit(0, 0, True, True, False)
            with eng.Fori(0, (NSEQ - 2) // 2) as i:
                emit(i * 2 + 1, 1, True, True, True)
                emit(i * 2 + 2, 0, True, True, True)
            if before_scan:
                before_scan()
            emit(NSEQ - 1, 1, True, False, True)
            if before_tail:
                before_tail()
            emit(NSEQ, 0, False, False, 1)

        def run_peeled(eng, count, emit):
            emit(0)
            with eng.Fori(1, count) as i:
                emit(i)

        NTAP = KC - 1

        def half_of(m):
            return slice(m * MW, (m + 1) * MW)

        def tile_of(t):
            return slice(t * P, (t + 1) * P)

        loads = []

        @block.sync
        def _(sp):
            def units(i):
                for k in range(UNITS):
                    g = i * UNITS + k
                    if not isinstance(i, int):
                        sp.wait_ge(u_in[k], i * 16)
                        settle(sp)
                    sp.dma_start(x_all[:, ds(g * MT, MT), :], u_v[:, ds(g * MT, MT), :]).then_inc(u_in[k], 16)

            run_peeled(sp, NM // UNITS, units)

            def load(dst, src):
                loads.append(1)
                sp.dma_start(dst, src).then_inc(S["consts"], 16)

            load(tri[:, :], dram["c_tri"])
            load(bias4[:, :], dram["dt_bias"].unsqueeze(0).to_broadcast([P, H]))
            load(alog4[:, :], dram["A_log"].unsqueeze(0).to_broadcast([P, H]))
            load(mask_f, dram["c_mask"])
            load(rows_f[0:3 + 3 * H, :], dram["c_rows"])
            load(w_out[:, :, :], dram["out_proj_w"].rearrange("(c p) n -> p c n", p=P))
            load(w_gate[:, :], dram["gate_W"])
            load(nw[:, :], dram["norm_w_cols"])
            load(cw[:, :, :], dram["conv_w"].rearrange("(c p) k -> p c k", p=P))
            load(cb[:, :], dram["conv_b_cols"])
            load(sel_f, dram["c_sel"])
            load(rank0[:, :], dram["c_rank"])
            load(earlier[:, :], dram["c_earlier"])
            load(rscale[:, :], dram["route_scale"].unsqueeze(0).to_broadcast([P, 1]))
            load(w1[:, 0:NPAIR * P].rearrange("p (e h) -> p e h", e=NE), dram["W1"].rearrange("e d h -> d e h"))
            load(w1[:, NPAIR * P:], dram["Ws1"])
            load(b1[:, 0:NPAIR], dram["b1_cols"])
            load(b1[0:HID, NPAIR:NF], dram["bs1"].unsqueeze(1))
            load(w2[:, 0:NPAIR, :], dram["W2"].rearrange("(j a) h d -> (a h) j d", j=NPAIR))
            load(w2[0:HID, NPAIR, :], dram["Ws2"])
            for h in range(H):
                load(dskip[(h % 2) * HD:(h % 2 + 1) * HD, h // 2:h // 2 + 1],
                     dram["D_param"][h:h + 1].unsqueeze(0).to_broadcast([HD, 1]))
            sp.wait_ge(S["zeroed"], 1)
            for k in range(3):
                for n in range(3):
                    load(brow_f[SGRP * k + NE * n:SGRP * k + NE * n + NE, :], dram["b2"])
                load(brow_f[SGRP * k + ONE:SGRP * k + ONE + 1, :], dram["bs2"].unsqueeze(0))

            sp.wait_ge(S["pre_dve"], 17)
            for k in range(3):
                sp.dma_start(cs_rows[k, :].rearrange("(a r l) -> r a l", a=2, l=P),
                             csp[:, k, :].rearrange("p (a l) -> p a l", a=2)).then_inc(S["rows_out"], 16)
            sp.wait_ge(S["rows_out"], 48)

            def load_rows(s, half):
                HT = TPS // 2
                at = s * (TPS * H * P) + half * (HT * H * P)
                to = slice(half * HT, (half + 1) * HT)
                sp.dma_start(csr[0:3, to, :], cs_rows[:, ds(at, HT * H * P)].rearrange("k (t n) -> k t n", t=HT)
                             ).then_inc(cs_in[half], 16)
                for k in range(3):
                    src = cs_rows[k, ds(at, HT * H * P)].rearrange("(t h l) -> h t l", t=HT, h=H)
                    sp.dma_start(csl[3 + H * k:3 + H * k + H, to, :], src).then_inc(cs_in[half], 16)

            sp.wait_ge(S["consts_cast"], 4)
            load_rows(0, 0)
            load_rows(0, 1)

            def emit(s, par, scan, proj, prev):
                for what, k in steps(scan, proj, prev):
                    if what == "x1":
                        g = (s - k) * 2 + k
                        sp.wait_ge(S["x1_done"], g + 1)
                        settle(sp)
                        sp.dma_start(x_all[:, ds(g * MT, MT), :] if not isinstance(g, int)
                                     else x_all[:, g * MT:(g + 1) * MT, :], on[:, k, :, :]).then_inc(x1_saved[k], 16)
                    elif what == "chunk" and proj and k in (0, 3):
                        half = min(k, 1)
                        sp.wait_ge(S["de_done"], s * TPS + (half + 1) * TPS // 2)
                        sp.wait_ge(cs_in[half], (s + 1) * 64)
                        settle(sp)
                        load_rows(s + 1, half)

            run_bodies(sp, emit)
            emit(NSEQ, 0, False, False, 2)

            def store(i):
                for q in range(2):
                    g = i * 2 + q
                    sp.wait_ge(S["ob_done"], g + 3)
                    settle(sp)
                    if not isinstance(i, int):
                        sp.wait_ge(stored[q], i * 16)
                        settle(sp)
                    sp.dma_start(out_v[:, ds(g * MT, MT), :], outb[q]).then_inc(stored[q], 16)

            run_peeled(sp, NM // 2, store)
            for q in range(2):
                sp.wait_ge(stored[q], NM // 2 * 16)
            for k in range(2):
                sp.wait_ge(x1_saved[k], NSEQ * 16)

        @block.scalar
        def _(act):
            act.dma_start(ident[:, :], dram["c_ident"]).then_inc(S["first_consts"], 16)
            act.dma_start(w_in[:, :], dram["in_proj_w"]).then_inc(S["first_consts"], 16)
            act.wait_ge(S["started"], 1)
            act.dma_start(w_dt[:, 0:H], dram["in_proj_w"][:, DT0:DT0 + H]).then_inc(S["first_consts"], 16)

            def copy_dt(i):
                act.wait_ge(S["p0_dt"], i * 2 + 1)
                nc.scalar.activation(stage[:, :], dt_bank, ACT.Copy).then_inc(S["p0_dtread"], 1)

            def read_dt(i):
                act.wait_ge(S["p0_dt"], i * 2 + 2)
                nc.scalar.activation(
                    dt_all[:, ds(i * NC, NC), :].rearrange("p (k t) h -> p t k h", k=UNITS),
                    dt_back.rearrange("p (t k c) -> p t k c", t=MT, c=SGRP)[:, :, :, 0:H], ACT.Copy
                    ).then_inc(S["p0_dtread"], 1)

            def first_norm(i):
                act.wait_ge(S["p0_shift"], i + 1)
                for k in (2, 3):
                    wait(act, "p0_tr", (i - 1) * UNITS + k + 1)
                    for t in range(MT):
                        n = k * MT + t
                        last = nc.scalar.activation(xn3[k][:, t, :],
                                                    x_all[:, ds(i * NC + n, 1), :].rearrange("p t d -> p (t d)"),
                                                    ACT.Identity, scale=rst[:, n:n + 1], bias=shift[:, n:n + 1])
                    last.then_inc(S["p0_norm_act"], 1)
                for k in range(UNITS):
                    g, q = i * UNITS + k, k % 2
                    act.wait_ge(S["p0_tr"], g + 1)
                    nc.scalar.activation(xT_all[:, ds(g * MW, MW)], proj_bank[q][:, :], ACT.Copy
                                         ).then_inc(S["p0_evac"], 1)
                    if k >= 2 and not isinstance(i, int):
                        (copy_dt, read_dt)[k - 2](i - 1)

            run_peeled(act, NM // UNITS, first_norm)
            copy_dt(NM // UNITS - 1)
            read_dt(NM // UNITS - 1)

            act.wait_ge(S["consts"], 16 * len(loads))

            def sizes(k):
                if k == 0:
                    act.wait_ge(S["pre_dve"], 2)
                    nc.scalar.activation(s1[2], s1[1], ACT.Exp, scale=-1.0).then_inc(S["pre_exp"], 1)
                    nc.scalar.activation(s1[11][:, 0:H], alog4[:, :], ACT.Exp).then_inc(S["pre_exp"], 1)
                if k == 1:
                    act.wait_ge(S["pre_dve"], 3)
                    nc.scalar.activation(s1[4], s1[3], ACT.Ln).then_inc(S["pre_exp"], 1)
                if k == 3:
                    act.wait_ge(S["pre_dve"], 12)
                    nc.scalar.activation(dec_all[:, :, :].rearrange("p t h -> p (t h)"), s1[9], ACT.Exp
                                         ).then_inc(S["pre_exp"], 1)
                    nc.scalar.activation(tot_all[:, :, :].rearrange("p t h -> p (t h)"), ys_bank[:, 0:TN], ACT.Exp
                                         ).then_inc(S["pre_exp"], 1)

            def emit(s, par, scan, proj, prev):
                for what, k in steps(scan, proj, prev):
                    T = s * TPS + k
                    if what == "sizes":
                        sizes(k)
                    elif what == "exp":
                        act.wait_ge(S["de_done"], T + 1)
                        wait(act, "c_done", (s - 1) * TPS + k + 1)
                        nc.scalar.activation(LE[:, k % TPS, :, :], exp_bank[:, :, :], ACT.Exp).then_inc(S["exp_done"], 1)
                    elif what == "chunk":
                        act.wait_ge(S["bt_done"], T + 1)
                        wait(act, "c_done", T - 1)
                        nc.scalar.activation(Btok[:, k % 2, :], bt_bank[:, 0:P], ACT.Copy).then_inc(S["btok_done"], 1)
                    elif what == "job":
                        c, m = JOBS[k]
                        act.wait_ge(S["proj_done"], (s + 1) * NJOB + k + 1)
                        if c < NCONV:
                            wait(act, "y_done", s * TPS)
                            nc.scalar.activation(xbc[:, 1 - par, c, half_of(m)], proj_bank[k % 2][:, :], ACT.Identity,
                                                 scale=cw[:, c, NTAP:KC], bias=cb[:, c:c + 1]).then_inc(S["a0_done"], 1)
                            wait(act, "taps", ((s + 1) * NCONV + c - 1) * NTAP)
                            nc.scalar.activation(raw[:, c % 2, NTAP + m * MW:NTAP + (m + 1) * MW],
                                                 proj_bank[k % 2][:, :], ACT.Copy).then_inc(S["proj_read"], 1)
                        else:
                            wait(act, "ms_done", s * 2 - 1 + m)
                            nc.scalar.activation(zs[:, 1 - par, c - NCONV, half_of(m)],
                                                 proj_bank[k % 2][:, :], ACT.Silu).then_inc(S["proj_read"], 1)
                    elif what == "silu":
                        act.wait_ge(S["taps"], ((s + 1) * NCONV + k + 1) * NTAP)
                        nc.scalar.activation(xbc[:, 1 - par, k, :], xbc[:, 1 - par, k, :], ACT.Silu
                                             ).then_inc(S["xbc_ready"], 1)
                    elif what == "square":
                        g, pq = (s - k) * 2 + k, par if k == 0 else 1 - par
                        act.wait_ge(S["g_done"], g + 1)
                        nc.scalar.activation(zs[:, pq, :, half_of(k)], gbuf[:, :, half_of(k)], ACT.Square
                                             ).then_inc(S["sq_done"], 1)
                    elif what == "ms":
                        g = (s - k) * 2 + k
                        act.wait_ge(S["ms_done"], g + 1)
                        wait(act, "on_done", g)
                        nc.scalar.activation(msb[:, :], bt_bank[:, P:P + MT], ACT.Copy, scale=EPS / INTER,
                                             bias=EPS * EPS).then_inc(S["ms_read"], 1)
                    elif what == "back":
                        g = (s - 1) * 2 + k
                        act.wait_ge(S["tr_done"], g + 1)
                        wait(act, "lg_done", g)
                        nc.scalar.activation(stage[:, :], tail_bank[:, :], ACT.Copy).then_inc(S["xft_done"], 1)
                        nc.scalar.activation(xT_all[:, ds(g * MW, MW)] if not isinstance(g, int)
                                             else xT_all[:, g * MW:(g + 1) * MW], tail_bank[:, :], ACT.Copy
                                             ).then_inc(S["xft_done"], 1)
                    elif what == "logits":
                        g = (s - 1) * 2 + k
                        act.wait_ge(S["lg_done"], g + 1)
                        nc.scalar.activation(
                            (logits[:, ds(g * MT, MT), :] if not isinstance(g, int)
                             else logits[:, g * MT:(g + 1) * MT, :]).rearrange("p t e -> p (t e)"),
                            bt_bank[:, 2 * P:2 * P + MT * NE], ACT.Copy).then_inc(S["lg_read"], 1)

            def route_exp(tiles):
                nc.scalar.activation(r1[0][:, tiles, :], logits[:, tiles, :], ACT.Exp, scale=-1.0
                                     ).then_inc(S["route_exp"], 1)

            def first_scores():
                act.wait_ge(S["taps"], NSEQ * NCONV * NTAP)
                act.wait_ge(S["lg_read"], NM - 4)
                route_exp(slice(0, NT - 2 * PT))

            run_bodies(act, emit, first_scores)
            act.wait_ge(S["y_done"], NT)

            def last_norm(g, q):
                act.wait_ge(S["fout_newton"], (g + 3) * (NEWTON + 1))
                act.wait_ge(S["ob_done"], g + 1)
                for t in range(MT):
                    n = q * MT + t
                    last = nc.scalar.activation(onf[q][:, t, :], fout_bank[q][:, t * D:(t + 1) * D], ACT.Identity,
                                                scale=rst[:, n:n + 1], bias=shift[:, n:n + 1])
                last.then_inc(S["onf_done"], 1)

            def ffn(i):
                for q in range(2):
                    g = i * 2 + q
                    act.wait_ge(S["gtt_done"], g + 1)
                    wait(act, "fout_done", g - 1)
                    nc.scalar.activation(gt[q], gt_bank, ACT.Copy).then_inc(S["gt_done"], 1)
                    for n in range(NF):
                        j = (n - 1) % NF
                        if isinstance(i, int) and q and n == NF - 1:
                            emit(NSEQ, 0, False, False, 4)
                            act.wait_ge(S["lg_read"], NM)
                            route_exp(slice(NT - 2 * PT, NT))
                        act.wait_ge(S["f1_done"], g * NF + n + 1)
                        src = proj_bank[(q * NF + n) % 2]
                        if j < NPAIR:
                            wait(act, "hg_done", g * NPAIR + j - 1)
                            nc.scalar.activation(hbuf[j % 2], src[:, :], ACT.Gelu, bias=b1[:, j:j + 1]
                                                 ).then_inc(S["gelu_done"], 1)
                        else:
                            nc.scalar.activation(hg[q][j][0:HID, :], src[0:HID, :], ACT.Gelu, bias=b1[0:HID, j:j + 1]
                                                 ).then_inc(S["gelu_done"], 1)
                    if not isinstance(i, int):
                        last_norm(g - 2, q)
                    elif q == 0:
                        emit(NSEQ, 0, False, False, 2)

            ffn(0)
            with act.Fori(1, NM // 2) as i:
                ffn(i)
            last_norm(NM - 2, 0)
            last_norm(NM - 1, 1)

        @block.gpsimd
        def _(pool):
            nc.gpsimd.memset(w_dt[:, :], 0.0)
            nc.gpsimd.memset(ones[:, :], 1.0).then_inc(S["started"], 1)
            nc.gpsimd.memset(brow_f, 0.0).then_inc(S["zeroed"], 1)
            nc.gpsimd.memset(raw[:, :, 0:NTAP], 0.0).then_inc(S["zeroed"], 1)
            nc.gpsimd.memset(three_halves[:, :], 1.5)
            nc.gpsimd.memset(gst[:, :, :, :], 0.0).then_inc(S["zeroed"], 1)
            pool.wait_ge(S["zeroed"], 3)
            nc.gpsimd.memset(gst[:, :, :, 0:3 * SGRP].rearrange("p a t (k c) -> p a t k c", c=SGRP)[:, :, :, :, ONE:ONE + 1],
                             1.0).then_inc(S["zeroed"], 1)

            pool.wait_ge(S["first_consts"], 48)
            pool.wait_ge(S["consts"], 16 * len(loads))
            nc.gpsimd.tensor_copy(identb[:, :], ident[:, :]).then_inc(S["consts_cast"], 1)
            nc.gpsimd.tensor_copy(maskb[:, :, :], mask_f.unsqueeze(1).to_broadcast([P, H, P])).then_inc(S["consts_cast"], 1)
            R = 3 + 3 * H
            nc.gpsimd.tensor_copy(csr[0:R, :, :], rows_f[0:R, 0:H * P].unsqueeze(1).to_broadcast([R, TPS, H * P])
                                  ).then_inc(S["consts_cast"], 1)
            nc.gpsimd.tensor_copy(csl[0:R, :, :], rows_f[0:R, H * P:H * P + P].unsqueeze(1).to_broadcast([R, TPS, P])
                                  ).then_inc(S["consts_cast"], 1)
            for c in range(2):
                nc.gpsimd.tensor_scalar(w_out[:, c, :], w_out[:, c, :], nw[:, c:c + 1], None, ALU.mult
                                        ).then_inc(S["consts_cast"], 1)
            nc.gpsimd.tensor_copy(selb[:, :, :].rearrange("p j m -> p (j m)"), sel_f).then_inc(S["consts_cast"], 1)
            nc.gpsimd.tensor_copy(brow_p[:, 0, :], brow_f).then_inc(S["consts_cast"], 1)
            pool.wait_ge(S["consts_cast"], 8)
            nc.gpsimd.tensor_tensor(brow_r[:, 0, :], brow_f, brow_p[:, 0, :], ALU.subtract).then_inc(S["consts_cast"], 1)
            pool.wait_ge(S["consts_cast"], 9)
            nc.gpsimd.tensor_copy(brow_p[:, 1, :], brow_r[:, 0, :]).then_inc(S["consts_cast"], 1)
            pool.wait_ge(S["consts_cast"], 10)
            nc.gpsimd.tensor_tensor(brow_r[:, 1, :], brow_r[:, 0, :], brow_p[:, 1, :], ALU.subtract
                                    ).then_inc(S["consts_cast"], 1)
            pool.wait_ge(S["consts_cast"], 11)
            nc.gpsimd.tensor_copy(brow_p[:, 2, :], brow_r[:, 1, :]).then_inc(S["consts_cast"], 1)
            pool.wait_ge(S["consts_cast"], 12)
            for k in range(4):
                rows = slice(SGRP * k, SGRP * (k + 1))
                nc.gpsimd.tensor_copy(brow[rows, :], brow_p[rows, k % 3, :]).then_inc(S["consts_cast"], 1)

            def decay_state(s, k):
                T = s * TPS + k
                pool.wait_ge(S["s_ready"], s * (TPS - 1) + k)
                tot = tot_all[:, T, :] if isinstance(T, int) else tot_all[:, ds(T, 1), :].rearrange("p t h -> p (t h)")
                nc.gpsimd.tensor_tensor(Sd[:, :].rearrange("p (h d) -> p h d", h=H),
                                        St[:, (k - 1) % 2, :].rearrange("p (h d) -> p h d", h=H),
                                        tot.unsqueeze(2).to_broadcast([P, H, HD]), ALU.mult).then_inc(S["sd_done"], 1)

            def emit(s, par, scan, proj, prev):
                for what, k in steps(scan, proj, prev):
                    T = s * TPS + k
                    if what == "chunk":
                        if 2 <= k < TPS:
                            decay_state(s, k - 1)
                        if k >= 1:
                            pool.wait_ge(S["exp_done"], T + 1)
                            pool.wait_ge(S["xbc_ready"], (s + 1) * NCONV)
                            e = LE[:, k, 0, :].rearrange("p (h l) -> p h l", h=H)
                            nc.gpsimd.tensor_tensor(e, e, xbc[:, par, NCONV - 1, tile_of(k)].unsqueeze(1)
                                                    .to_broadcast([P, H, P]), ALU.mult).then_inc(S["ch_done"], 1)
                        if k < TPS - 1:
                            pool.wait_ge(S["xdt_done"], T + 1)
                            wait(pool, "c_done", T - 1)
                            dec = dec_all[:, T, :] if isinstance(T, int) else dec_all[:, ds(T, 1), :].rearrange(
                                "p t h -> p (t h)")
                            nc.gpsimd.tensor_tensor(Xw[:, k % 2, :].rearrange("p (h d) -> p h d", h=H),
                                                    Xdt[:, k % 2, :].rearrange("p (h d) -> p h d", h=H),
                                                    dec.unsqueeze(2).to_broadcast([P, H, HD]), ALU.mult
                                                    ).then_inc(S["xw_done"], 1)
                    elif what == "sum":
                        g, pq = (s - k) * 2 + k, par if k == 0 else 1 - par
                        pool.wait_ge(S["sq_done"], g + 1)
                        nc.gpsimd.tensor_tensor(zs[:, pq, 0, half_of(k)], zs[:, pq, 0, half_of(k)],
                                                zs[:, pq, 1, half_of(k)], ALU.add).then_inc(S["sqs_done"], 1)
                    elif what == "newton":
                        g = (s - k) * 2 + k
                        pool.wait_ge(S["chained"], (g + 1) * TAIL_CHAIN)
                        newton_steps(g * NEWTON, slice(0 if k == 1 or scan else MT, 2 * MT if prev else MT))
                        if prev:
                            wait(pool, "tr_done", g - 1)
                            settle(pool)
                            for t in range(MT):
                                last = nc.gpsimd.tensor_scalar(xn3[0][:, t, :], on[:, 1 - k, t, :],
                                                               nmean[:, MT + t:MT + t + 1], rst[:, MT + t:MT + t + 1],
                                                               ALU.add, ALU.mult)
                            last.then_inc(S["xn3_done"], 1)
                    elif what == "x1":
                        g = (s - k) * 2 + k
                        pool.wait_ge(S["on_done"], g + 1)
                        nc.gpsimd.tensor_tensor(on[:, k, :, :], on[:, k, :, :],
                                                x_all[:, ds(g * MT, MT), :] if not isinstance(g, int)
                                                else x_all[:, g * MT:(g + 1) * MT, :], ALU.add
                                                ).then_inc(S["x1_done"], 1)

            def newton_steps(at, cols, chain="newton"):
                def link(ins):
                    nonlocal at
                    at = at + 1
                    ins.then_inc(S[chain], 1)
                    pool.wait_ge(S[chain], at)

                y = nt_y
                for n in range(3):
                    new = rst if n == 2 else pn_y
                    link(nc.gpsimd.tensor_tensor(pn_a[:, cols], y[:, cols], y[:, cols], ALU.mult))
                    link(nc.gpsimd.tensor_tensor(pn_b[:, cols], pn_a[:, cols], mhalf[:, cols], ALU.mult))
                    link(nc.gpsimd.tensor_tensor(pn_c[:, cols], pn_b[:, cols], three_halves[:, cols], ALU.add))
                    link(nc.gpsimd.tensor_tensor(new[:, cols], pn_c[:, cols], y[:, cols], ALU.mult))
                    y = pn_y

            def keep_earlier(i):
                pool.wait_ge(S["compared"], i + 1)
                wait(pool, "weighed", i * WEIGH)
                nc.gpsimd.tensor_tensor(before, beats, earlier[:, :].rearrange("p (e f) -> p e f", f=NE).unsqueeze(1)
                                        .to_broadcast([P, PT, NE, NE]), ALU.mult).then_inc(S["kept"], 1)

            run_bodies(pool, emit, lambda: keep_earlier(0))
            def output(i, q):
                g = i * 2 + q
                pool.wait_ge(S["onf_done"], g + 3)
                if not isinstance(i, int) or i:
                    pool.wait_ge(stored[q], i * 16)
                settle(pool)
                nc.gpsimd.tensor_tensor(outb[q], onf[q], x_all[:, ds(g * MT, MT), :] if not isinstance(g, int)
                                        else x_all[:, g * MT:(g + 1) * MT, :], ALU.add).then_inc(S["ob_done"], 1)

            pool.sem_inc(S["ob_done"], 2)
            pool.sem_inc(S["onf_done"], 2)
            pool.sem_inc(S["fout_newton"], 2 * (NEWTON + 1))

            def last_newton(i, q):
                g = i * 2 + q
                cols = slice(q * MT, (q + 1) * MT)
                pool.wait_ge(S["fout_chain"], (g + 1) * TAIL_CHAIN)
                pool.wait_ge(S["onf_done"], g + 1)
                at = (g + 2) * (NEWTON + 1)
                newton_steps(at, cols, "fout_newton")
                nc.gpsimd.tensor_tensor(shift[:, cols], nmean[:, cols], rst[:, cols], ALU.mult
                                        ).then_inc(S["fout_newton"], 1)
                pool.wait_ge(S["fout_newton"], at + NEWTON + 1)

            NP = NM // 2
            keep_earlier(1)
            emit(NSEQ, 0, False, False, 2)
            emit(NSEQ, 0, False, False, 3)
            for k in range(2):
                pool.wait_ge(x1_saved[k], NSEQ * 16)
            keep_earlier(2)
            last_newton(0, 0)
            last_newton(0, 1)
            output(0, 0)
            keep_earlier(3)
            last_newton(1, 0)
            output(0, 1)
            last_newton(1, 1)
            output(1, 0)
            with pool.Fori(3, NP - 1) as i:
                keep_earlier(i + 1)
                last_newton(i - 1, 0)
                output(i - 2, 1)
                last_newton(i - 1, 1)
                output(i - 1, 0)
            last_newton(NP - 2, 0)
            output(NP - 3, 1)
            last_newton(NP - 2, 1)
            output(NP - 2, 0)
            last_newton(NP - 1, 0)
            output(NP - 2, 1)
            last_newton(NP - 1, 1)
            output(NP - 1, 0)
            output(NP - 1, 1)

        @block.vector
        def _(dve):
            MAGIC = float(0x5F3759DF)

            def norm_coefs(sources, chain, at, first, last_col, variance=None, guess_only=False):
                def link(ins):
                    nonlocal at
                    at = at + 1
                    ins.then_inc(S[chain], 1)
                    dve.wait_ge(S[chain], at)

                cols = slice(first, last_col)
                v, a, b, yy = veps[:, cols], nt_a[:, cols], nt_b[:, cols], nt_y[:, cols]
                for n, source in enumerate(sources):
                    last = nc.vector.bn_stats(st6[:, first + n, :], source)
                link(last)
                settle(dve)
                for n in range(first, last_col):
                    last = nc.vector.bn_aggr(mv[:, n, :], st6[:, n, :])
                link(last)
                if variance is None:
                    nc.vector.tensor_scalar(nmean[:, cols], mv[:, cols, 0], -1.0, None, ALU.mult)
                    link(nc.vector.tensor_scalar(v, mv[:, cols, 1], EPS, None, ALU.add))
                else:
                    link(variance())
                link(nc.vector.tensor_scalar(a.bitcast(i32), v.bitcast(i32), 1, None, ALU.logical_shift_right))
                link(nc.vector.tensor_scalar(yy.bitcast(i32), a.bitcast(i32), -1.0, MAGIC, ALU.mult, ALU.add))
                if guess_only:
                    link(nc.vector.tensor_scalar(mhalf[:, cols], v, -0.5, None, ALU.mult))
                    return
                for n in range(3):
                    link(nc.vector.tensor_tensor(a, yy, yy, ALU.mult))
                    link(nc.vector.scalar_tensor_tensor(b, a, -0.5, v, ALU.mult, ALU.mult))
                    link(nc.vector.scalar_tensor_tensor(rst[:, cols] if n == 2 else yy, b, 1.5, yy, ALU.add, ALU.mult))

            def first_norm(i):
                sources = []
                for k in range(UNITS):
                    dve.wait_ge(u_in[k], i * 16 + 16)
                    for t in range(MT):
                        at = (i * UNITS + k) * MT + t
                        sources.append(x_all[:, ds(at, 1), :].rearrange("p t d -> p (t d)"))
                wait(dve, "p0_norm_act", i * 2)
                settle(dve)
                norm_coefs(sources, "p0_chain", i * LN_CHAIN, 0, NC)
                nc.vector.scalar_tensor_tensor(shift[:, :], mv[:, :, 0], -1.0, rst[:, :], ALU.mult, ALU.mult
                                               ).then_inc(S["p0_shift"], 1)
                for k in range(UNITS // 2):
                    wait(dve, "p0_tr", (i - 1) * UNITS + k + 1)
                    for t in range(MT):
                        n = k * MT + t
                        last = nc.vector.tensor_scalar(xn3[k][:, t, :], sources[n], mv[:, n, 0:1], rst[:, n:n + 1],
                                                       ALU.subtract, ALU.mult)
                    last.then_inc(S["p0_norm"], 1)

            run_peeled(dve, NM // UNITS, first_norm)

            dve.wait_ge(S["consts"], 16 * len(loads))
            dve.wait_ge(S["first_consts"], 48)
            dve.wait_ge(S["zeroed"], 4)

            sized = 0

            def pre(ins):
                nonlocal sized
                sized += 1
                ins.then_inc(S["pre_dve"], 1)
                dve.wait_ge(S["pre_dve"], sized)

            def sizes(k):
                if k == 0:
                    dve.wait_ge(S["p0_dtread"], NM // UNITS * 2)
                    v3 = s1[0].rearrange("p (t h) -> p t h", h=H)
                    pre(nc.vector.tensor_tensor(v3, dt_all[:, :, :], bias4[:, :].unsqueeze(1).to_broadcast([P, NT, H]), ALU.add))
                    pre(nc.vector.scalar_tensor_tensor(s1[1], s1[0], -1.0, s1[0], ALU.mult, ALU.max))
                if k == 1:
                    dve.wait_ge(S["pre_exp"], 1)
                    pre(nc.vector.tensor_scalar(s1[3], s1[2], 1.0, None, ALU.add))
                    pre(nc.vector.tensor_scalar(s1[5], s1[3], -1.0, None, ALU.add))
                    pre(nc.vector.tensor_tensor(s1[6], s1[2], s1[5], ALU.subtract))
                    pre(nc.vector.reciprocal(s1[7], s1[3]))
                    pre(nc.vector.tensor_tensor(s1[5], s1[6], s1[7], ALU.mult))
                if k == 2:
                    dve.wait_ge(S["pre_exp"], 3)
                    pre(nc.vector.scalar_tensor_tensor(s1[6], s1[0], 0.0, s1[4], ALU.max, ALU.add))
                    pre(nc.vector.tensor_tensor(dt_all[:, :, :].rearrange("p t h -> p (t h)"), s1[6], s1[5], ALU.add))
                    pre(nc.vector.scalar_tensor_tensor(s1[8].rearrange("p (t h) -> p t h", h=H), dt_all[:, :, :], -1.0,
                                                       s1[11][:, 0:H].unsqueeze(1).to_broadcast([P, NT, H]), ALU.mult, ALU.mult))
                if k == 3:
                    dve.wait_ge(S["pre_pe"], 1)
                    pre(nc.vector.tensor_copy(s1[10], sx_bank[:, 0:TN]))
                    pre(nc.vector.tensor_tensor(s1[9], ys_bank[:, 0:TN], s1[10], ALU.subtract))
                if k == 4:
                    dve.wait_ge(S["pre_pe"], 2)
                    pre(nc.vector.tensor_copy(csp[:, 0, :], tail_bank[:, 0:TN]))
                    pre(nc.vector.tensor_tensor(s1[0], tail_bank[:, 0:TN], csp[:, 0, :], ALU.subtract))
                    pre(nc.vector.tensor_copy(csp[:, 1, :], s1[0]))
                    pre(nc.vector.tensor_tensor(s1[1], s1[0], csp[:, 1, :], ALU.subtract))
                    pre(nc.vector.tensor_copy(csp[:, 2, :], s1[1]))

            def emit(s, par, scan, proj, prev):
                for what, k in steps(scan, proj, prev):
                    T = s * TPS + k
                    if what == "sizes":
                        sizes(k)
                    elif what == "chunk":
                        dve.wait_ge(S["b_done"], T + 1)
                        wait(dve, "c_done", T - 1)
                        dt = dt_all[:, T, :] if isinstance(T, int) else dt_all[:, ds(T, 1), :].rearrange(
                            "p t h -> p (t h)")
                        nc.vector.tensor_tensor(Xdt[:, k % 2, :].rearrange("p (h d) -> p h d", h=H),
                                                sx_bank[:, P:P + INTER].rearrange("p (h d) -> p h d", h=H),
                                                dt.unsqueeze(2).to_broadcast([P, H, HD]), ALU.mult
                                                ).then_inc(S["xdt_done"], 1)
                        dve.wait_ge(S["exp_done"], T + 1)
                        m = LE[:, k, 1, :].rearrange("p (h l) -> p h l", h=H)
                        nc.vector.tensor_tensor(m, m, sx_bank[:, 0:P].unsqueeze(1).to_broadcast([P, H, P]), ALU.mult
                                                ).then_inc(S["m_done"], 1)
                    elif what == "conv":
                        n = (s + 1) * NCONV + k
                        dve.wait_ge(S["a0_done"], 2 * n + 2)
                        dve.wait_ge(S["proj_read"],
                                    (s + 1) * NJOB + max(j for j, job in enumerate(JOBS) if job[0] == k) + 1)
                        y = xbc[:, 1 - par, k, :]
                        for i in range(NTAP):
                            if i:
                                dve.wait_ge(S["taps"], n * NTAP + i)
                            nc.vector.scalar_tensor_tensor(y, raw[:, k % 2, i:i + SEQ], cw[:, k, i:i + 1], y,
                                                           ALU.mult, ALU.add).then_inc(S["taps"], 1)
                    elif what == "state":
                        dve.wait_ge(S["c_done"], T + 1)
                        if k == 0:
                            nc.vector.tensor_copy(St[:, 0, :], ys_bank[:, INTER:2 * INTER]).then_inc(S["s_ready"], 1)
                        elif k < TPS - 1:
                            dve.wait_ge(S["sd_done"], s * (TPS - 2) + k)
                            nc.vector.tensor_tensor(St[:, k % 2, :], ys_bank[:, INTER:2 * INTER], Sd[:, :], ALU.add
                                                    ).then_inc(S["s_ready"], 1)
                        wait(dve, "out_done", s * 2 - 1 + (k // MT))
                        for c in range(2):
                            last = nc.vector.scalar_tensor_tensor(
                                gbuf[:, c, tile_of(k)], xbc[:, par, c, tile_of(k)], dskip[:, c:c + 1],
                                ys_bank[:, c * P:(c + 1) * P], ALU.mult, ALU.add)
                        last.then_inc(S["y_done"], 1)
                    elif what == "gate":
                        if k == 0:
                            dve.wait_ge(S["proj_read"], (s + 1) * NJOB)
                        dve.wait_ge(S["y_done"], s * TPS + (k + 1) * MT)
                        nc.vector.tensor_tensor(gbuf[:, :, half_of(k)], gbuf[:, :, half_of(k)],
                                                zs[:, par, :, half_of(k)], ALU.mult).then_inc(S["g_done"], 1)
                    elif what == "chain":
                        g = (s - k) * 2 + k
                        norm1 = k == 1 or scan
                        sources = []
                        if norm1:
                            dve.wait_ge(S["out_done"], g + 1)
                            sources += [tail_bank[:, t * D:(t + 1) * D] for t in range(MT)]
                        if prev:
                            dve.wait_ge(S["x1_done"], g)
                            dve.wait_ge(S["newton"], g * NEWTON)
                            wait(dve, "xn3_done", g - 1)
                            sources += [on[:, 1 - k, t, :] for t in range(MT)]

                        def variance():
                            if prev:
                                last = nc.vector.tensor_scalar(veps[:, MT:2 * MT], mv[:, MT:2 * MT, 1], EPS, None, ALU.add)
                                last = nc.vector.tensor_scalar(nmean[:, MT:2 * MT], mv[:, MT:2 * MT, 0], -1.0, None, ALU.mult)
                            if norm1:
                                dve.wait_ge(S["ms_read"], g + 1)
                                last = nc.vector.tensor_tensor(veps[:, 0:MT], msb[:, :], mv[:, 0:MT, 1], ALU.add)
                            return last

                        norm_coefs(sources, "chained", g * TAIL_CHAIN, 0 if norm1 else MT, 2 * MT if prev else MT,
                                   variance, guess_only=True)
                    elif what == "apply":
                        g = (s - k) * 2 + k
                        dve.wait_ge(S["newton"], (g + 1) * NEWTON)
                        if not isinstance(s, int) or s - k > 0:
                            dve.wait_ge(x1_saved[k], (s - k) * 16)
                        for t in range(MT):
                            last = nc.vector.tensor_scalar(on[:, k, t, :], tail_bank[:, t * D:(t + 1) * D],
                                                           mv[:, t, 0:1], rst[:, t:t + 1],
                                                           ALU.subtract, ALU.mult)
                        last.then_inc(S["on_done"], 1)

            done = 0

            def rt(ins):
                nonlocal done
                done += 1
                ins.then_inc(S["route"], 1)
                dve.wait_ge(S["route"], done)

            def scores(tiles):
                rt(nc.vector.tensor_scalar(r1[1][:, tiles, :], r1[0][:, tiles, :], 1.0, None, ALU.add))
                rt(nc.vector.reciprocal(r1[2][:, tiles, :], r1[1][:, tiles, :]))
                rt(nc.vector.tensor_scalar(r1[3][:, tiles, :], r1[2][:, tiles, :], rscale[:, 0:1], None, ALU.mult))

            def first_scores():
                dve.wait_ge(S["route_exp"], 1)
                scores(slice(0, NT - 2 * PT))
                compare(0)

            def compare(i):
                wait(dve, "kept", i)
                s_t = r1[3][:, ds(i * PT, PT), :]
                nc.vector.tensor_tensor(beats, s_t.unsqueeze(2).to_broadcast([P, PT, NE, NE]),
                                        s_t.unsqueeze(3).to_broadcast([P, PT, NE, NE]), ALU.is_ge
                                        ).then_inc(S["compared"], 1)

            def gates(i, first=True, second=True):
                at = i * WEIGH + (0 if first else WEIGH - 5)

                def link(ins):
                    nonlocal at
                    at = at + 1
                    ins.then_inc(S["weighed"], 1)
                    dve.wait_ge(S["weighed"], at)

                if first:
                    dve.wait_ge(S["kept"], i + 1)
                    rank_and_weigh(i, link)
                if second:
                    split(i, link)

            def rank_and_weigh(i, link):
                link(nc.vector.reduce_sum(wins, before, mybir.AxisListType.X))
                link(nc.vector.reduce_sum(losses, before.rearrange("p t e f -> p t f e"), mybir.AxisListType.X))
                link(nc.vector.tensor_tensor(wins, wins, losses, ALU.subtract))
                link(nc.vector.tensor_tensor(rank, wins, rank0[:, :].unsqueeze(1).to_broadcast([P, PT, NE]), ALU.add))
                link(nc.vector.scalar_tensor_tensor(gate, rank, 1.5, r1[3][:, ds(i * PT, PT), :], ALU.is_lt, ALU.mult))
                link(nc.vector.reduce_sum(gtot[:, 0:PT], gate, mybir.AxisListType.X))
                link(nc.vector.reciprocal(gtot[:, PT:2 * PT], gtot[:, 0:PT]))
                link(nc.vector.tensor_tensor(gate, gate, gtot[:, PT:2 * PT].unsqueeze(2).to_broadcast([P, PT, NE]), ALU.mult))

            def split(i, link):
                wait(dve, "gtt_done", i * 2)
                copies = gst[:, :, :, 0:3 * SGRP].rearrange("p a t (k c) -> p (a t) k c", c=SGRP)
                for k in range(3):
                    part = copies[:, :, :, k * NE:(k + 1) * NE]
                    link(nc.vector.tensor_copy(part, gate.unsqueeze(2).to_broadcast([P, PT, 3, NE])))
                    if k < 2:
                        link(nc.vector.tensor_tensor(gate, gate, part[:, :, 0, :], ALU.subtract))

            run_bodies(dve, emit, first_scores, lambda: gates(0))

            def gated(g, q, j):
                dve.wait_ge(S["gelu_done"], g * NF + j + 2)
                dve.wait_ge(S["gb_done"], g * NPAIR + j + 1)
                if j == 0:
                    wait(dve, "fout_done", g - 1)
                nc.vector.tensor_tensor(hg[q][j], hbuf[j % 2], exp_bank[:, j % 2, :], ALU.mult
                                        ).then_inc(S["hg_done"], 1)

            def last_norm(g, q):
                dve.wait_ge(S["fout_done"], g + 1)
                dve.wait_ge(S["fout_newton"], (g + 1) * (NEWTON + 1))
                norm_coefs([fout_bank[q][:, t * D:(t + 1) * D] for t in range(MT)], "fout_chain", g * TAIL_CHAIN,
                           q * MT, (q + 1) * MT, guess_only=True)

            def ffn(i, more=True):
                for q in range(2):
                    g = i * 2 + q
                    gated(g, q, 0)
                    if q == 0 and more:
                        compare(i + 1)
                    if isinstance(i, int) and i == 0:
                        for j in range(1, NPAIR):
                            gated(g, q, j)
                            if q == 0 and j == 1:
                                emit(NSEQ, 0, False, False, 2)
                            if q and j == 1:
                                gates(1, first=False)
                        if q == 0:
                            emit(NSEQ, 0, False, False, 3)
                    else:
                        last_norm(g - 2, q)
                        for j in range(1, NPAIR):
                            gated(g, q, j)
                            if q and j == 1 and more:
                                gates(i + 1, first=False)
                    if q == 0 and more:
                        gates(i + 1, second=False)

            ffn(0)
            dve.wait_ge(S["route_exp"], 2)
            scores(slice(NT - 2 * PT, NT))
            with dve.Fori(1, NM // 2 - 1) as i:
                ffn(i)
            ffn(NM // 2 - 1, False)
            last_norm(NM - 2, 0)
            last_norm(NM - 1, 1)

        @block.tensor
        def _(pe):
            mm = nc.tensor.matmul
            pe.wait_ge(S["first_consts"], 48)

            def project_dt(i):
                pe.wait_ge(S["p0_evac"], (i + 1) * UNITS)
                wait(pe, "p0_dtread", i * 2)
                for k in range(UNITS):
                    last = mm(dt_bank[k * SGRP:(k + 1) * SGRP, :], w_dt[:, :],
                              xT_all[:, (i * UNITS + k) * MW:(i * UNITS + k + 1) * MW], start=True, stop=True)
                last.then_inc(S["p0_dt"], 1)

            def turn_dt(i):
                pe.wait_ge(S["p0_dtread"], i * 2 + 1)
                for t in range(MT):
                    last = nc.tensor.transpose(dt_back[:, tile_of(t)], stage[:, tile_of(t)], ident[:, :])
                last.then_inc(S["p0_dt"], 1)

            def first_norm(i):
                for k in range(UNITS):
                    g, q = i * UNITS + k, k % 2
                    if k < 2:
                        pe.wait_ge(S["p0_norm"], i * 2 + k + 1)
                    else:
                        pe.wait_ge(S["p0_norm_act"], i * 2 + k - 1)
                    wait(pe, "p0_evac", g - 1)
                    for t in range(MT):
                        last = nc.tensor.transpose(proj_bank[q][:, tile_of(t)], xn3[k][:, t, :], ident[:, :])
                    last.then_inc(S["p0_tr"], 1)
                    if k >= 2 and i:
                        (project_dt, turn_dt)[k - 2](i - 1)

            for i in range(NM // UNITS):
                first_norm(i)
            project_dt(NM // UNITS - 1)
            turn_dt(NM // UNITS - 1)

            def sizes(k):
                if k == 2:
                    pe.wait_ge(S["consts"], 16 * len(loads))
                    pe.wait_ge(S["started"], 1)
                    pe.wait_ge(S["pre_dve"], 10)
                    mm(sx_bank[:, 0:TN], tri[:, :], s1[8], start=True, stop=True)
                    mm(ys_bank[:, 0:TN], ones[:, :], s1[8], start=True, stop=True).then_inc(S["pre_pe"], 1)
                if k == 3:
                    pe.wait_ge(S["pre_dve"], 11)
                    for a in range(2):
                        last = nc.tensor.transpose(tail_bank[:, tile_of(a)], s1[10][:, tile_of(a)], ident[:, :])
                    last.then_inc(S["pre_pe"], 1)
                if k == 4:
                    pe.wait_ge(S["consts_cast"], 16)
                    pe.wait_ge(S["pre_exp"], 5)
                    pe.wait_ge(S["p0_dtread"], NM // UNITS * 2)

            def emit(s, par, scan, proj, prev):
                seen = 0
                for what, k in steps(scan, proj, prev):
                    T = s * TPS + k
                    B, C = xbc[:, par, NCONV - 2, :], xbc[:, par, NCONV - 1, :]
                    if what == "sizes":
                        sizes(k)
                    elif what == "exp":
                        j = k % TPS
                        if j % (TPS // 2) == 0:
                            pe.wait_ge(cs_in[j // (TPS // 2)], (s + k // TPS + 1) * 64)
                        wait(pe, "exp_done", T)
                        mm(exp_bank[:, 0, :], csl[0:3, j, :], csr[0:3, j, :], start=True, stop=True)
                        mm(exp_bank[:, 1, :], csl[:, j, :], csr[:, j, :], start=True, stop=False)
                        mm(exp_bank[:, 1, :], identb[:, :], maskb[:, :, :].rearrange("p h l -> p (h l)"),
                           start=False, stop=True).then_inc(S["de_done"], 1)
                    elif what == "chunk":
                        if k == 0:
                            pe.wait_ge(S["xbc_ready"], (s + 1) * NCONV)
                        wait(pe, "m_done", T)
                        nc.tensor.transpose(sx_bank[:, P:2 * P], xbc[:, par, 0, tile_of(k)], ident[:, :])
                        nc.tensor.transpose(sx_bank[:, 2 * P:3 * P], xbc[:, par, 1, tile_of(k)], ident[:, :])
                        mm(sx_bank[:, 0:P], B[:, tile_of(k)], C[:, tile_of(k)], start=True, stop=True
                           ).then_inc(S["b_done"], 1)
                        seen = k + 1
                        wait(pe, "btok_done", T)
                        if k == chunk_after(("logits", 1)):
                            wait(pe, "lg_read", s * 2 - 2 if k == 0 else s * 2)
                        if k == chunk_after(("ms", 1)) and prev:
                            wait(pe, "ms_read", s * 2)
                        if k == chunk_after(("logits", 0)) and prev:
                            wait(pe, "lg_read", s * 2 - 1)
                        if k == chunk_after(("ms", 0)):
                            wait(pe, "ms_read", s * 2 + 1)
                        nc.tensor.transpose(bt_bank[:, 0:P], B[:, tile_of(k)], ident[:, :]).then_inc(S["bt_done"], 1)
                    elif what == "state":
                        wait(pe, "y_done", T)
                        pe.wait_ge(S["m_done"], T + 1)
                        if k < TPS - 1:
                            pe.wait_ge(S["btok_done"], T + 1)
                            pe.wait_ge(S["xw_done"], s * (TPS - 1) + k + 1)
                            mm(ys_bank[:, INTER:2 * INTER], Btok[:, k % 2, :], Xw[:, k % 2, :], start=True, stop=True)
                        if k:
                            pe.wait_ge(S["ch_done"], s * (TPS - 1) + k)
                            pe.wait_ge(S["s_ready"], s * (TPS - 1) + k)
                        for c in range(2):
                            for part in range(2 if k else 1):
                                for a in range(2):
                                    h = 2 * c + a
                                    lhs = (Xdt[:, k % 2, :] if part == 0 else St[:, (k - 1) % 2, :])[:, h * HD:(h + 1) * HD]
                                    last = mm(ys_bank[a * HD:(a + 1) * HD, c * P:(c + 1) * P], lhs,
                                              LE[:, k, 1 - part, h * P:(h + 1) * P], start=(part == 0),
                                              stop=(part == 1 or not k))
                        last.then_inc(S["c_done"], 1)
                    elif what == "job":
                        c, m = JOBS[k]
                        J = (s + 1) * NJOB + k
                        col = CONV0 + c * P if c < NCONV else (c - NCONV) * P
                        wait(pe, "proj_read", J - 1)
                        at = (s + 1) * SEQ + m * MW
                        mm(proj_bank[k % 2][:, :], w_in[:, col:col + P],
                           xT_all[:, ds(at, MW)] if not isinstance(at, int) else xT_all[:, at:at + MW],
                           start=True, stop=True).then_inc(S["proj_done"], 1)
                    elif what == "outproj":
                        g = (s - k) * 2 + k
                        pe.wait_ge(S["g_done"], g + 1)
                        wait(pe, "xft_done", 2 * g - 2)
                        for t in range(MT):
                            at = k * MW + t * P
                            for c in range(2):
                                last = mm(tail_bank[:, t * D:(t + 1) * D], gbuf[:, c, at:at + P], w_out[:, c, :],
                                          start=(c == 0), stop=(c == 1))
                        last.then_inc(S["out_done"], 1)
                    elif what == "ms":
                        g, pq = (s - k) * 2 + k, par if k == 0 else 1 - par
                        pe.wait_ge(S["sqs_done"], g + 1)
                        pe.wait_ge(S["btok_done"], s * TPS + seen)
                        if not scan:
                            pe.wait_ge(S["lg_read"], g - 1)
                        for t in range(MT):
                            at = k * MW + t * P
                            last = mm(bt_bank[:, P + t:P + t + 1], zs[:, pq, 0, at:at + P], ones[:, 0:1],
                                      start=True, stop=True)
                        last.then_inc(S["ms_done"], 1)
                    elif what == "back":
                        g = (s - 1) * 2 + k
                        pe.wait_ge(S["xn3_done"], g + 1)
                        if k == 0 or scan:
                            pe.wait_ge(S["on_done"], g + 2)
                        else:
                            pe.wait_ge(S["xft_done"], 2 * g)
                        for t in range(MT):
                            last = nc.tensor.transpose(tail_bank[:, tile_of(t)], xn3[0][:, t, :], ident[:, :])
                        last.then_inc(S["tr_done"], 1)
                    elif what == "logits":
                        g = (s - 1) * 2 + k
                        pe.wait_ge(S["xft_done"], 2 * g + 1)
                        pe.wait_ge(S["btok_done"], s * TPS + seen)
                        wait(pe, "ms_read", g + 2 if k == 0 or scan else g + 1)
                        for t in range(MT):
                            last = mm(bt_bank[:, 2 * P + t * NE:2 * P + (t + 1) * NE],
                                      stage[:, tile_of(t)], w_gate[:, :], start=True, stop=True)
                        last.then_inc(S["lg_done"], 1)

            run_bodies(pe, emit)

            def second(g, q, t):
                if t == 0:
                    pe.wait_ge(S["hg_done"], (g + 1) * NPAIR)
                    pe.wait_ge(S["gelu_done"], (g + 1) * NF)
                    pe.wait_ge(S["onf_done"], g + 1)
                o = fout_bank[q][:, t * D:(t + 1) * D]
                for j in range(NPAIR):
                    mm(o, hg[q][j][:, tile_of(t)], w2[:, j, :], start=(j == 0), stop=False)
                mm(o, hg[q][NPAIR][0:HID, tile_of(t)], w2[0:HID, NPAIR, :], start=False, stop=False)
                last = mm(o, gt[q][:, tile_of(t)], brow[:, :], start=False, stop=True)
                if t == MT - 1:
                    last.then_inc(S["fout_done"], 1)

            pe.wait_ge(S["lg_read"], NM - 2)
            pe.wait_ge(S["ms_read"], NM)

            def ffn(i):
                for q in range(2):
                    g = i * 2 + q
                    pe.wait_ge(S["weighed"], (i + 1) * WEIGH)
                    wait(pe, "gt_done", g)
                    for t in range(MT):
                        last = nc.tensor.transpose(gt_bank[:, tile_of(t)], gst[:, q, t, :], identb[:, :])
                    last.then_inc(S["gtt_done"], 1)
                    for n in range(NF):
                        j = (n - 1) % NF
                        if isinstance(i, int) and q and n == NF - 1:
                            emit(NSEQ, 0, False, False, 4)
                        wait(pe, "gelu_done", g * NF + n - 1)
                        at = g * MW
                        src = xT_all[:, ds(at, MW)] if not isinstance(at, int) else xT_all[:, at:at + MW]
                        if j < NPAIR:
                            mm(proj_bank[(q * NF + n) % 2][:, :], w1[:, j * P:(j + 1) * P], src, start=True, stop=True
                               ).then_inc(S["f1_done"], 1)
                            if j == 0:
                                pe.wait_ge(S["gt_done"], g + 1)
                            wait(pe, "hg_done", g * NPAIR + j - 1)
                            mm(exp_bank[:, j % 2, :], selb[:, j, :], gt[q], start=True, stop=True).then_inc(S["gb_done"], 1)
                            if not (isinstance(g, int) and g == 0):
                                second(g - 1, 1 - q, j)
                        else:
                            settle(pe)
                            mm(proj_bank[(q * NF + n) % 2][0:HID, :], w1[:, NPAIR * P:], src, start=True, stop=True
                               ).then_inc(S["f1_done"], 1)
                    if isinstance(i, int):
                        if q == 0:
                            pe.wait_ge(S["gt_done"], 1)
                            emit(NSEQ, 0, False, False, 2)
                        pe.wait_ge(S["lg_read"], NM - 1 + q)

            run_peeled(pe, NM // 2, ffn)
            for t in range(MT):
                second(NM - 1, 1, t)


def kernel(**inputs):
    import numpy as _np
    import concourse.bacc as _bacc
    from concourse import mybir as _mybir
    from concourse.bass_utils import run_bass_kernel_spmd as _run

    given = {n.replace("L0_attn_", "").replace("L0_ffn_", ""): _np.asarray(v) for n, v in inputs.items()}
    arrays = {n: given[n] for n in ("u", "in_proj_w", "conv_w", "dt_bias", "A_log", "D_param", "out_proj_w",
                                    "gate_W", "W1", "W2", "b2", "Ws1", "bs1", "Ws2", "bs2", "norm_w")}
    arrays["route_scale"] = given["route_scale"].reshape(1)
    arrays["norm_w_cols"] = given["norm_w"].reshape(-1, 128).T
    arrays["conv_b_cols"] = given["conv_b"].reshape(-1, 128).T
    arrays["b1_cols"] = given["b1"].reshape(-1, 128).T
    one = _np.ones((128, 128), _np.float32)
    arrays["c_ident"] = _np.eye(128, dtype=_np.float32)
    arrays["c_tri"] = _np.triu(one)
    arrays["c_mask"] = _np.tril(one, -1) * _np.float32(-1e30)
    heads = given["dt_bias"].shape[0]
    rows = _np.zeros((3 + 3 * heads, heads * 128 + 128), _np.float32)
    rows[0:3, heads * 128:] = 1.0
    for r in range(3 * heads):
        h = r % heads
        rows[3 + r, h * 128:(h + 1) * 128] = -1.0
    arrays["c_rows"] = rows
    experts, hid = given["W1"].shape[0], given["W1"].shape[2]
    sel = _np.zeros((128, experts * hid), _np.float32)
    for e in range(experts):
        for k in range(3):
            sel[experts * k + e, e * hid:(e + 1) * hid] = 1.0
    arrays["c_sel"] = sel
    arrays["c_rank"] = _np.tile(_np.arange(experts - 1, -1, -1, dtype=_np.float32), (128, 1))
    arrays["c_earlier"] = _np.tile(_np.tril(_np.ones((experts, experts), _np.float32), -1).reshape(1, -1), (128, 1))

    nc = _bacc.Bacc("TRN2", target_bir_lowering=False, num_devices=1)
    feeds, dram = {}, {}
    for name, a in arrays.items():
        a = _np.ascontiguousarray(a)
        feeds[f"in_{name}"] = a
        dram[name] = nc.dram_tensor(f"in_{name}", a.shape, _mybir.dt.from_np(a.dtype), kind="ExternalInput").ap()
    out = nc.dram_tensor("out_dram", given["u"].shape, _mybir.dt.float32, kind="ExternalOutput").ap()
    ssd_moe_block(nc, dram, out)
    r = _run(nc, [feeds], core_ids=[0])
    return r.results[0]["out_dram"]
```
